# Optimizing a Trainium2 kernel written in Bass

```python
import numpy as np
import jax
import jax.numpy as jnp

def _softmax(x, axis=-1):
    return jax.nn.softmax(x, axis=axis)

def _gelu(x):
    return jax.nn.gelu(x, approximate=True)

def _silu(x):
    return jax.nn.silu(x)

def _sigmoid(x):
    return jax.nn.sigmoid(x)

def _layernorm(x, axis=-1, eps=1e-05):
    m = jnp.mean(x, axis=axis, keepdims=True)
    v = jnp.var(x, axis=axis, keepdims=True)
    return (x - m) / jnp.sqrt(v + eps)

def _scatter_add(tgt, idx, src, axis=0):
    return tgt.at[idx].add(src)

def _segment_sum(src, seg, n):
    return jax.ops.segment_sum(src, seg, n)
kernel_name = 'mk_decoder_postln_d1_seqx_r8_fc8ad4'

def setup_inputs(seed: int=0):
    np.random.seed(seed)
    _w = jnp.asarray

    def _rec_inputs():
        import jax
        import jax.numpy as jnp
        _rk = jax.random.key(seed)
        x = -0.0003929 + 0.9999 * jax.random.normal(jax.random.fold_in(_rk, 1), (16, 64, 512), jnp.float32)
        _lenS = 64 - jax.random.randint(jax.random.fold_in(_rk, 7), (16,), 0, max(1, 64 // 4) + 1, jnp.int32)
        _lenS2 = 64 - jax.random.randint(jax.random.fold_in(_rk, 8), (16,), 0, max(1, 64 // 4) + 1, jnp.int32)
        _ctx_4096P = jax.random.normal(jax.random.fold_in(_rk, 11), (16, 16, 512), jnp.float32)
        _ctx_4096c = jax.random.dirichlet(jax.random.fold_in(_rk, 511), 0.3 * jnp.ones((16,), jnp.float32), (16, 64))
        _ctx_4096t = jnp.einsum('bsk,bkd->bsd', _ctx_4096c, _ctx_4096P)
        _ctx_4096t = _ctx_4096t * jax.lax.rsqrt(jnp.mean(jnp.square(_ctx_4096t)) + 1e-12) * 0.953939
        ctx_4096 = 2.81802e-05 + 1.00001 * (_ctx_4096t + 0.3 * jax.random.normal(jax.random.fold_in(_rk, 611), (16, 64, 512), jnp.float32))
        return (x, ctx_4096)
    x, ctx_4096 = _rec_inputs()

    def _L0_attn_setup():
        import jax, jax.numpy as jnp
        import numpy as np
        HIDDEN = 512
        NUM_HEADS = 32
        HEAD_DIM = HIDDEN // NUM_HEADS
        B, S = (2, 128)

        def _alibi_slopes(n):
            start = 2.0 ** (-2.0 ** (-(np.log2(n) - 3)))
            return np.array([start ** (i + 1) for i in range(n)], dtype=np.float32)
        key = jax.random.key(seed)
        k1, k2, k3, k4 = jax.random.split(key, 4)
        hidden_states = jax.random.normal(k1, (B, S, HIDDEN), jnp.float32)
        Wq = jax.random.normal(k2, (HIDDEN, HIDDEN), jnp.float32) * 0.02
        Wkv = jax.random.normal(k3, (HIDDEN, 2 * HEAD_DIM), jnp.float32) * 0.02
        Wo = jax.random.normal(k4, (HIDDEN, HIDDEN), jnp.float32) * 0.02
        return {'hidden_states': hidden_states, 'Wq': Wq, 'Wkv': Wkv, 'Wo': Wo}
    _L0_attn_all = _L0_attn_setup()
    _L0_attn_in = {k: v for k, v in _L0_attn_all.items() if k in ('Wq', 'Wkv', 'Wo')}
    del _L0_attn_all

    def _L0_xattn_setup():
        import jax, jax.numpy as jnp
        import numpy as np
        HEADS = 8
        DIM_HEAD = 64
        DIM = 64
        HIDDEN = HEADS * DIM_HEAD
        B, N = (8, 512)
        key = jax.random.key(seed)
        ks = jax.random.split(key, 7)
        s = 0.02
        return {'x': jax.random.normal(ks[0], (B, DIM, N), dtype=jnp.float32), 'context': jax.random.normal(ks[1], (B, DIM, N), dtype=jnp.float32), 'Wq': jax.random.normal(ks[2], (HIDDEN, DIM), dtype=jnp.float32) * s, 'Wkv': jax.random.normal(ks[3], (2 * HIDDEN, DIM), dtype=jnp.float32) * s, 'Wout': jax.random.normal(ks[4], (DIM, HIDDEN), dtype=jnp.float32) * s, 'b_out': jnp.zeros((DIM,), dtype=jnp.float32), 'g': jnp.ones((1, DIM, 1), dtype=jnp.float32)}
    _L0_xattn_all = _L0_xattn_setup()
    _L0_xattn_in = {k: v for k, v in _L0_xattn_all.items() if k in ('Wq', 'Wkv', 'Wout', 'b_out', 'g')}
    del _L0_xattn_all

    def _L0_ffn_setup():
        import jax, jax.numpy as jnp
        import numpy as np
        HID, INT, LAT, NE, K = (512, 1024, 256, 8, 2)
        LN_EPS = 1e-05

        def _layernorm(x, gamma, beta):
            mu = jnp.mean(x, axis=-1, keepdims=True)
            var = jnp.var(x, axis=-1, keepdims=True)
            return (x - mu) * jax.lax.rsqrt(var + LN_EPS) * gamma + beta
        key = jax.random.key(seed)
        ks = jax.random.split(key, 8)
        s = lambda d: 1.0 / np.sqrt(d)
        return {'hidden_states': jax.random.normal(ks[0], (4, 256, HID), jnp.float32), 'gate_w': jax.random.normal(ks[1], (HID, NE), jnp.float32) * s(HID), 'up_w': jax.random.normal(ks[2], (HID, INT), jnp.float32) * s(HID), 'down_w': jax.random.normal(ks[3], (INT, HID), jnp.float32) * s(INT), 'fc1_w': jax.random.normal(ks[4], (HID, LAT), jnp.float32) * s(HID), 'fc2_w': jax.random.normal(ks[5], (LAT, HID), jnp.float32) * s(LAT), 'expert_w': jax.random.normal(ks[6], (LAT, LAT), jnp.float32), 'ln_gamma': jnp.ones((HID,), jnp.float32), 'ln_beta': jnp.zeros((HID,), jnp.float32)}
    _L0_ffn_all = _L0_ffn_setup()
    _L0_ffn_in = {k: v for k, v in _L0_ffn_all.items() if k in ('gate_w', 'up_w', 'down_w', 'fc1_w', 'fc2_w', 'expert_w', 'ln_gamma', 'ln_beta')}
    del _L0_ffn_all
    return {'x': x, 'ctx_4096': ctx_4096, 'L0_attn_Wq': _L0_attn_in['Wq'], 'L0_attn_Wkv': _L0_attn_in['Wkv'], 'L0_attn_Wo': _L0_attn_in['Wo'], 'L0_xattn_Wq': _L0_xattn_in['Wq'], 'L0_xattn_Wkv': _L0_xattn_in['Wkv'], 'L0_xattn_Wout': _L0_xattn_in['Wout'], 'L0_xattn_b_out': _L0_xattn_in['b_out'], 'L0_xattn_g': _L0_xattn_in['g'], 'L0_ffn_gate_w': _L0_ffn_in['gate_w'], 'L0_ffn_up_w': _L0_ffn_in['up_w'], 'L0_ffn_down_w': _L0_ffn_in['down_w'], 'L0_ffn_fc1_w': _L0_ffn_in['fc1_w'], 'L0_ffn_fc2_w': _L0_ffn_in['fc2_w'], 'L0_ffn_expert_w': _L0_ffn_in['expert_w'], 'L0_ffn_ln_gamma': _L0_ffn_in['ln_gamma'], 'L0_ffn_ln_beta': _L0_ffn_in['ln_beta']}

def reference(x, ctx_4096, L0_attn_Wq, L0_attn_Wkv, L0_attn_Wo, L0_xattn_Wq, L0_xattn_Wkv, L0_xattn_Wout, L0_xattn_b_out, L0_xattn_g, L0_ffn_gate_w, L0_ffn_up_w, L0_ffn_down_w, L0_ffn_fc1_w, L0_ffn_fc2_w, L0_ffn_expert_w, L0_ffn_ln_gamma, L0_ffn_ln_beta):
    import jax
    import jax.numpy as jnp

    def _L0_attn_ref(hidden_states, Wq, Wkv, Wo):
        import jax, jax.numpy as jnp
        import numpy as np
        HIDDEN = 512
        NUM_HEADS = 32
        HEAD_DIM = HIDDEN // NUM_HEADS
        B, S = (2, 128)

        def _alibi_slopes(n):
            start = 2.0 ** (-2.0 ** (-(np.log2(n) - 3)))
            return np.array([start ** (i + 1) for i in range(n)], dtype=np.float32)
        b, s, h = hidden_states.shape
        scale = HEAD_DIM ** (-0.5)
        q = (hidden_states @ Wq).reshape(b, s, NUM_HEADS, HEAD_DIM)
        kv = hidden_states @ Wkv
        k, v = (kv[..., :HEAD_DIM], kv[..., HEAD_DIM:])
        scores = jnp.einsum('bqhd,bkd->bhqk', q, k) * scale
        pos = jnp.arange(s)
        slopes = jnp.asarray(_alibi_slopes(NUM_HEADS))
        bias = slopes[:, None, None] * (pos[None, None, :] - pos[None, :, None]).astype(jnp.float32)
        causal = pos[None, :] <= pos[:, None]
        scores = jnp.where(causal[None, None], scores + bias[None], -jnp.inf)
        attn = jax.nn.softmax(scores, axis=-1)
        out = jnp.einsum('bhqk,bkd->bqhd', attn, v).reshape(b, s, h)
        return out @ Wo

    def _L0_xattn_ref(x, context, Wq, Wkv, Wout, b_out, g):
        import jax, jax.numpy as jnp
        import numpy as np
        HEADS = 8
        DIM_HEAD = 64
        DIM = 64
        HIDDEN = HEADS * DIM_HEAD
        B, N = (8, 512)
        scale = DIM_HEAD ** (-0.5)
        q = jnp.einsum('oc,bcn->bon', Wq, x)
        kv = jnp.einsum('oc,bcn->bon', Wkv, context)
        k, v = jnp.split(kv, 2, axis=1)

        def split_heads(t):
            b, hc, n = t.shape
            return t.reshape(b, HEADS, DIM_HEAD, n)
        q = jax.nn.softmax(split_heads(q), axis=-2) * scale
        k = jax.nn.softmax(split_heads(k), axis=-1)
        v = split_heads(v)
        ctx = jnp.einsum('bhdn,bhen->bhde', k, v)
        out = jnp.einsum('bhde,bhdn->bhen', ctx, q)
        b, h, e, n = out.shape
        out = out.reshape(b, h * e, n)
        out = jnp.einsum('oc,bcn->bon', Wout, out) + b_out[None, :, None]
        mean = jnp.mean(out, axis=1, keepdims=True)
        var = jnp.var(out, axis=1, keepdims=True)
        return (out - mean) * jax.lax.rsqrt(var + 1e-05) * g

    def _L0_ffn_ref(hidden_states, gate_w, up_w, down_w, fc1_w, fc2_w, expert_w, ln_gamma, ln_beta):
        import jax, jax.numpy as jnp
        import numpy as np
        HID, INT, LAT, NE, K = (512, 1024, 256, 8, 2)
        LN_EPS = 1e-05

        def _layernorm(x, gamma, beta):
            mu = jnp.mean(x, axis=-1, keepdims=True)
            var = jnp.var(x, axis=-1, keepdims=True)
            return (x - mu) * jax.lax.rsqrt(var + LN_EPS) * gamma + beta
        logits = jnp.einsum('bsh,he->bse', hidden_states, gate_w)
        routing_weights, selected_experts = jax.lax.top_k(logits, K)
        h = jax.nn.relu(jnp.einsum('bsh,hi->bsi', hidden_states, up_w)) ** 2
        shared_out = jnp.einsum('bsi,ih->bsh', h, down_w)
        x_latent = jnp.einsum('bsh,hl->bsl', hidden_states, fc1_w)
        expert_out = jnp.einsum('bsl,lm->bsm', x_latent, expert_w)
        moe_out = expert_out * jnp.sum(routing_weights, axis=-1, keepdims=True)
        routed_out = jnp.einsum('bsl,lh->bsh', moe_out, fc2_w)
        return _layernorm(shared_out + routed_out, ln_gamma, ln_beta)
    x = _layernorm(x + _L0_attn_ref(x, L0_attn_Wq, L0_attn_Wkv, L0_attn_Wo), axis=-1)
    x = _layernorm(x + _L0_xattn_ref(x, ctx_4096, L0_xattn_Wq, L0_xattn_Wkv, L0_xattn_Wout, L0_xattn_b_out, L0_xattn_g), axis=-1)
    x = _layernorm(x + _L0_ffn_ref(x, L0_ffn_gate_w, L0_ffn_up_w, L0_ffn_down_w, L0_ffn_fc1_w, L0_ffn_fc2_w, L0_ffn_expert_w, L0_ffn_ln_gamma, L0_ffn_ln_beta), axis=-1)
    return x

_drawn_inputs = setup_inputs


def setup_inputs(seed=0):
    import zlib

    import numpy as np

    out = dict(_drawn_inputs(seed))
    spreads = {'L0_xattn_b_out': (0.0, 0.8),
     'L0_xattn_g': (1.0, 0.6),
     'L0_ffn_ln_gamma': (1.0, 0.2),
     'L0_ffn_ln_beta': (0.0, 0.1)}
    factors = {'ctx_4096': 8.0,
     'L0_attn_Wq': 3.348,
     'L0_xattn_Wq': 8.0,
     'L0_xattn_Wkv': 8.0,
     'L0_xattn_Wout': 8.0}
    for name, (base, spread) in spreads.items():
        noise = np.random.default_rng([zlib.crc32(name.encode()), seed]).standard_normal(out[name].shape)
        drawn = base * np.exp(spread * noise) if base else spread * noise
        out[name] = jnp.asarray(drawn.astype(out[name].dtype))
    for name, factor in factors.items():
        out[name] = (out[name] * factor).astype(out[name].dtype)
    return out
```

```python
from contextlib import ExitStack

import numpy as np

import concourse.bass as bass
from concourse import mybir

F32 = mybir.dt.float32
F32R = mybir.dt.float32r
ALU = mybir.AluOpType
ACT = mybir.ActivationFunctionType
ALONG_FREE = mybir.AxisListType.X

P = 128
BATCH, SEQ, DM = 16, 64, 512
PAIRS = BATCH * SEQ // P
KC = DM // P
HEADS, HD = 32, 16
GROUPS = 4
HG = HEADS // GROUPS
XH, XD = 8, 64
INT, LAT, NE = 1024, 256, 8
IC, LC = INT // P, LAT // P
EPS = 1e-5
MASKED = -1e30
WINDOW = 3 * 2 * HD
ROUNDS = 24
UNITS = 8


def shape_tables():
    start = 2.0 ** (-2.0 ** (-(np.log2(HEADS) - 3)))
    slopes = np.array([start ** (i + 1) for i in range(HEADS)], dtype=np.float32)
    pos = np.arange(SEQ)
    causal = np.where(pos[None, :] <= pos[:, None], 0.0, MASKED).astype(np.float32)
    causal = np.concatenate([causal, causal], 0)
    own = np.zeros((P, HG), np.float32)
    for h in range(HG):
        own[h * HD:(h + 1) * HD, h] = 1.0
    q = np.tile(pos, 2).astype(np.float32)
    left = np.zeros((P, GROUPS, P), np.float32)
    right = np.zeros((P, HG, SEQ), np.float32)
    for h in range(HG):
        for g in range(GROUPS):
            for r, v in ((0, slopes[g * HG + h] * np.ones(P, np.float32)), (2, slopes[g * HG + h] * q)):
                v = v.astype(np.float32)
                hi = (v.view(np.uint32) & np.uint32(0xFFFFF000)).view(np.float32)
                left[r * HG + h, g] = hi
                left[(r + 1) * HG + h, g] = v - hi
        right[h, h] = right[HG + h, h] = pos
        right[2 * HG + h, h] = right[3 * HG + h, h] = -1.0
    return (np.concatenate([np.eye(P, dtype=np.float32), causal, own], 1),
            np.stack([left.reshape(P, -1), right.reshape(P, -1)], 1))


T_IDENT, T_CAUSAL, T_OWN, T_ALL = 0, P, P + SEQ, P + SEQ + HG


class Signal:

    def __init__(self, sem, per):
        self.sem, self.per = sem, per

    def wait(self, eng, pair, nth):
        value = pair * self.per + nth
        if not isinstance(value, int) or value > 0:
            eng.wait_ge(self.sem, value)


def decoder_kernel(nc, x, ctx, wq, wkv, wo, xwq, xwkv, xwout, xb_out, xg, gate_w, up_w, down_w,
                   fc1_w, fc2_w, expert_w, ln_gamma, ln_beta, tables, bias_rows, out):
    stack = ExitStack()
    with stack:
        def sb(name, shape, dt=F32):
            return stack.enter_context(nc.sbuf_tensor(name, shape, dt))

        def sem(name):
            return stack.enter_context(nc.semaphore(name))

        def sig(name, per=1):
            return Signal(sem(name), per)

        tab = sb("tab", [P, T_ALL])
        ident = tab[:, T_IDENT:T_IDENT + P]
        own = tab[:, T_OWN:T_OWN + HG]
        ident_r = sb("ident_r", [P, P], F32R)
        causal_r = sb("causal_r", [P, SEQ], F32R)
        left_r = sb("left_r", [P, GROUPS, P], F32R)
        right_r = sb("right_r", [P, HG * SEQ], F32R)
        wq_hi, wq_lo = sb("wq_hi", [P, KC, DM], F32R), sb("wq_lo", [P, KC, DM], F32R)
        wk_hi, wk_lo = sb("wk_hi", [P, KC, P], F32R), sb("wk_lo", [P, KC, P], F32R)
        wv_hi, wv_lo = sb("wv_hi", [P, KC, HD], F32R), sb("wv_lo", [P, KC, HD], F32R)
        wo_sb = sb("wo_sb", [P, KC, DM])
        xwq_hi, xwq_lo = sb("xwq_hi", [P, DM], F32R), sb("xwq_lo", [P, DM], F32R)
        xwk_hi, xwk_lo = sb("xwk_hi", [P, DM], F32R), sb("xwk_lo", [P, DM], F32R)
        vout = sb("vout", [XD, XH * SEQ])
        bout = sb("bout", [P, SEQ])
        gcol = sb("gcol", [P, 1])
        gate_sb = sb("gate_sb", [P, KC, NE])
        gate_hi, gate_lo = sb("gate_hi", [P, KC, NE], F32R), sb("gate_lo", [P, KC, NE], F32R)
        up_hi, up_lo = sb("up_hi", [P, KC, INT], F32R), sb("up_lo", [P, KC, INT], F32R)
        down_sb = sb("down_sb", [P, IC, DM])
        wr_hi, wr_lo = sb("wr_hi", [P, KC, DM], F32R), sb("wr_lo", [P, KC, DM], F32R)
        gamma, beta = sb("gamma", [P, DM]), sb("beta", [P, DM])
        minus_half = sb("minus_half", [P, UNITS])

        x_in, x_keep, x1 = sb("x_in", [P, DM]), sb("x_keep", [P, DM]), sb("x1", [P, DM])
        xt_hi, xt_lo = sb("xt_hi", [P, KC, P], F32R), sb("xt_lo", [P, KC, P], F32R)
        qt_hi, qt_lo = sb("qt_hi", [P, GROUPS, 3 * SEQ], F32R), sb("qt_lo", [P, GROUPS, 3 * SEQ], F32R)
        kt_hi, kt_lo = sb("kt_hi", [P, P], F32R), sb("kt_lo", [P, P], F32R)
        kd_hi, kd_lo = sb("kd_hi", [P, 2, HG, SEQ], F32R), sb("kd_lo", [P, 2, HG, SEQ], F32R)
        vwin = sb("vwin", [P, 2, 2 * WINDOW + 2 * HD])
        prob = sb("prob", [P, 2, HG * SEQ])
        pt_sb = sb("pt_sb", [P, 2, DM])
        ao_sb = sb("ao_sb", [P, GROUPS, P])
        smax, ssum, srec = sb("smax", [P, GROUPS, HG]), sb("ssum", [P, GROUPS, HG]), sb("srec", [P, GROUPS, HG])
        c_in = sb("c_in", [P, DM])
        xs, cs = sb("xs", [P, 2, DM], F32R), sb("cs", [P, 2, DM], F32R)
        ct_sb = sb("ct_sb", [P, KC, P])
        ek, ekt = sb("ek", [P, 2, DM]), sb("ekt", [P, 2, DM])
        tctx = sb("tctx", [XD, DM])
        mt = sb("mt", [P, 2, KC, SEQ])
        eq, eqt = sb("eq", [P, 2, DM]), sb("eqt", [P, 2, DM])
        kneg, ksum, krec = sb("kneg", [P, UNITS]), sb("ksum", [P, UNITS]), sb("krec", [P, UNITS])
        kmax = sb("kmax", [P, UNITS])
        qmax, qsum, qrec = sb("qmax", [P, UNITS, XH]), sb("qsum", [P, UNITS, XH]), sb("qrec", [P, UNITS, XH])
        o_sb, x2 = sb("o_sb", [P, DM]), sb("x2", [P, DM])
        zb_sb = o_sb
        omean, ovar, orstd = sb("omean", [P, UNITS]), sb("ovar", [P, UNITS]), sb("orstd", [P, UNITS])
        x2t_hi, x2t_lo = sb("x2t_hi", [P, KC, P], F32R), sb("x2t_lo", [P, KC, P], F32R)
        cw = sb("cw", [P, 8, DM])
        h_sb, ht_sb = cw[:, 0:2, :], cw[:, 2:4, :]
        routed, f_sb, x2_beta, y_sb = cw[:, 4, :], cw[:, 5, :], cw[:, 6, :], cw[:, 7, :]
        top8, rsum = sb("top8", [P, NE]), sb("rsum", [P, 1])
        stats = [sb(f"stats{n}", [P, 6]) for n in range(4)]
        meanvar = [sb(f"meanvar{n}", [P, 2]) for n in range(4)]
        var_eps = [sb(f"var_eps{n}", [P, 1]) for n in range(4)]
        rstd = [sb(f"rstd{n}", [P, 1]) for n in range(4)]

        wait_pad = sb("wait_pad", [P, 1])

        bank = [stack.enter_context(nc.psum_tensor(f"bank{n}", [P, DM], F32)) for n in range(8)]
        A0, A1, A2, B0, B1, B2, C0, C1 = bank

        ld_tab, ld_bias, ld_wq, ld_wkv, ld_wo = sem("ld_tab"), sem("ld_bias"), sem("ld_wq"), sem("ld_wkv"), sem("ld_wo")
        ld_xwq, ld_xwk, ld_xwv, ld_xwo, ld_xb = (sem("ld_xwq"), sem("ld_xwk"), sem("ld_xwv"), sem("ld_xwo"),
                                                 sem("ld_xb"))
        ld_up, ld_down, ld_gate, ld_fc, ld_gb = sem("ld_up"), sem("ld_down"), sem("ld_gate"), sem("ld_fc"), sem("ld_gb")
        tab_r, hi_a, lo_a, zeroed = sem("tab_r"), sem("hi_a"), sem("lo_a"), sem("zeroed")
        tr_b, hi_b, lo_b, g_b = sem("tr_b"), sem("hi_b"), sem("lo_b"), sem("g_b")
        hi_c, lo_c, fold_ps, fold_sb, wr_ps, wr_h, wr_l = (sem("hi_c"), sem("lo_c"), sem("fold_ps"), sem("fold_sb"),
                                                           sem("wr_ps"), sem("wr_h"), sem("wr_l"))
        halves = sem("halves")

        x_load, x_kept = sig("x_load", 16), sig("x_kept")
        xt_ps, xt_h, xt_l = sig("xt_ps"), sig("xt_h"), sig("xt_l")
        qt_ps, qt_h, qt_l = sig("qt_ps"), sig("qt_h"), sig("qt_l")
        kv_ps, kt_h, kt_l, v_win = sig("kv_ps"), sig("kt_h"), sig("kt_l"), sig("v_win")
        kd_done = sig("kd_done", 4)
        s_ps, s_max, s_sub, s_exp = sig("s_ps", 4), sig("s_max", 4), sig("s_sub", 4), sig("s_exp", 4)
        s_sum, s_rec, s_nrm = sig("s_sum", 4), sig("s_rec", 4), sig("s_nrm", 4)
        pt_ps, pt_done, ao_ps, ao_done = sig("pt_ps", 4), sig("pt_done", 4), sig("ao_ps", 4), sig("ao_done")
        y_ps, z_done = sig("y_ps"), sig("z_done")
        ln_stat = [sig(f"ln_stat{n}") for n in range(4)]
        ln_mean = [sig(f"ln_mean{n}") for n in range(4)]
        ln_eps = [sig(f"ln_eps{n}") for n in range(4)]
        ln_rstd = [sig(f"ln_rstd{n}") for n in range(4)]
        x1_done = sig("x1_done")
        c_load, ct_ps, ct_done = sig("c_load", 16), sig("ct_ps"), sig("ct_done")
        cs_h, cs_l, xs_h, xs_l = sig("cs_h", 2), sig("cs_l", 2), sig("xs_h", 2), sig("xs_l", 2)
        k_ps, k_max, k_neg, k_exp = sig("k_ps", 8), sig("k_max", 8), sig("k_neg", 8), sig("k_exp", 8)
        kt_ps, ekt_done, t_ps, t_done, m_ps = sig("kt_ps", 8), sig("ekt_done", 8), sig("t_ps", 8), sig("t_done", 2), sig("m_ps", 2)
        k_rec, k_scl, mt_done = sig("k_rec", 2), sig("k_scl", 2), sig("mt_done", 2)
        q_ps, q_max, q_sub, q_exp = sig("q_ps", 8), sig("q_max", 8), sig("q_sub", 8), sig("q_exp", 8)
        q_sum, q_rec, q_nrm = sig("q_sum", 8), sig("q_rec", 8), sig("q_nrm", 8)
        eqt_ps, eqt_done, o_ps = sig("eqt_ps", 8), sig("eqt_done", 8), sig("o_ps", 8)
        o_add, o_sum, o_mean, o_cen, o_sq, o_var, o_eps, o_rstd, o_nrm = (
            sig("o_add"), sig("o_sum"), sig("o_mean"), sig("o_cen"), sig("o_sq"), sig("o_var"), sig("o_eps"),
            sig("o_rstd"), sig("o_nrm"))
        ot_ps, zb_done, x2_done = sig("ot_ps"), sig("zb_done"), sig("x2_done")
        x2t_ps, x2t_h, x2t_l, xb_done = sig("x2t_ps"), sig("x2t_h"), sig("x2t_l"), sig("xb_done")
        lg_ps, lg_top, lg_sum = sig("lg_ps"), sig("lg_top"), sig("lg_sum")
        h_ps, h_relu, h_sq, ht_ps, ht_done = sig("h_ps", 2), sig("h_relu", 2), sig("h_sq", 2), sig("ht_ps", 2), sig("ht_done", 2)
        sh_ps, ro_ps, ro_done, f_add, f_nrm, f_gam, f_res, y_done, y_out = (
            sig("sh_ps"), sig("ro_ps"), sig("ro_done"), sig("f_add"), sig("f_nrm"), sig("f_gam"), sig("f_res"),
            sig("y_done"), sig("y_out", 16))

        block = stack.enter_context(nc.Block())

        def drive(eng, setup_a, setup_b, setup_c, step):
            setup_a()
            step(0, None, None)
            setup_b()
            step(1, 0, None)
            setup_c()
            step(2, 1, 0)
            with eng.Fori(3, PAIRS) as i:
                step(i, i - 1, i - 2)
            step(None, PAIRS - 1, PAIRS - 2)
            step(None, None, PAIRS - 1)

        def first(p):
            return isinstance(p, int) and p == 0

        def f32(ap):
            return ap.bitcast(F32)

        @block.sync
        def _(sp):
            sp.dma_start(x_in[:], x[0]).then_inc(x_load.sem, 16)
            sp.dma_start(tab[:], tables).then_inc(ld_tab, 16)
            sp.dma_start(ekt[:], bias_rows).then_inc(ld_bias, 16)
            sp.dma_start(cw[:, 0, 0:KC * 2 * HD].rearrange("p (k n) -> p k n", k=KC),
                         wkv.rearrange("(k p) n -> p k n", p=P)).then_inc(ld_wkv, 16)
            sp.dma_start(cw[:, 1:5, :], wq.rearrange("(k p) n -> p k n", p=P)).then_inc(ld_wq, 16)
            sp.dma_start(wo_sb[:], wo.rearrange("(k p) n -> p k n", p=P)).then_inc(ld_wo, 16)
            for slot, s, rows in ((ek, ld_xwq, xwq), (eq, ld_xwk, xwkv[0:DM, :])):
                for twice in range(2):
                    sp.dma_start(slot[:, 0, :].rearrange("p (k t c) -> p k t c", k=KC, t=2)[:, :, twice, :],
                                 rows.rearrange("(k p) c -> p k c", p=P)).then_inc(s, 16)
            sp.wait_ge(tab_r, 4)
            sp.dma_start(ekt[0:XD, 0, :].rearrange("e (h c) -> e h c", h=XH),
                         xwkv[DM:2 * DM, :].rearrange("(h e) c -> e h c", h=XH)).then_inc(ld_xwv, 16)
            sp.dma_start(ekt[0:SEQ, 1, :], xwout).then_inc(ld_xwo, 16)
            sp.dma_start(bout[:], xb_out.partition_broadcast(P)).then_inc(ld_xb, 16)
            for b in range(2):
                sp.dma_start(gcol[b * SEQ:(b + 1) * SEQ, :], xg.rearrange("a c n -> (a c) n")).then_inc(ld_xb, 16)
            sp.dma_start(down_sb[:], down_w.rearrange("(k p) n -> p k n", p=P)).then_inc(ld_down, 16)
            sp.dma_start(gamma[:], ln_gamma.partition_broadcast(P)).then_inc(ld_gb, 16)
            sp.dma_start(beta[:], ln_beta.partition_broadcast(P)).then_inc(ld_gb, 16)
            sp.wait_ge(hi_a, 3)
            sp.wait_ge(lo_a, 3)
            sp.dma_start(cw[:].rearrange("p (k j) n -> p k j n", k=KC),
                         up_w.rearrange("(k p) (j n) -> p k j n", p=P, j=2)).then_inc(ld_up, 16)
            sp.dma_start(gate_sb[:],
                         gate_w.rearrange("(k p) n -> p k n", p=P)).then_inc(ld_gate, 16)
            sp.wait_ge(hi_c, 1)
            sp.wait_ge(lo_c, 1)
            sp.dma_start(cw[:, 0:2, :].rearrange("p j n -> p (j n)").rearrange("p (k n) -> p k n", k=KC),
                         fc1_w.rearrange("(k p) n -> p k n", p=P)).then_inc(ld_fc, 16)
            sp.dma_start(cw[:, 2, :].rearrange("p (k n) -> p k n", k=LC),
                         expert_w.rearrange("(k p) n -> p k n", p=P)).then_inc(ld_fc, 16)
            sp.dma_start(cw[:, 3:5, :], fc2_w.rearrange("(k p) n -> p k n", p=P)).then_inc(ld_fc, 16)
            y_out.wait(sp, PAIRS, 0)

        @block.tensor
        def _(pe):
            def product(o, pairs_of, start, stop, **kw):
                n = len(pairs_of)
                for j, (l, r) in enumerate(pairs_of):
                    ins = pe.matmul(o, l, r, start=start and j == 0, stop=stop and j == n - 1, **kw)
                return ins

            def split(l_hi, l_lo, r_hi, r_lo):
                return [(l_hi, r_hi), (l_hi, r_lo), (l_lo, r_hi)]

            def turn(o, src):
                for j in range(KC):
                    ins = pe.transpose(o[:, j * P:(j + 1) * P], src[:, j * P:(j + 1) * P], ident)
                return ins

            def setup_a():
                pe.wait_ge(ld_tab, 16)

            def setup_b():
                for s, slot, o in ((ld_xwq, ek, B0), (ld_xwk, eq, B1)):
                    pe.wait_ge(s, 32)
                    turn(o, slot[:, 0, :]).then_inc(tr_b, 1)
                pe.wait_ge(ld_xwo, 16)
                for h in range(XH):
                    ins = pe.transpose(B2[0:XD, h * SEQ:(h + 1) * SEQ], ekt[0:SEQ, 1, h * XD:(h + 1) * XD],
                                       ident[0:SEQ, 0:SEQ])
                ins.then_inc(tr_b, 1)
                pe.wait_ge(hi_b, 3)
                pe.wait_ge(lo_b, 2)
                pe.wait_ge(ld_xwv, 16)
                for h in range(XH):
                    ins = pe.matmul(B0[0:XD, h * SEQ:(h + 1) * SEQ], ekt[0:XD, 0, h * XD:(h + 1) * XD],
                                    eqt[0:XD, 0, h * SEQ:(h + 1) * SEQ], start=True, stop=True)
                ins.then_inc(tr_b, 1)
                pe.wait_ge(g_b, 1)

            def setup_c():
                pe.wait_ge(ld_fc, 48)
                fc1 = cw[:, 0:2, :].rearrange("p j n -> p (j n)").rearrange("p (k n) -> p k n", k=KC)
                for l, o in enumerate((C0, C1)):
                    for k in range(KC):
                        ins = pe.transpose(o[:, k * P:(k + 1) * P], fc1[:, k, l * P:(l + 1) * P], ident)
                    ins.then_inc(fold_ps, 1)
                pe.wait_ge(fold_sb, 2)
                for m, o in enumerate((C0, C1)):
                    product(o[:], [(cw[:, 2, l * LAT + m * P:l * LAT + (m + 1) * P], cw[:, 5 + l, :])
                                   for l in range(LC)], True, True).then_inc(fold_ps, 1)
                pe.wait_ge(fold_sb, 4)
                for k in range(KC):
                    if k >= 2:
                        pe.wait_ge(wr_h, k - 1)
                        pe.wait_ge(wr_l, k - 1)
                    product((C0, C1)[k % 2][:], [(cw[:, m, k * P:(k + 1) * P], cw[:, 3 + m, :]) for m in range(LC)],
                            True, True).then_inc(wr_ps, 1)
                pe.wait_ge(wr_h, 4)
                pe.wait_ge(wr_l, 4)
                pe.wait_ge(hi_c, 2)
                pe.wait_ge(lo_c, 2)
                pe.wait_ge(ld_down, 16)

            def x_turn(p):
                x_load.wait(pe, p, 16)
                pt_done.wait(pe, p, 0)
                turn(A0, x_in).then_inc(xt_ps.sem, 1)

            def qkv(p):
                if first(p):
                    pe.wait_ge(hi_a, 3)
                    pe.wait_ge(lo_a, 3)
                xt_h.wait(pe, p, 1)
                xt_l.wait(pe, p, 1)
                z_done.wait(pe, p, 0)
                for g in range(GROUPS):
                    cols = slice(g * P, (g + 1) * P)
                    ins = product(A1[:, cols], [t for k in range(KC) for t in
                                                split(wq_hi[:, k, cols], wq_lo[:, k, cols],
                                                      xt_hi[:, k, :], xt_lo[:, k, :])], True, True)
                ins.then_inc(qt_ps.sem, 1)
                ao_done.wait(pe, p, 0)
                product(A2[:, 0:P], [t for k in range(KC) for t in
                                     split(wk_hi[:, k, :], wk_lo[:, k, :], xt_hi[:, k, :], xt_lo[:, k, :])],
                        True, True)
                product(A2[:, P:P + HD], [t for k in range(KC) for t in
                                          split(xt_hi[:, k, :], xt_lo[:, k, :], wv_hi[:, k, :], wv_lo[:, k, :])],
                        True, True).then_inc(kv_ps.sem, 1)

            S_BANK = (A0, A1, A2, A1)

            def scores(p, g):
                if g == 0:
                    if first(p):
                        pe.wait_ge(tab_r, 4)
                        pe.wait_ge(zeroed, 3)
                    qt_h.wait(pe, p, 1)
                    qt_l.wait(pe, p, 1)
                    kd_done.wait(pe, p, 4)
                if g == 2:
                    v_win.wait(pe, p, 1)
                if g == 3:
                    s_sub.wait(pe, p, 2)
                terms = []
                for b in range(2):
                    qh = qt_hi[:, g, b * SEQ:b * SEQ + P]
                    ql = qt_lo[:, g, b * SEQ:b * SEQ + P]
                    kh = kd_hi[:, b].rearrange("p h k -> p (h k)")
                    kl = kd_lo[:, b].rearrange("p h k -> p (h k)")
                    terms += split(qh, ql, kh, kl)
                terms.append((left_r[:, g, :], right_r[:]))
                terms.append((ident_r[:], causal_r[:, None, :].broadcast_to([P, HG, SEQ])))
                product(S_BANK[g][:], terms, True, True).then_inc(s_ps.sem, 1)

            PT_BANK = (A0, A0, A1, A0)

            def prob_turn(p, g):
                s_nrm.wait(pe, p, g + 1)
                if g in (1, 3):
                    pt_done.wait(pe, p, g)
                if g == 2:
                    s_sub.wait(pe, p, 4)
                turn(PT_BANK[g], prob[:, g % 2, :]).then_inc(pt_ps.sem, 1)

            def values(p, g):
                pt_done.wait(pe, p, g + 1)
                if g == 0:
                    s_sub.wait(pe, p, 3)
                for b in range(2):
                    ins = product(A2[:, g * P + b * SEQ:g * P + (b + 1) * SEQ],
                                  [(vwin[:, b, WINDOW - 2 * HD * j:WINDOW - 2 * HD * j + P],
                                    pt_sb[:, g % 2, j * P + b * SEQ:j * P + (b + 1) * SEQ])
                                   for j in range(HG // 2)], True, True)
                ins.then_inc(ao_ps.sem, 1)

            def project(p):
                if first(p):
                    pe.wait_ge(ld_wo, 16)
                ao_done.wait(pe, p, 1)
                pt_done.wait(pe, p, 3)
                product(A1[:], [(ao_sb[:, g, :], wo_sb[:, g, :]) for g in range(GROUPS)],
                        True, True).then_inc(y_ps.sem, 1)

            def c_turn(p):
                c_load.wait(pe, p, 16)
                q_sub.wait(pe, p, 0)
                turn(B0, c_in).then_inc(ct_ps.sem, 1)

            def keys(p, u):
                b, blk = divmod(u, KC)
                if u == 0:
                    cs_h.wait(pe, p, 2)
                    cs_l.wait(pe, p, 2)
                    ct_done.wait(pe, p, 1)
                else:
                    k_exp.wait(pe, p, u)
                cols = slice(blk * P, (blk + 1) * P)
                product(B0[:], [(xwk_hi[:, cols], cs[:, b, :]), (xwk_lo[:, cols], cs[:, b, :])],
                        True, True).then_inc(k_ps.sem, 1)

            def keys_turn(p, u):
                k_exp.wait(pe, p, u + 1)
                if u == 0:
                    zb_done.wait(pe, p, 0)
                else:
                    ekt_done.wait(pe, p, u)
                turn(B1, ek[:, u % 2, :]).then_inc(kt_ps.sem, 1)

            def context(p, u):
                b, blk = divmod(u, KC)
                ekt_done.wait(pe, p, u + 1)
                if u == 0:
                    o_add.wait(pe, p, 0)
                    ct_done.wait(pe, p, 1)
                if u == KC:
                    mt_done.wait(pe, p, 1)
                product(B2[0:SEQ, blk * P:(blk + 1) * P],
                        [(ct_sb[:, n, b * SEQ:(b + 1) * SEQ], ekt[:, u % 2, n * P:(n + 1) * P]) for n in range(KC)],
                        True, True).then_inc(t_ps.sem, 1)

            def combine(p, b):
                t_done.wait(pe, p, b + 1)
                for blk in range(KC):
                    cols = slice(blk * P, (blk + 1) * P)
                    ins = pe.matmul(B2[:, cols], tctx[:, cols], vout[:, cols], start=True, stop=True)
                ins.then_inc(m_ps.sem, 1)

            def queries(p, v):
                b, n = divmod(v, KC)
                if v == 0:
                    xs_h.wait(pe, p, 2)
                    xs_l.wait(pe, p, 2)
                    k_exp.wait(pe, p, 8)
                else:
                    q_sub.wait(pe, p, v)
                cols = slice(n * P, (n + 1) * P)
                product(B0[:], [(xs[:, b, cols], xwq_hi[:]), (xs[:, b, cols], xwq_lo[:])],
                        True, True).then_inc(q_ps.sem, 1)

            def queries_turn(p, v):
                q_nrm.wait(pe, p, v + 1)
                if v == 0:
                    ekt_done.wait(pe, p, 8)
                else:
                    eqt_done.wait(pe, p, v)
                turn(B1, eq[:, v % 2, :]).then_inc(eqt_ps.sem, 1)

            def attend(p, v):
                b, n = divmod(v, KC)
                eqt_done.wait(pe, p, v + 1)
                if v == 0:
                    mt_done.wait(pe, p, 2)
                product(B2[:, n * P + b * SEQ:n * P + (b + 1) * SEQ],
                        [(eqt[:, v % 2, blk * P:(blk + 1) * P], mt[:, b, blk, :]) for blk in range(KC)],
                        True, True).then_inc(o_ps.sem, 1)

            def o_turn(p):
                o_nrm.wait(pe, p, 1)
                eqt_done.wait(pe, p, 8)
                turn(B1, o_sb).then_inc(ot_ps.sem, 1)

            def x2_turn(p):
                x2_done.wait(pe, p, 1)
                f_add.wait(pe, p, 0)
                turn(C0, x2).then_inc(x2t_ps.sem, 1)

            def logits(p):
                x2t_h.wait(pe, p, 1)
                x2t_l.wait(pe, p, 1)
                ro_done.wait(pe, p, 0)
                product(C1[:, 0:NE], [t for k in range(KC) for t in
                                      split(x2t_hi[:, k, :], x2t_lo[:, k, :], gate_hi[:, k, :], gate_lo[:, k, :])],
                        True, True).then_inc(lg_ps.sem, 1)

            def hidden(p, j):
                if j == 1:
                    lg_top.wait(pe, p, 1)
                cols = slice(j * DM, (j + 1) * DM)
                product((C0, C1)[j][:], [t for k in range(KC) for t in
                                         split(x2t_hi[:, k, :], x2t_lo[:, k, :], up_hi[:, k, cols], up_lo[:, k, cols])],
                        True, True).then_inc(h_ps.sem, 1)

            def hidden_turn(p, j):
                h_sq.wait(pe, p, j + 1)
                turn((C0, C1)[j], h_sb[:, j, :]).then_inc(ht_ps.sem, 1)

            def shared(p):
                ht_done.wait(pe, p, 2)
                product(C0[:], [(ht_sb[:, j, k * P:(k + 1) * P], down_sb[:, j * KC + k, :])
                                for j in range(2) for k in range(KC)], True, True).then_inc(sh_ps.sem, 1)

            def routing(p):
                product(C1[:], [t for k in range(KC) for t in
                                split(x2t_hi[:, k, :], x2t_lo[:, k, :], wr_hi[:, k, :], wr_lo[:, k, :])],
                        True, True).then_inc(ro_ps.sem, 1)

            def step(a, b, c):
                for r in range(ROUNDS):
                    if c is not None:
                        if r == 2:
                            x2_turn(c)
                        if r == 3:
                            logits(c)
                            hidden(c, 0)
                        if r == 4:
                            hidden(c, 1)
                        if r in (5, 6):
                            hidden_turn(c, r - 5)
                        if r == 7:
                            shared(c)
                        if r == 8:
                            routing(c)
                    if b is not None:
                        if r == 0:
                            c_turn(b)
                        if 12 <= r < 20:
                            attend(b, r - 12)
                        if 10 <= r < 18:
                            queries_turn(b, r - 10)
                        if 1 <= r < 9:
                            keys_turn(b, r - 1)
                        if 2 <= r < 6:
                            context(b, r - 2)
                        if 7 <= r < 11:
                            context(b, r - 3)
                        if r in (6, 11):
                            combine(b, r // 11)
                        if r < 8:
                            keys(b, r)
                        if 8 <= r < 16:
                            queries(b, r - 8)
                        if r == 21:
                            o_turn(b)
                    if a is not None:
                        if r == 8:
                            x_turn(a)
                        if r == 9:
                            qkv(a)
                        if 11 <= r < 15:
                            scores(a, r - 11)
                        if 13 <= r < 17:
                            prob_turn(a, r - 13)
                        if 15 <= r < 19:
                            values(a, r - 15)
                        if r == 20:
                            project(a)

            drive(pe, setup_a, setup_b, setup_c, step)

        @block.vector
        def _(dve):
            def low(o, whole, hi):
                return dve.tensor_tensor(o, whole, f32(hi), ALU.subtract)

            def statistics(n, p, z):
                dve.bn_stats(stats[n][:], z).then_inc(ln_stat[n].sem, 1)
                ln_stat[n].wait(dve, p, 1)
                dve.memset(wait_pad[:], 0.0)
                dve.bn_aggr(meanvar[n][:], stats[n][:]).then_inc(ln_mean[n].sem, 1)
                ln_mean[n].wait(dve, p, 1)
                dve.tensor_scalar(var_eps[n][:], meanvar[n][:, 1:2], EPS, None, ALU.add).then_inc(ln_eps[n].sem, 1)

            def normalize(n, p, o, z):
                ln_rstd[n].wait(dve, p, 1)
                return dve.tensor_scalar(o, z, meanvar[n][:, 0:1], rstd[n][:, 0:1], ALU.subtract, ALU.mult)

            def setup_a():
                for z in (qt_hi, qt_lo):
                    dve.memset(f32(z[:, :, SEQ:2 * SEQ]), 0.0).then_inc(zeroed, 1)
                dve.memset(vwin[:], 0.0).then_inc(zeroed, 1)
                dve.wait_ge(zeroed, 3)
                dve.wait_ge(ld_wkv, 16)
                wkv_v = cw[:, 0, 0:KC * 2 * HD].rearrange("p (k n) -> p k n", k=KC)
                dve.wait_ge(hi_a, 2)
                for k in range(KC):
                    ins = low(wk_lo[:, k, :].rearrange("p (h d) -> p h d", h=HG),
                              wkv_v[:, k, None, 0:HD].broadcast_to([P, HG, HD]),
                              wk_hi[:, k, :].rearrange("p (h d) -> p h d", h=HG))
                ins.then_inc(lo_a, 1)
                low(wv_lo[:], wkv_v[:, :, HD:2 * HD], wv_hi[:]).then_inc(lo_a, 1)
                dve.wait_ge(hi_a, 3)
                low(wq_lo[:], cw[:, 1:5, :], wq_hi[:]).then_inc(lo_a, 1)

            def setup_b():
                for n, (o, hi, ps) in enumerate(((xwq_lo, xwq_hi, B0), (xwk_lo, xwk_hi, B1))):
                    dve.wait_ge(hi_b, n + 1)
                    low(o[:], ps[:], hi[:]).then_inc(lo_b, 1)
                dve.wait_ge(ld_xb, 48)

            def setup_c():
                dve.wait_ge(hi_c, 1)
                low(up_lo[:].rearrange("p k n -> p (k n)"), cw[:].rearrange("p s n -> p (s n)"),
                    up_hi[:].rearrange("p k n -> p (k n)")).then_inc(lo_c, 1)
                dve.wait_ge(hi_c, 2)
                low(gate_lo[:], gate_sb[:], gate_hi[:]).then_inc(lo_c, 1)
                for k in range(KC):
                    dve.wait_ge(wr_h, k + 1)
                    low(wr_lo[:, k, :], (C0, C1)[k % 2][:], wr_hi[:, k, :]).then_inc(wr_l, 1)

            def x_low(p):
                xt_h.wait(dve, p, 1)
                low(xt_lo[:].rearrange("p k n -> p (k n)"), A0[:], xt_hi[:].rearrange("p k n -> p (k n)"))\
                    .then_inc(xt_l.sem, 1)

            def q_low(p):
                qt_h.wait(dve, p, 1)
                for b in range(2):
                    ins = dve.scalar_tensor_tensor(
                        qt_lo[:, :, 2 * b * SEQ:(2 * b + 1) * SEQ],
                        A1[:].rearrange("p (g t) -> p g t", g=GROUPS)[:, :, b * SEQ:(b + 1) * SEQ], HD ** -0.5,
                        f32(qt_hi[:, :, 2 * b * SEQ:(2 * b + 1) * SEQ]), ALU.mult, ALU.subtract)
                ins.then_inc(qt_l.sem, 1)
                kt_h.wait(dve, p, 1)
                low(kt_lo[:], A2[:, 0:P], kt_hi[:]).then_inc(kt_l.sem, 1)
                for b in range(2):
                    for half in range(2):
                        ins = dve.tensor_copy(
                            vwin[half * SEQ:(half + 1) * SEQ, b, WINDOW + half * HD:WINDOW + (half + 1) * HD],
                            A2[b * SEQ:(b + 1) * SEQ, P:P + HD])
                ins.then_inc(v_win.sem, 1)

            def heads(ap):
                return ap.rearrange("p (h k) -> p h k", h=HG)

            def score_max(p, g):
                ps = (A0, A1, A2, A1)[g]
                s_ps.wait(dve, p, g + 1)
                dve.tensor_reduce(smax[:, g, :], heads(ps[:]), ALONG_FREE, ALU.max).then_inc(s_max.sem, 1)
                s_max.wait(dve, p, g + 1)
                if g < 2:
                    pt_ps.wait(dve, p, 0)
                else:
                    pt_ps.wait(dve, p, g - 1)
                dve.tensor_tensor(heads(prob[:, g % 2, :]), heads(ps[:]),
                                  smax[:, g, :, None].broadcast_to([P, HG, SEQ]), ALU.subtract).then_inc(s_sub.sem, 1)

            def prob_sum(p, g):
                s_exp.wait(dve, p, g + 1)
                dve.tensor_reduce(ssum[:, g, :], heads(prob[:, g % 2, :]), ALONG_FREE, ALU.add).then_inc(s_sum.sem, 1)
                s_sum.wait(dve, p, g + 1)
                dve.reciprocal(srec[:, g, :], ssum[:, g, :]).then_inc(s_rec.sem, 1)

            def residual_a(p):
                y_ps.wait(dve, p, 1)
                x_kept.wait(dve, p, 1)
                dve.tensor_tensor(x_keep[:], A1[:], x_keep[:], ALU.add).then_inc(z_done.sem, 1)
                z_done.wait(dve, p, 1)
                statistics(0, p, x_keep[:])

            def finish_a(p):
                zb_done.wait(dve, p, 0)
                xs_h.wait(dve, p, 0)
                normalize(0, p, x1[:], x_keep[:]).then_inc(x1_done.sem, 1)

            def stacks(p, src, o, h, l):
                h.wait(dve, p, 2)
                for b in range(2):
                    rows, other = slice(b * SEQ, (b + 1) * SEQ), slice((1 - b) * SEQ, (2 - b) * SEQ)
                    dve.tensor_tensor(o[other, b, :], src[rows, :], f32(o[rows, b, :]), ALU.subtract)\
                        .then_inc(l.sem, 1)

            def key_max(p, u):
                k_ps.wait(dve, p, u + 1)
                dve.tensor_reduce(kmax[:, u:u + 1], B0[:], ALONG_FREE, ALU.max).then_inc(k_max.sem, 1)
                k_max.wait(dve, p, u + 1)
                dve.tensor_scalar(kneg[:, u:u + 1], kmax[:, u:u + 1], -1.0, None, ALU.mult).then_inc(k_neg.sem, 1)

            def key_turned(p, u):
                kt_ps.wait(dve, p, u + 1)
                if u < 2:
                    t_ps.wait(dve, p, 0)
                else:
                    t_ps.wait(dve, p, u - 1)
                dve.tensor_copy(ekt[:, u % 2, :], B1[:]).then_inc(ekt_done.sem, 1)

            def key_scale(p, b):
                cols = slice(b * KC, (b + 1) * KC)
                k_exp.wait(dve, p, (b + 1) * KC)
                dve.reciprocal(krec[:, cols], ksum[:, cols]).then_inc(k_rec.sem, 1)
                k_rec.wait(dve, p, b + 1)
                dve.tensor_scalar(krec[:, cols], krec[:, cols], XD ** -0.5, None, ALU.mult).then_inc(k_scl.sem, 1)
                k_scl.wait(dve, p, b + 1)
                m_ps.wait(dve, p, b + 1)
                for half in range(2):
                    rows = slice(half * XD, (half + 1) * XD)
                    ins = dve.tensor_tensor(
                        mt[rows, b], B2[rows, :].rearrange("p (k o) -> p k o", k=KC)[:, :, half * SEQ:(half + 1) * SEQ],
                        krec[rows, cols][:, :, None].broadcast_to([XD, KC, SEQ]), ALU.mult)
                ins.then_inc(mt_done.sem, 1)

            def xheads(ap):
                return ap.rearrange("p (h d) -> p h d", h=XH)

            def query_max(p, v):
                q_ps.wait(dve, p, v + 1)
                dve.tensor_reduce(qmax[:, v, :], xheads(B0[:]), ALONG_FREE, ALU.max).then_inc(q_max.sem, 1)
                q_max.wait(dve, p, v + 1)
                if v < 2:
                    eqt_ps.wait(dve, p, 0)
                    o_sq.wait(dve, p, 0)
                    o_var.wait(dve, p, 0)
                else:
                    eqt_ps.wait(dve, p, v - 1)
                dve.tensor_tensor(xheads(eq[:, v % 2, :]), xheads(B0[:]),
                                  qmax[:, v, :, None].broadcast_to([P, XH, XD]), ALU.subtract).then_inc(q_sub.sem, 1)

            def query_sum(p, v):
                q_exp.wait(dve, p, v + 1)
                dve.tensor_reduce(qsum[:, v, :], xheads(eq[:, v % 2, :]), ALONG_FREE, ALU.add).then_inc(q_sum.sem, 1)
                q_sum.wait(dve, p, v + 1)
                dve.reciprocal(qrec[:, v, :], qsum[:, v, :]).then_inc(q_rec.sem, 1)

            def tiles(ap):
                return ap.rearrange("p (t o) -> p t o", o=SEQ)

            def output_center(p):
                o_ps.wait(dve, p, 8)
                x2_done.wait(dve, p, 0)
                dve.tensor_tensor(tiles(o_sb[:]), tiles(B2[:]), bout[:, None, :].broadcast_to([P, UNITS, SEQ]),
                                  ALU.add).then_inc(o_add.sem, 1)
                o_add.wait(dve, p, 1)
                dve.tensor_reduce(omean[:], tiles(o_sb[:]), ALONG_FREE, ALU.add).then_inc(o_sum.sem, 1)
                o_sum.wait(dve, p, 1)
                dve.tensor_scalar(omean[:], omean[:], 1.0 / SEQ, None, ALU.mult).then_inc(o_mean.sem, 1)
                o_mean.wait(dve, p, 1)
                dve.tensor_tensor(tiles(o_sb[:]), tiles(o_sb[:]), omean[:, :, None].broadcast_to([P, UNITS, SEQ]),
                                  ALU.subtract).then_inc(o_cen.sem, 1)

            def output_var(p):
                o_sq.wait(dve, p, 1)
                dve.tensor_reduce(ovar[:], tiles(eq[:, 0, :]), ALONG_FREE, ALU.add).then_inc(o_var.sem, 1)
                o_var.wait(dve, p, 1)
                dve.tensor_scalar(ovar[:], ovar[:], 1.0 / SEQ, EPS, ALU.mult, ALU.add).then_inc(o_eps.sem, 1)

            def residual_b(p):
                ot_ps.wait(dve, p, 1)
                dve.scalar_tensor_tensor(zb_sb[:], B1[:], gcol[:, 0:1], x1[:], ALU.mult, ALU.add)\
                    .then_inc(zb_done.sem, 1)
                zb_done.wait(dve, p, 1)
                statistics(1, p, zb_sb[:])

            def finish_b(p):
                x2t_ps.wait(dve, p, 0)
                xb_done.wait(dve, p, 0)
                normalize(1, p, x2[:], zb_sb[:]).then_inc(x2_done.sem, 1)

            def x2_low(p):
                x2t_h.wait(dve, p, 1)
                low(x2t_lo[:].rearrange("p k n -> p (k n)"), C0[:], x2t_hi[:].rearrange("p k n -> p (k n)"))\
                    .then_inc(x2t_l.sem, 1)

            def route(p):
                lg_ps.wait(dve, p, 1)
                dve.memset(wait_pad[:], 0.0)
                dve.max(top8[:], C1[:, 0:NE]).then_inc(lg_top.sem, 1)
                lg_top.wait(dve, p, 1)
                ro_done.wait(dve, p, 0)
                dve.tensor_tensor(rsum[:], top8[:, 0:1], top8[:, 1:2], ALU.add).then_inc(lg_sum.sem, 1)

            def ffn_sum(p):
                ro_done.wait(dve, p, 1)
                sh_ps.wait(dve, p, 1)
                dve.tensor_tensor(f_sb, C0[:], routed, ALU.add).then_inc(f_add.sem, 1)
                f_add.wait(dve, p, 1)
                statistics(2, p, f_sb)

            def ffn_norm(p):
                normalize(2, p, f_sb, f_sb).then_inc(f_nrm.sem, 1)

            def residual_c(p):
                f_gam.wait(dve, p, 1)
                xb_done.wait(dve, p, 1)
                dve.tensor_tensor(f_sb, f_sb, x2_beta, ALU.add).then_inc(f_res.sem, 1)
                f_res.wait(dve, p, 1)
                statistics(3, p, f_sb)

            def finish_c(p):
                y_out.wait(dve, p, 0)
                normalize(3, p, y_sb, f_sb).then_inc(y_done.sem, 1)

            def step(a, b, c):
                for r in range(ROUNDS):
                    if c is not None:
                        if r == 2:
                            x2_low(c)
                        if r == 3:
                            route(c)
                        if r == 9:
                            ffn_sum(c)
                        if r == 10:
                            ffn_norm(c)
                        if r == 12:
                            residual_c(c)
                        if r == 13:
                            finish_c(c)
                    if b is not None:
                        if r == 0:
                            stacks(b, c_in, cs, cs_h, cs_l)
                        if r == 1:
                            stacks(b, x1, xs, xs_h, xs_l)
                        if 1 <= r < 9:
                            key_turned(b, r - 1)
                        if r < 8:
                            key_max(b, r)
                        if r in (6, 11):
                            key_scale(b, r // 11)
                        if 9 <= r < 17:
                            query_sum(b, r - 9)
                        if 8 <= r < 16:
                            query_max(b, r - 8)
                        if r == 20:
                            output_center(b)
                            output_var(b)
                        if r == 21:
                            residual_b(b)
                        if r == 22:
                            finish_b(b)
                    if a is not None:
                        if r == 8:
                            x_low(a)
                        if r == 9:
                            q_low(a)
                        if 12 <= r < 16:
                            prob_sum(a, r - 12)
                        if 11 <= r < 15:
                            score_max(a, r - 11)
                        if r == 20:
                            residual_a(a)
                        if r == 22:
                            finish_a(a)

            drive(dve, setup_a, setup_b, setup_c, step)

        @block.scalar
        def _(act):
            def copy(o, i, scale=1.0):
                return act.activation(o, i, ACT.Copy, scale=scale)

            def setup_a():
                act.wait_ge(ld_wkv, 16)
                wkv_v = cw[:, 0, 0:KC * 2 * HD].rearrange("p (k n) -> p k n", k=KC)
                for k in range(KC):
                    ins = copy(wk_hi[:, k, :].rearrange("p (h d) -> p h d", h=HG),
                               wkv_v[:, k, None, 0:HD].broadcast_to([P, HG, HD]))
                ins.then_inc(hi_a, 1)
                copy(wv_hi[:], wkv_v[:, :, HD:2 * HD]).then_inc(hi_a, 1)
                act.wait_ge(ld_wq, 16)
                copy(wq_hi[:], cw[:, 1:5, :]).then_inc(hi_a, 1)
                act.wait_ge(ld_tab, 16)
                copy(ident_r[:], ident).then_inc(tab_r, 1)
                copy(causal_r[:], tab[:, T_CAUSAL:T_CAUSAL + SEQ]).then_inc(tab_r, 1)
                act.wait_ge(ld_bias, 16)
                copy(left_r[:].rearrange("p g t -> p (g t)"), ekt[:, 0, :]).then_inc(tab_r, 1)
                copy(right_r[:], ekt[:, 1, :]).then_inc(tab_r, 1)

            def setup_b():
                act.wait_ge(tr_b, 1)
                copy(xwq_hi[:], B0[:]).then_inc(hi_b, 1)
                act.wait_ge(tr_b, 2)
                copy(xwk_hi[:], B1[:]).then_inc(hi_b, 1)
                act.wait_ge(tr_b, 3)
                copy(eqt[0:XD, 0, :], B2[0:XD, :]).then_inc(hi_b, 1)
                act.wait_ge(tr_b, 4)
                copy(vout[:], B0[0:XD, :]).then_inc(g_b, 1)

            def setup_c():
                act.wait_ge(ld_up, 16)
                copy(up_hi[:].rearrange("p k n -> p (k n)"), cw[:].rearrange("p s n -> p (s n)")).then_inc(hi_c, 1)
                act.wait_ge(ld_gate, 16)
                copy(gate_hi[:], gate_sb[:]).then_inc(hi_c, 1)
                for n in range(4):
                    act.wait_ge(fold_ps, n + 1)
                    copy(cw[:, (5, 6, 0, 1)[n], :], (C0, C1)[n % 2][:]).then_inc(fold_sb, 1)
                for k in range(KC):
                    act.wait_ge(wr_ps, k + 1)
                    copy(wr_hi[:, k, :], (C0, C1)[k % 2][:]).then_inc(wr_h, 1)

            def load_x(p):
                if first(p):
                    return
                xt_ps.wait(act, p, 0)
                x_kept.wait(act, p, 0)
                act.dma_start(x_in[:], x[p]).then_inc(x_load.sem, 16)

            def load_c(p):
                ct_ps.wait(act, p, 0)
                cs_h.wait(act, p, 0)
                cs_l.wait(act, p, 0)
                act.dma_start(c_in[:], ctx[p]).then_inc(c_load.sem, 16)

            def store_y(p):
                y_done.wait(act, p, 1)
                act.dma_start(out[p], y_sb).then_inc(y_out.sem, 16)

            def keep(p):
                x_load.wait(act, p, 16)
                x1_done.wait(act, p, 0)
                copy(x_keep[:], x_in[:]).then_inc(x_kept.sem, 1)

            def x_high(p):
                xt_ps.wait(act, p, 1)
                copy(xt_hi[:].rearrange("p k n -> p (k n)"), A0[:]).then_inc(xt_h.sem, 1)

            def q_high(p):
                qt_ps.wait(act, p, 1)
                for b in range(2):
                    ins = copy(qt_hi[:, :, 2 * b * SEQ:(2 * b + 1) * SEQ],
                               A1[:].rearrange("p (g t) -> p g t", g=GROUPS)[:, :, b * SEQ:(b + 1) * SEQ], HD ** -0.5)
                ins.then_inc(qt_h.sem, 1)
                kv_ps.wait(act, p, 1)
                copy(kt_hi[:], A2[:, 0:P]).then_inc(kt_h.sem, 1)

            def prob_exp(p, g):
                s_sub.wait(act, p, g + 1)
                act.activation(prob[:, g % 2, :], prob[:, g % 2, :], ACT.Exp).then_inc(s_exp.sem, 1)

            def prob_turned(p, g):
                pt_ps.wait(act, p, g + 1)
                if g < 2:
                    ao_ps.wait(act, p, 0)
                else:
                    ao_ps.wait(act, p, g - 1)
                copy(pt_sb[:, g % 2, :], (A0, A0, A1, A0)[g][:]).then_inc(pt_done.sem, 1)

            def values_out(p):
                ao_ps.wait(act, p, 4)
                copy(ao_sb[:].rearrange("p g t -> p (g t)"), A2[:]).then_inc(ao_done.sem, 1)

            def stacks(p, src, o, h):
                for b in range(2):
                    rows = slice(b * SEQ, (b + 1) * SEQ)
                    copy(o[rows, b, :], src[rows, :]).then_inc(h.sem, 1)

            def c_high(p):
                c_load.wait(act, p, 16)
                k_ps.wait(act, p, 0)
                stacks(p, c_in, cs, cs_h)
                ct_ps.wait(act, p, 1)
                copy(ct_sb[:].rearrange("p k n -> p (k n)"), B0[:]).then_inc(ct_done.sem, 1)

            def x_stack(p):
                x1_done.wait(act, p, 1)
                q_ps.wait(act, p, 0)
                stacks(p, x1, xs, xs_h)

            def key_exp(p, u):
                k_neg.wait(act, p, u + 1)
                if u < 2:
                    kt_ps.wait(act, p, 0)
                    mt_done.wait(act, p, 0)
                else:
                    kt_ps.wait(act, p, u - 1)
                act.activation(ek[:, u % 2, :], B0[:], ACT.Exp, bias=kneg[:, u:u + 1],
                               accum_out=ksum[:, u:u + 1]).then_inc(k_exp.sem, 1)

            def context_out(p, b):
                t_ps.wait(act, p, (b + 1) * KC)
                copy(tctx[:], B2[0:SEQ, :]).then_inc(t_done.sem, 1)

            def query_exp(p, v):
                q_sub.wait(act, p, v + 1)
                act.activation(eq[:, v % 2, :], eq[:, v % 2, :], ACT.Exp).then_inc(q_exp.sem, 1)

            def query_turned(p, v):
                eqt_ps.wait(act, p, v + 1)
                if v < 2:
                    o_ps.wait(act, p, 0)
                else:
                    o_ps.wait(act, p, v - 1)
                copy(eqt[:, v % 2, :], B1[:]).then_inc(eqt_done.sem, 1)

            def output_square(p):
                o_cen.wait(act, p, 1)
                eqt_ps.wait(act, p, 8)
                act.activation(eq[:, 0, :], o_sb[:], ACT.Square).then_inc(o_sq.sem, 1)

            def x2_high(p):
                x2t_ps.wait(act, p, 1)
                copy(x2t_hi[:].rearrange("p k n -> p (k n)"), C0[:]).then_inc(x2t_h.sem, 1)

            def relu(p, j):
                h_ps.wait(act, p, j + 1)
                act.activation(h_sb[:, j, :], (C0, C1)[j][:], ACT.Relu).then_inc(h_relu.sem, 1)

            def hidden_turned(p, j):
                ht_ps.wait(act, p, j + 1)
                copy(ht_sb[:, j, :], (C0, C1)[j][:]).then_inc(ht_done.sem, 1)

            def routed_out(p):
                ro_ps.wait(act, p, 1)
                lg_sum.wait(act, p, 1)
                f_add.wait(act, p, 0)
                copy_scaled = act.activation(routed, C1[:], ACT.Copy, scale=rsum[:, 0:1])
                copy_scaled.then_inc(ro_done.sem, 1)

            def step(a, b, c):
                for r in range(ROUNDS):
                    if c is not None:
                        if r == 2:
                            x2_high(c)
                        if r in (3, 4):
                            relu(c, r - 3)
                        if r in (5, 6):
                            hidden_turned(c, r - 5)
                        if r == 9:
                            routed_out(c)
                        if r == 15:
                            store_y(c)
                    if b is not None:
                        if r == 0:
                            c_high(b)
                        if r == 1:
                            x_stack(b)
                        if r < 8:
                            key_exp(b, r)
                        if r in (5, 10):
                            context_out(b, r // 10)
                        if 10 <= r < 18:
                            query_turned(b, r - 10)
                        if 8 <= r < 16:
                            query_exp(b, r - 8)
                        if r == 20:
                            output_square(b)
                    if a is not None:
                        if r == 2:
                            load_x(a)
                        if r == 12:
                            load_c(a)
                        if r == 8:
                            x_high(a)
                            keep(a)
                        if r == 9:
                            q_high(a)
                        if 13 <= r < 17:
                            prob_turned(a, r - 13)
                        if 11 <= r < 15:
                            prob_exp(a, r - 11)
                        if r == 19:
                            values_out(a)

            drive(act, setup_a, setup_b, setup_c, step)

        @block.gpsimd
        def _(pool):
            def root(n, p):
                ln_eps[n].wait(pool, p, 1)
                pool.tensor_tensor(rstd[n][:], var_eps[n][:], minus_half[:, 0:1], ALU.pow).then_inc(ln_rstd[n].sem, 1)

            def setup_a():
                pool.memset(minus_half[:], -0.5).then_inc(halves, 1)
                pool.wait_ge(halves, 1)
                pool.wait_ge(ld_tab, 16)

            def setup_b():
                pass

            def setup_c():
                pool.wait_ge(ld_gb, 32)
                pool.wait_ge(wr_l, 4)
                pool.wait_ge(lo_c, 2)

            def keys_by_head(p):
                for part, s, kt, kd in ((0, kt_h, kt_hi, kd_hi), (1, kt_l, kt_lo, kd_lo)):
                    s.wait(pool, p, 1)
                    for b in range(2):
                        pool.tensor_tensor(kd[:, b], f32(kt[:, None, b * SEQ:(b + 1) * SEQ]).broadcast_to([P, HG, SEQ]),
                                           own[:, :, None].broadcast_to([P, HG, SEQ]), ALU.mult)\
                            .then_inc(kd_done.sem, 1)

            def prob_norm(p, g):
                s_rec.wait(pool, p, g + 1)
                v = prob[:, g % 2, :].rearrange("p (h k) -> p h k", h=HG)
                pool.tensor_tensor(v, v, srec[:, g, :, None].broadcast_to([P, HG, SEQ]), ALU.mult)\
                    .then_inc(s_nrm.sem, 1)

            def query_norm(p, v):
                q_rec.wait(pool, p, v + 1)
                w = eq[:, v % 2, :].rearrange("p (h d) -> p h d", h=XH)
                pool.tensor_tensor(w, w, qrec[:, v, :, None].broadcast_to([P, XH, XD]), ALU.mult)\
                    .then_inc(q_nrm.sem, 1)

            def output_norm(p):
                o_eps.wait(pool, p, 1)
                pool.tensor_tensor(orstd[:], ovar[:], minus_half[:], ALU.pow).then_inc(o_rstd.sem, 1)
                o_rstd.wait(pool, p, 1)
                w = o_sb[:].rearrange("p (t o) -> p t o", o=SEQ)
                pool.tensor_tensor(w, w, orstd[:, :, None].broadcast_to([P, UNITS, SEQ]), ALU.mult)\
                    .then_inc(o_nrm.sem, 1)

            def add_beta(p):
                x2_done.wait(pool, p, 1)
                f_res.wait(pool, p, 0)
                pool.tensor_tensor(x2_beta, x2[:], beta[:], ALU.add).then_inc(xb_done.sem, 1)

            def square(p, j):
                h_relu.wait(pool, p, j + 1)
                pool.tensor_tensor(h_sb[:, j, :], h_sb[:, j, :], h_sb[:, j, :], ALU.mult).then_inc(h_sq.sem, 1)

            def times_gamma(p):
                f_nrm.wait(pool, p, 1)
                pool.tensor_tensor(f_sb, f_sb, gamma[:], ALU.mult).then_inc(f_gam.sem, 1)

            def step(a, b, c):
                for r in range(ROUNDS):
                    if c is not None:
                        if r == 2:
                            add_beta(c)
                        if r in (3, 4):
                            square(c, r - 3)
                        if r == 9:
                            root(2, c)
                        if r == 11:
                            times_gamma(c)
                        if r == 12:
                            root(3, c)
                    if b is not None:
                        if 9 <= r < 17:
                            query_norm(b, r - 9)
                        if r == 20:
                            output_norm(b)
                        if r == 21:
                            root(1, b)
                    if a is not None:
                        if r == 9:
                            keys_by_head(a)
                        if 12 <= r < 16:
                            prob_norm(a, r - 12)
                        if r == 20:
                            root(0, a)

            drive(pool, setup_a, setup_b, setup_c, step)


_INS = ["x", "ctx_4096", "L0_attn_Wq", "L0_attn_Wkv", "L0_attn_Wo", "L0_xattn_Wq", "L0_xattn_Wkv", "L0_xattn_Wout",
        "L0_xattn_b_out", "L0_xattn_g", "L0_ffn_gate_w", "L0_ffn_up_w", "L0_ffn_down_w", "L0_ffn_fc1_w",
        "L0_ffn_fc2_w", "L0_ffn_expert_w", "L0_ffn_ln_gamma", "L0_ffn_ln_beta"]


def kernel(**inputs):
    import numpy as _np
    import concourse.bacc as _bacc
    from concourse.bass_utils import run_bass_kernel_spmd as _run

    nc = _bacc.Bacc("TRN2", target_bir_lowering=False, num_devices=1)
    arrays, args = {}, []
    for name in _INS:
        v = _np.ascontiguousarray(inputs[name])
        if name in ("x", "ctx_4096"):
            v = v.reshape(PAIRS, P, DM)
        arrays[f"in_{name}"] = v
        args.append(nc.dram_tensor(f"in_{name}", v.shape, F32, kind="ExternalInput").ap())
    arrays["tables"], arrays["bias_rows"] = shape_tables()
    args.append(nc.dram_tensor("tables", (P, T_ALL), F32, kind="ExternalInput").ap())
    args.append(nc.dram_tensor("bias_rows", (P, 2, DM), F32, kind="ExternalInput").ap())
    args.append(nc.dram_tensor("out", (PAIRS, P, DM), F32, kind="ExternalOutput").ap())
    decoder_kernel(nc, *args)
    r = _run(nc, [arrays], core_ids=[0])
    return r.results[0]["out"].reshape(BATCH, SEQ, DM)
```

```python
from contextlib import ExitStack

import numpy as np

import concourse.bass as bass
from concourse import mybir

F32 = mybir.dt.float32
F32R = mybir.dt.float32r
ALU = mybir.AluOpType
ACT = mybir.ActivationFunctionType
ALONG_FREE = mybir.AxisListType.X

P = 128
BATCH, SEQ, DM = 16, 64, 512
PAIRS = BATCH * SEQ // P
KC = DM // P
HEADS, HD = 32, 16
GROUPS = 4
HG = HEADS // GROUPS
XH, XD = 8, 64
INT, LAT, NE = 1024, 256, 8
IC, LC = INT // P, LAT // P
EPS = 1e-5
MASKED = -1e30
WINDOW = 3 * 2 * HD
ROUNDS, DEPTH = 16, 4
UNITS = 8


WHEN = {
    "load_x": [0], "load_c": [1],
    "x_turn": [2], "kv": [3], "q": [4, 5], "scores": [6, 7, 8, 9], "prob_sum": [7, 8, 9, 10],
    "prob_turn": [8, 9, 10, 11], "values": [10, 12], "project": [13, 14], "residual_a": [15], "finish_a": [16],
    "c_split": [4], "c_turn": [5], "keys": list(range(10, 18)), "keys_turn": list(range(11, 19)),
    "context": list(range(13, 21)), "combine": [17, 21], "combined": [18, 22],
    "queries": list(range(18, 26)), "query_sum": list(range(19, 27)), "queries_turn": list(range(20, 28)),
    "attend": list(range(21, 29)), "o_center": [28], "o_var": [29], "o_turn": [30], "residual_b": [31],
    "finish_b": [32],
    "x2_turn": [35], "logits": [36], "add_beta": [38], "hidden": [38, 39], "hidden_turn": [40, 41],
    "shared": [43, 46, 47, 48], "routing": [49], "ffn_sum": [50], "ffn_norm": [51], "residual_c": [52],
    "finish_c": [53], "store": [54],
}


def shape_tables():
    start = 2.0 ** (-2.0 ** (-(np.log2(HEADS) - 3)))
    slopes = np.array([start ** (i + 1) for i in range(HEADS)], dtype=np.float32)
    pos = np.arange(SEQ)
    causal = np.where(pos[None, :] <= pos[:, None], 0.0, MASKED).astype(np.float32)
    causal = np.concatenate([causal, causal], 0)
    own = np.zeros((P, HG), np.float32)
    for h in range(HG):
        own[h * HD:(h + 1) * HD, h] = 1.0
    q = np.tile(pos, 2).astype(np.float32)
    left = np.zeros((P, GROUPS, P), np.float32)
    right = np.zeros((P, HG, SEQ), np.float32)
    for h in range(HG):
        for g in range(GROUPS):
            for r, v in ((0, slopes[g * HG + h] * np.ones(P, np.float32)), (2, slopes[g * HG + h] * q)):
                v = v.astype(np.float32)
                hi = (v.view(np.uint32) & np.uint32(0xFFFFF000)).view(np.float32)
                left[r * HG + h, g] = hi
                left[(r + 1) * HG + h, g] = v - hi
        right[h, h] = right[HG + h, h] = pos
        right[2 * HG + h, h] = right[3 * HG + h, h] = -1.0
    return (np.concatenate([np.eye(P, dtype=np.float32), causal, own], 1),
            np.stack([left.reshape(P, -1), right.reshape(P, -1)], 1))


T_IDENT, T_CAUSAL, T_OWN, T_ALL = 0, P, P + SEQ, P + SEQ + HG


class Signal:

    def __init__(self, sem, per):
        self.sem, self.per = sem, per

    def wait(self, eng, pair, nth):
        value = pair * self.per + nth
        if not isinstance(value, int) or value > 0:
            eng.wait_ge(self.sem, value)


def decoder_kernel(nc, x, ctx, wq, wkv, wo, xwq, xwkv, xwout, xb_out, xg, gate_w, up_w, down_w,
                   fc1_w, fc2_w, expert_w, ln_gamma, ln_beta, tables, bias_rows, out):
    stack = ExitStack()
    with stack:
        def sb(name, shape, dt=F32):
            return stack.enter_context(nc.sbuf_tensor(name, shape, dt))

        def sem(name):
            return stack.enter_context(nc.semaphore(name))

        def sig(name, per=1):
            return Signal(sem(name), per)

        tab = sb("tab", [P, T_ALL])
        ident = tab[:, T_IDENT:T_IDENT + P]
        own = tab[:, T_OWN:T_OWN + HG]
        ident_r = sb("ident_r", [P, P], F32R)
        causal_r = sb("causal_r", [P, SEQ], F32R)
        left_r = sb("left_r", [P, GROUPS, P], F32R)
        right_r = sb("right_r", [P, HG * SEQ], F32R)
        wq_hi, wq_lo = sb("wq_hi", [P, KC, DM], F32R), sb("wq_lo", [P, KC, DM], F32R)
        wk_hi, wk_lo = sb("wk_hi", [P, KC, P], F32R), sb("wk_lo", [P, KC, P], F32R)
        wv_hi, wv_lo = sb("wv_hi", [P, KC, HD], F32R), sb("wv_lo", [P, KC, HD], F32R)
        wo_sb = sb("wo_sb", [P, KC, DM])
        xwq_hi, xwq_lo = sb("xwq_hi", [P, DM], F32R), sb("xwq_lo", [P, DM], F32R)
        xwk_hi, xwk_lo = sb("xwk_hi", [P, DM], F32R), sb("xwk_lo", [P, DM], F32R)
        vout = sb("vout", [XD, XH * SEQ])
        bout = sb("bout", [P, SEQ])
        gcol = sb("gcol", [P, 1])
        gate_sb = sb("gate_sb", [P, KC, NE])
        gate_hi, gate_lo = sb("gate_hi", [P, KC, NE], F32R), sb("gate_lo", [P, KC, NE], F32R)
        up_hi, up_lo = sb("up_hi", [P, KC, INT], F32R), sb("up_lo", [P, KC, INT], F32R)
        down_sb = sb("down_sb", [P, IC, DM])
        wr_hi, wr_lo = sb("wr_hi", [P, KC, DM], F32R), sb("wr_lo", [P, KC, DM], F32R)
        gamma, beta = sb("gamma", [P, DM]), sb("beta", [P, DM])
        minus_half = sb("minus_half", [P, UNITS])

        x_in, x_keep, x1 = sb("x_in", [P, DM]), sb("x_keep", [P, DM]), sb("x1", [P, DM])
        xt_hi, xt_lo = sb("xt_hi", [P, KC, P], F32R), sb("xt_lo", [P, KC, P], F32R)
        qt_hi, qt_lo = sb("qt_hi", [P, GROUPS, 3 * SEQ], F32R), sb("qt_lo", [P, GROUPS, 3 * SEQ], F32R)
        kt_hi, kt_lo = sb("kt_hi", [P, P], F32R), sb("kt_lo", [P, P], F32R)
        kd_hi, kd_lo = sb("kd_hi", [P, 2, HG, SEQ], F32R), sb("kd_lo", [P, 2, HG, SEQ], F32R)
        vwin = sb("vwin", [P, 2, 2 * WINDOW + 2 * HD])
        prob = sb("prob", [P, 2, HG * SEQ])
        pt_sb = sb("pt_sb", [P, 2, DM])
        ao_sb = sb("ao_sb", [P, GROUPS, P])
        smax, ssum, srec = sb("smax", [P, GROUPS, HG]), sb("ssum", [P, GROUPS, HG]), sb("srec", [P, GROUPS, HG])
        c_in = sb("c_in", [P, DM])
        xs, cs = sb("xs", [P, 2, DM], F32R), sb("cs", [P, 2, DM], F32R)
        ct_sb = sb("ct_sb", [P, KC, P])
        ek, ekt = sb("ek", [P, 2, DM]), sb("ekt", [P, 2, DM])
        tctx = sb("tctx", [XD, DM])
        mt = sb("mt", [P, 2, KC, SEQ])
        eq, eqt = sb("eq", [P, 2, DM]), sb("eqt", [P, 2, DM])
        kneg, ksum, krec = sb("kneg", [P, UNITS]), sb("ksum", [P, UNITS]), sb("krec", [P, UNITS])
        kmax = sb("kmax", [P, UNITS])
        qmax, qsum, qrec = sb("qmax", [P, UNITS, XH]), sb("qsum", [P, UNITS, XH]), sb("qrec", [P, UNITS, XH])
        o_sb, x2 = sb("o_sb", [P, DM]), sb("x2", [P, DM])
        zb_sb = o_sb
        omean, ovar, orstd = sb("omean", [P, UNITS]), sb("ovar", [P, UNITS]), sb("orstd", [P, UNITS])
        x2t_hi, x2t_lo = sb("x2t_hi", [P, KC, P], F32R), sb("x2t_lo", [P, KC, P], F32R)
        cw = sb("cw", [P, 8, DM])
        h_sb, ht_sb = cw[:, 0:2, :], cw[:, 2:4, :]
        routed, f_sb, x2_beta, y_sb = cw[:, 4, :], cw[:, 5, :], cw[:, 6, :], cw[:, 7, :]
        top8, rsum = sb("top8", [P, NE]), sb("rsum", [P, 1])
        stats = [sb(f"stats{n}", [P, 6]) for n in range(4)]
        meanvar = [sb(f"meanvar{n}", [P, 2]) for n in range(4)]
        var_eps = [sb(f"var_eps{n}", [P, 1]) for n in range(4)]
        rstd = [sb(f"rstd{n}", [P, 1]) for n in range(4)]

        wait_pad = sb("wait_pad", [P, 1])

        bank = [stack.enter_context(nc.psum_tensor(f"bank{n}", [P, DM], F32)) for n in range(8)]
        A0, A1, A2, B0, B1, B2, C0, C1 = bank

        ld_tab, ld_bias, ld_wq, ld_wkv, ld_wo = sem("ld_tab"), sem("ld_bias"), sem("ld_wq"), sem("ld_wkv"), sem("ld_wo")
        ld_xwq, ld_xwk, ld_xwv, ld_xwo, ld_xb = (sem("ld_xwq"), sem("ld_xwk"), sem("ld_xwv"), sem("ld_xwo"),
                                                 sem("ld_xb"))
        ld_up, ld_down, ld_gate, ld_fc, ld_gb = sem("ld_up"), sem("ld_down"), sem("ld_gate"), sem("ld_fc"), sem("ld_gb")
        tab_r, hi_a, lo_a, zeroed = sem("tab_r"), sem("hi_a"), sem("lo_a"), sem("zeroed")
        tr_b, hi_b, lo_b, g_b = sem("tr_b"), sem("hi_b"), sem("lo_b"), sem("g_b")
        hi_c, lo_c, fold_ps, fold_sb, wr_ps, wr_h, wr_l = (sem("hi_c"), sem("lo_c"), sem("fold_ps"), sem("fold_sb"),
                                                           sem("wr_ps"), sem("wr_h"), sem("wr_l"))
        halves = sem("halves")

        x_load, x_kept = sig("x_load", 16), sig("x_kept")
        xt_ps, xt_h, xt_l = sig("xt_ps"), sig("xt_h"), sig("xt_l")
        qt_ps, qt_h, qt_l = sig("qt_ps"), sig("qt_h"), sig("qt_l")
        kv_ps, kt_h, kt_l, v_win = sig("kv_ps"), sig("kt_h"), sig("kt_l"), sig("v_win")
        kd_done = sig("kd_done", 4)
        s_ps, s_max, s_sub, s_exp = sig("s_ps", 4), sig("s_max", 4), sig("s_sub", 4), sig("s_exp", 4)
        s_sum, s_rec, s_nrm = sig("s_sum", 4), sig("s_rec", 4), sig("s_nrm", 4)
        pt_ps, pt_done, ao_ps, ao_done = sig("pt_ps", 4), sig("pt_done", 4), sig("ao_ps", 2), sig("ao_done")
        y_ps, z_done = sig("y_ps"), sig("z_done")
        ln_stat = [sig(f"ln_stat{n}") for n in range(4)]
        ln_mean = [sig(f"ln_mean{n}") for n in range(4)]
        ln_eps = [sig(f"ln_eps{n}") for n in range(4)]
        ln_rstd = [sig(f"ln_rstd{n}") for n in range(4)]
        x1_done = sig("x1_done")
        c_load, ct_ps, ct_done = sig("c_load", 16), sig("ct_ps"), sig("ct_done")
        cs_h, cs_l, xs_h, xs_l = sig("cs_h", 2), sig("cs_l", 2), sig("xs_h", 2), sig("xs_l", 2)
        k_ps, k_max, k_neg, k_exp = sig("k_ps", 8), sig("k_max", 8), sig("k_neg", 8), sig("k_exp", 8)
        kt_ps, ekt_done, t_ps, t_done, m_ps = sig("kt_ps", 8), sig("ekt_done", 8), sig("t_ps", 8), sig("t_done", 2), sig("m_ps", 2)
        k_rec, k_scl, mt_done = sig("k_rec", 2), sig("k_scl", 2), sig("mt_done", 2)
        q_ps, q_max, q_sub, q_exp = sig("q_ps", 8), sig("q_max", 8), sig("q_sub", 8), sig("q_exp", 8)
        q_sum, q_rec, q_nrm = sig("q_sum", 8), sig("q_rec", 8), sig("q_nrm", 8)
        eqt_ps, eqt_done, o_ps = sig("eqt_ps", 8), sig("eqt_done", 8), sig("o_ps", 8)
        o_add, o_sum, o_mean, o_cen, o_sq, o_var, o_eps, o_rstd, o_nrm = (
            sig("o_add"), sig("o_sum"), sig("o_mean"), sig("o_cen"), sig("o_sq"), sig("o_var"), sig("o_eps"),
            sig("o_rstd"), sig("o_nrm"))
        ot_ps, zb_done, x2_done = sig("ot_ps"), sig("zb_done"), sig("x2_done")
        x2t_ps, x2t_h, x2t_l, xb_done = sig("x2t_ps"), sig("x2t_h"), sig("x2t_l"), sig("xb_done")
        lg_ps, lg_top, lg_sum = sig("lg_ps"), sig("lg_top"), sig("lg_sum")
        h_ps, h_relu, h_sq, ht_ps, ht_done = sig("h_ps", 2), sig("h_relu", 2), sig("h_sq", 2), sig("ht_ps", 2), sig("ht_done", 2)
        sh_ps, ro_ps, ro_done, f_add, f_nrm, f_gam, f_res, y_done, y_out = (
            sig("sh_ps"), sig("ro_ps"), sig("ro_done"), sig("f_add"), sig("f_nrm"), sig("f_gam"), sig("f_res"),
            sig("y_done"), sig("y_out", 16))

        block = stack.enter_context(nc.Block())

        def due(pairs, rnd):
            def of(name):
                return [(pairs[t // ROUNDS], part) for part, t in enumerate(WHEN[name])
                        if t % ROUNDS == rnd and pairs[t // ROUNDS] is not None]
            return of

        def drive(eng, setup_a, setup_b, setup_c, work):
            def step(i):
                inside = [i - k if not isinstance(i, int) or 0 <= i - k < PAIRS else None for k in range(DEPTH)]
                for rnd in range(ROUNDS):
                    work(due(inside, rnd))

            setup_a()
            setup_b()
            step(0)
            step(1)
            setup_c()
            step(2)
            with eng.Fori(DEPTH - 1, PAIRS) as i:
                step(i)
            for i in range(PAIRS, PAIRS + DEPTH - 1):
                step(i)

        def first(p):
            return isinstance(p, int) and p == 0

        def f32(ap):
            return ap.bitcast(F32)

        @block.sync
        def _(sp):
            sp.dma_start(x_in[:], x[0]).then_inc(x_load.sem, 16)
            sp.dma_start(tab[:], tables).then_inc(ld_tab, 16)
            sp.dma_start(ekt[:], bias_rows).then_inc(ld_bias, 16)
            sp.dma_start(cw[:, 0, 0:KC * 2 * HD].rearrange("p (k n) -> p k n", k=KC),
                         wkv.rearrange("(k p) n -> p k n", p=P)).then_inc(ld_wkv, 16)
            sp.dma_start(cw[:, 1:5, :], wq.rearrange("(k p) n -> p k n", p=P)).then_inc(ld_wq, 16)
            sp.dma_start(wo_sb[:], wo.rearrange("(k p) n -> p k n", p=P)).then_inc(ld_wo, 16)
            for slot, s, rows in ((ek, ld_xwq, xwq), (eq, ld_xwk, xwkv[0:DM, :])):
                for twice in range(2):
                    sp.dma_start(slot[:, 0, :].rearrange("p (k t c) -> p k t c", k=KC, t=2)[:, :, twice, :],
                                 rows.rearrange("(k p) c -> p k c", p=P)).then_inc(s, 16)
            sp.wait_ge(tab_r, 4)
            sp.dma_start(ekt[0:XD, 0, :].rearrange("e (h c) -> e h c", h=XH),
                         xwkv[DM:2 * DM, :].rearrange("(h e) c -> e h c", h=XH)).then_inc(ld_xwv, 16)
            sp.dma_start(ekt[0:SEQ, 1, :], xwout).then_inc(ld_xwo, 16)
            sp.dma_start(bout[:], xb_out.partition_broadcast(P)).then_inc(ld_xb, 16)
            for b in range(2):
                sp.dma_start(gcol[b * SEQ:(b + 1) * SEQ, :], xg.rearrange("a c n -> (a c) n")).then_inc(ld_xb, 16)
            sp.dma_start(down_sb[:], down_w.rearrange("(k p) n -> p k n", p=P)).then_inc(ld_down, 16)
            sp.dma_start(gamma[:], ln_gamma.partition_broadcast(P)).then_inc(ld_gb, 16)
            sp.dma_start(beta[:], ln_beta.partition_broadcast(P)).then_inc(ld_gb, 16)
            sp.wait_ge(hi_a, 3)
            sp.wait_ge(lo_a, 3)
            sp.dma_start(cw[:].rearrange("p (k j) n -> p k j n", k=KC),
                         up_w.rearrange("(k p) (j n) -> p k j n", p=P, j=2)).then_inc(ld_up, 16)
            sp.dma_start(gate_sb[:],
                         gate_w.rearrange("(k p) n -> p k n", p=P)).then_inc(ld_gate, 16)
            sp.wait_ge(hi_c, 1)
            sp.wait_ge(lo_c, 1)
            sp.dma_start(cw[:, 0:2, :].rearrange("p j n -> p (j n)").rearrange("p (k n) -> p k n", k=KC),
                         fc1_w.rearrange("(k p) n -> p k n", p=P)).then_inc(ld_fc, 16)
            sp.dma_start(cw[:, 2, :].rearrange("p (k n) -> p k n", k=LC),
                         expert_w.rearrange("(k p) n -> p k n", p=P)).then_inc(ld_fc, 16)
            sp.dma_start(cw[:, 3:5, :], fc2_w.rearrange("(k p) n -> p k n", p=P)).then_inc(ld_fc, 16)
            y_out.wait(sp, PAIRS, 0)

        @block.tensor
        def _(pe):
            def product(o, pairs_of, start, stop, **kw):
                n = len(pairs_of)
                for j, (l, r) in enumerate(pairs_of):
                    ins = pe.matmul(o, l, r, start=start and j == 0, stop=stop and j == n - 1, **kw)
                return ins

            def split(l_hi, l_lo, r_hi, r_lo):
                return [(l_hi, r_hi), (l_hi, r_lo), (l_lo, r_hi)]

            def turn(o, src):
                for j in range(KC):
                    ins = pe.transpose(o[:, j * P:(j + 1) * P], src[:, j * P:(j + 1) * P], ident)
                return ins

            def setup_a():
                pe.wait_ge(ld_tab, 16)

            def setup_b():
                for s, slot, o in ((ld_xwq, ek, B0), (ld_xwk, eq, B1)):
                    pe.wait_ge(s, 32)
                    turn(o, slot[:, 0, :]).then_inc(tr_b, 1)
                pe.wait_ge(ld_xwo, 16)
                for h in range(XH):
                    ins = pe.transpose(B2[0:XD, h * SEQ:(h + 1) * SEQ], ekt[0:SEQ, 1, h * XD:(h + 1) * XD],
                                       ident[0:SEQ, 0:SEQ])
                ins.then_inc(tr_b, 1)
                pe.wait_ge(hi_b, 3)
                pe.wait_ge(lo_b, 2)
                pe.wait_ge(ld_xwv, 16)
                for h in range(XH):
                    ins = pe.matmul(B0[0:XD, h * SEQ:(h + 1) * SEQ], ekt[0:XD, 0, h * XD:(h + 1) * XD],
                                    eqt[0:XD, 0, h * SEQ:(h + 1) * SEQ], start=True, stop=True)
                ins.then_inc(tr_b, 1)
                pe.wait_ge(g_b, 1)

            def setup_c():
                pe.wait_ge(ld_fc, 48)
                fc1 = cw[:, 0:2, :].rearrange("p j n -> p (j n)").rearrange("p (k n) -> p k n", k=KC)
                for l, o in enumerate((C0, C1)):
                    for k in range(KC):
                        ins = pe.transpose(o[:, k * P:(k + 1) * P], fc1[:, k, l * P:(l + 1) * P], ident)
                    ins.then_inc(fold_ps, 1)
                pe.wait_ge(fold_sb, 2)
                for m, o in enumerate((C0, C1)):
                    product(o[:], [(cw[:, 2, l * LAT + m * P:l * LAT + (m + 1) * P], cw[:, 5 + l, :])
                                   for l in range(LC)], True, True).then_inc(fold_ps, 1)
                pe.wait_ge(fold_sb, 4)
                for k in range(KC):
                    if k >= 2:
                        pe.wait_ge(wr_h, k - 1)
                        pe.wait_ge(wr_l, k - 1)
                    product((C0, C1)[k % 2][:], [(cw[:, m, k * P:(k + 1) * P], cw[:, 3 + m, :]) for m in range(LC)],
                            True, True).then_inc(wr_ps, 1)
                pe.wait_ge(wr_h, 4)
                pe.wait_ge(wr_l, 4)
                pe.wait_ge(hi_c, 2)
                pe.wait_ge(lo_c, 2)
                pe.wait_ge(ld_down, 16)

            def x_turn(p):
                x_load.wait(pe, p, 16)
                pt_done.wait(pe, p, 0)
                turn(A0, x_in).then_inc(xt_ps.sem, 1)

            def keys_values(p):
                if first(p):
                    pe.wait_ge(hi_a, 2)
                    pe.wait_ge(lo_a, 2)
                xt_h.wait(pe, p, 1)
                xt_l.wait(pe, p, 1)
                zb_done.wait(pe, p - 1, 0)
                product(A2[:, 0:P], [t for k in range(KC) for t in
                                     split(wk_hi[:, k, :], wk_lo[:, k, :], xt_hi[:, k, :], xt_lo[:, k, :])],
                        True, True)
                product(A2[:, P:P + HD], [t for k in range(KC) for t in
                                          split(xt_hi[:, k, :], xt_lo[:, k, :], wv_hi[:, k, :], wv_lo[:, k, :])],
                        True, True).then_inc(kv_ps.sem, 1)

            def head_queries(p, half):
                if first(p):
                    pe.wait_ge(hi_a, 3)
                    pe.wait_ge(lo_a, 3)
                if half == 0:
                    z_done.wait(pe, p, 0)
                for g in (2 * half, 2 * half + 1):
                    cols = slice(g * P, (g + 1) * P)
                    ins = product(A1[:, cols], [t for k in range(KC) for t in
                                                split(wq_hi[:, k, cols], wq_lo[:, k, cols],
                                                      xt_hi[:, k, :], xt_lo[:, k, :])], True, True)
                if half == 1:
                    ins.then_inc(qt_ps.sem, 1)

            S_BANK = (A0, A1, A2, A1)

            def scores(p, g):
                if g == 0:
                    if first(p):
                        pe.wait_ge(tab_r, 4)
                        pe.wait_ge(zeroed, 3)
                    qt_h.wait(pe, p, 1)
                    qt_l.wait(pe, p, 1)
                    kd_done.wait(pe, p, 4)
                if g == 2:
                    ct_done.wait(pe, p, 1)
                if g == 3:
                    s_sub.wait(pe, p, 2)
                terms = []
                for b in range(2):
                    qh = qt_hi[:, g, b * SEQ:b * SEQ + P]
                    ql = qt_lo[:, g, b * SEQ:b * SEQ + P]
                    kh = kd_hi[:, b].rearrange("p h k -> p (h k)")
                    kl = kd_lo[:, b].rearrange("p h k -> p (h k)")
                    terms += split(qh, ql, kh, kl)
                terms.append((left_r[:, g, :], right_r[:]))
                terms.append((ident_r[:], causal_r[:, None, :].broadcast_to([P, HG, SEQ])))
                product(S_BANK[g][:], terms, True, True).then_inc(s_ps.sem, 1)

            PT_BANK = (A0, A0, A1, A0)

            def prob_turn(p, g):
                s_nrm.wait(pe, p, g + 1)
                if g in (1, 3):
                    pt_done.wait(pe, p, g)
                if g == 2:
                    s_sub.wait(pe, p, 4)
                turn(PT_BANK[g], prob[:, g % 2, :]).then_inc(pt_ps.sem, 1)

            def values(p, half):
                pt_done.wait(pe, p, 2 * half + 2)
                if half == 0:
                    s_sub.wait(pe, p, 3)
                    v_win.wait(pe, p, 1)
                for b in range(2):
                    ins = product(A2[:].rearrange("p (g t) -> p g t", g=GROUPS)[:, 2 * half:2 * half + 2,
                                                                                b * SEQ:(b + 1) * SEQ],
                                  [(vwin[:, b, WINDOW - 2 * HD * j:WINDOW - 2 * HD * j + P],
                                    pt_sb[:, :, j * P + b * SEQ:j * P + (b + 1) * SEQ])
                                   for j in range(HG // 2)], True, True)
                ins.then_inc(ao_ps.sem, 1)

            def project(p, half):
                if first(p):
                    pe.wait_ge(ld_wo, 16)
                if half == 0:
                    ao_done.wait(pe, p, 1)
                    pt_done.wait(pe, p, 3)
                ins = product(A1[:], [(ao_sb[:, g, :], wo_sb[:, g, :]) for g in (2 * half, 2 * half + 1)],
                              half == 0, half == 1)
                if half == 1:
                    ins.then_inc(y_ps.sem, 1)

            def c_turn(p):
                c_load.wait(pe, p, 16)
                kt_l.wait(pe, p, 1)
                v_win.wait(pe, p, 1)
                turn(A2, c_in).then_inc(ct_ps.sem, 1)

            def keys(p, u):
                b, blk = divmod(u, KC)
                if u == 0:
                    cs_h.wait(pe, p, 2)
                    cs_l.wait(pe, p, 2)
                    q_sub.wait(pe, p, 0)
                else:
                    k_exp.wait(pe, p, u)
                cols = slice(blk * P, (blk + 1) * P)
                product(B0[:], [(xwk_hi[:, cols], cs[:, b, :]), (xwk_lo[:, cols], cs[:, b, :])],
                        True, True).then_inc(k_ps.sem, 1)

            def keys_turn(p, u):
                k_exp.wait(pe, p, u + 1)
                if u == 0:
                    eqt_done.wait(pe, p, 0)
                elif u == 7:
                    mt_done.wait(pe, p, 1)
                else:
                    ekt_done.wait(pe, p, u)
                turn(B1, ek[:, u % 2, :]).then_inc(kt_ps.sem, 1)

            def context(p, u):
                b, blk = divmod(u, KC)
                ekt_done.wait(pe, p, u + 1)
                if u == 0:
                    o_add.wait(pe, p, 0)
                    ct_done.wait(pe, p, 1)
                if u == KC:
                    t_done.wait(pe, p, 1)
                product(B2[0:SEQ, blk * P:(blk + 1) * P],
                        [(ct_sb[:, n, b * SEQ:(b + 1) * SEQ], ekt[:, u % 2, n * P:(n + 1) * P]) for n in range(KC)],
                        True, True).then_inc(t_ps.sem, 1)

            def combine(p, b):
                t_done.wait(pe, p, b + 1)
                if b == 0:
                    ekt_done.wait(pe, p, 7)
                else:
                    eqt_done.wait(pe, p, 2)
                for blk in range(KC):
                    cols = slice(blk * P, (blk + 1) * P)
                    ins = pe.matmul(B1[:, cols], tctx[:, cols], vout[:, cols], start=True, stop=True)
                ins.then_inc(m_ps.sem, 1)

            def queries(p, v):
                b, n = divmod(v, KC)
                if v == 0:
                    xs_h.wait(pe, p, 2)
                    xs_l.wait(pe, p, 2)
                    k_exp.wait(pe, p, 8)
                else:
                    q_sub.wait(pe, p, v)
                cols = slice(n * P, (n + 1) * P)
                product(B0[:], [(xs[:, b, cols], xwq_hi[:]), (xs[:, b, cols], xwq_lo[:])],
                        True, True).then_inc(q_ps.sem, 1)

            def queries_turn(p, v):
                q_nrm.wait(pe, p, v + 1)
                if v == 0:
                    ekt_done.wait(pe, p, 8)
                elif v == 2:
                    mt_done.wait(pe, p, 2)
                else:
                    eqt_done.wait(pe, p, v)
                turn(B1, eq[:, v % 2, :]).then_inc(eqt_ps.sem, 1)

            def attend(p, v):
                b, n = divmod(v, KC)
                eqt_done.wait(pe, p, v + 1)
                if v == 0:
                    t_done.wait(pe, p, 2)
                mt_done.wait(pe, p, b + 1)
                product(B2[:, n * P + b * SEQ:n * P + (b + 1) * SEQ],
                        [(eqt[:, v % 2, blk * P:(blk + 1) * P], mt[:, b, blk, :]) for blk in range(KC)],
                        True, True).then_inc(o_ps.sem, 1)

            def o_turn(p):
                o_nrm.wait(pe, p, 1)
                if not isinstance(p, int) or p + 1 < PAIRS:
                    ao_done.wait(pe, p + 1, 1)
                turn(A2, o_sb).then_inc(ot_ps.sem, 1)

            def x2_turn(p):
                x2_done.wait(pe, p, 1)
                f_add.wait(pe, p, 0)
                turn(C0, x2).then_inc(x2t_ps.sem, 1)

            def logits(p):
                x2t_h.wait(pe, p, 1)
                x2t_l.wait(pe, p, 1)
                ro_done.wait(pe, p, 0)
                product(C1[:, 0:NE], [t for k in range(KC) for t in
                                      split(x2t_hi[:, k, :], x2t_lo[:, k, :], gate_hi[:, k, :], gate_lo[:, k, :])],
                        True, True).then_inc(lg_ps.sem, 1)

            def hidden(p, j):
                if j == 1:
                    lg_top.wait(pe, p, 1)
                cols = slice(j * DM, (j + 1) * DM)
                product((C0, C1)[j][:], [t for k in range(KC) for t in
                                         split(x2t_hi[:, k, :], x2t_lo[:, k, :], up_hi[:, k, cols], up_lo[:, k, cols])],
                        True, True).then_inc(h_ps.sem, 1)

            def hidden_turn(p, j):
                h_sq.wait(pe, p, j + 1)
                turn((C0, C1)[j], h_sb[:, j, :]).then_inc(ht_ps.sem, 1)

            def shared(p, part):
                if part == 0:
                    ht_done.wait(pe, p, 2)
                ins = product(C0[:], [(ht_sb[:, n // KC, (n % KC) * P:(n % KC + 1) * P], down_sb[:, n, :])
                                      for n in (2 * part, 2 * part + 1)], part == 0, part == 3)
                if part == 3:
                    ins.then_inc(sh_ps.sem, 1)

            def routing(p):
                product(C1[:], [t for k in range(KC) for t in
                                split(x2t_hi[:, k, :], x2t_lo[:, k, :], wr_hi[:, k, :], wr_lo[:, k, :])],
                        True, True).then_inc(ro_ps.sem, 1)

            def work(due):
                for p, v in due("attend"):
                    attend(p, v)
                for p, u in due("context"):
                    context(p, u)
                for p, v in due("queries_turn"):
                    queries_turn(p, v)
                for p, u in due("keys_turn"):
                    keys_turn(p, u)
                for p, u in due("keys"):
                    keys(p, u)
                for p, v in due("queries"):
                    queries(p, v)
                for p, _ in due("x_turn"):
                    x_turn(p)
                for p, _ in due("kv"):
                    keys_values(p)
                for p, half in due("q"):
                    head_queries(p, half)
                for p, g in due("prob_turn"):
                    prob_turn(p, g)
                for p, g in due("scores"):
                    scores(p, g)
                for p, half in due("values"):
                    values(p, half)
                for p, half in due("project"):
                    project(p, half)
                for p, _ in due("c_turn"):
                    c_turn(p)
                for p, _ in due("x2_turn"):
                    x2_turn(p)
                for p, _ in due("logits"):
                    logits(p)
                for p, j in due("hidden"):
                    hidden(p, j)
                for p, j in due("hidden_turn"):
                    hidden_turn(p, j)
                for p, part in due("shared"):
                    shared(p, part)
                for p, _ in due("routing"):
                    routing(p)
                for p, b in due("combine"):
                    combine(p, b)
                for p, _ in due("o_turn"):
                    o_turn(p)

            drive(pe, setup_a, setup_b, setup_c, work)

        @block.vector
        def _(dve):
            def low(o, whole, hi):
                return dve.tensor_tensor(o, whole, f32(hi), ALU.subtract)

            def statistics(n, p, z):
                dve.bn_stats(stats[n][:], z).then_inc(ln_stat[n].sem, 1)
                ln_stat[n].wait(dve, p, 1)
                dve.memset(wait_pad[:], 0.0)
                dve.bn_aggr(meanvar[n][:], stats[n][:]).then_inc(ln_mean[n].sem, 1)
                ln_mean[n].wait(dve, p, 1)
                dve.tensor_scalar(var_eps[n][:], meanvar[n][:, 1:2], EPS, None, ALU.add).then_inc(ln_eps[n].sem, 1)

            def normalize(n, p, o, z):
                ln_rstd[n].wait(dve, p, 1)
                return dve.tensor_scalar(o, z, meanvar[n][:, 0:1], rstd[n][:, 0:1], ALU.subtract, ALU.mult)

            def setup_a():
                for z in (qt_hi, qt_lo):
                    dve.memset(f32(z[:, :, SEQ:2 * SEQ]), 0.0).then_inc(zeroed, 1)
                dve.memset(vwin[:], 0.0).then_inc(zeroed, 1)
                dve.wait_ge(zeroed, 3)
                dve.wait_ge(ld_wkv, 16)
                wkv_v = cw[:, 0, 0:KC * 2 * HD].rearrange("p (k n) -> p k n", k=KC)
                dve.wait_ge(hi_a, 2)
                for k in range(KC):
                    ins = low(wk_lo[:, k, :].rearrange("p (h d) -> p h d", h=HG),
                              wkv_v[:, k, None, 0:HD].broadcast_to([P, HG, HD]),
                              wk_hi[:, k, :].rearrange("p (h d) -> p h d", h=HG))
                ins.then_inc(lo_a, 1)
                low(wv_lo[:], wkv_v[:, :, HD:2 * HD], wv_hi[:]).then_inc(lo_a, 1)
                dve.wait_ge(hi_a, 3)
                low(wq_lo[:], cw[:, 1:5, :], wq_hi[:]).then_inc(lo_a, 1)

            def setup_b():
                for n, (o, hi, ps) in enumerate(((xwq_lo, xwq_hi, B0), (xwk_lo, xwk_hi, B1))):
                    dve.wait_ge(hi_b, n + 1)
                    low(o[:], ps[:], hi[:]).then_inc(lo_b, 1)
                dve.wait_ge(ld_xb, 48)

            def setup_c():
                dve.wait_ge(hi_c, 1)
                low(up_lo[:].rearrange("p k n -> p (k n)"), cw[:].rearrange("p s n -> p (s n)"),
                    up_hi[:].rearrange("p k n -> p (k n)")).then_inc(lo_c, 1)
                dve.wait_ge(hi_c, 2)
                low(gate_lo[:], gate_sb[:], gate_hi[:]).then_inc(lo_c, 1)
                for k in range(KC):
                    dve.wait_ge(wr_h, k + 1)
                    low(wr_lo[:, k, :], (C0, C1)[k % 2][:], wr_hi[:, k, :]).then_inc(wr_l, 1)

            def x_low(p):
                xt_h.wait(dve, p, 1)
                low(xt_lo[:].rearrange("p k n -> p (k n)"), A0[:], xt_hi[:].rearrange("p k n -> p (k n)"))\
                    .then_inc(xt_l.sem, 1)

            def kv_low(p):
                kt_h.wait(dve, p, 1)
                low(kt_lo[:], A2[:, 0:P], kt_hi[:]).then_inc(kt_l.sem, 1)
                for b in range(2):
                    for half in range(2):
                        ins = dve.tensor_copy(
                            vwin[half * SEQ:(half + 1) * SEQ, b, WINDOW + half * HD:WINDOW + (half + 1) * HD],
                            A2[b * SEQ:(b + 1) * SEQ, P:P + HD])
                ins.then_inc(v_win.sem, 1)

            def q_low(p):
                qt_h.wait(dve, p, 1)
                for b in range(2):
                    ins = dve.scalar_tensor_tensor(
                        qt_lo[:, :, 2 * b * SEQ:(2 * b + 1) * SEQ],
                        A1[:].rearrange("p (g t) -> p g t", g=GROUPS)[:, :, b * SEQ:(b + 1) * SEQ], HD ** -0.5,
                        f32(qt_hi[:, :, 2 * b * SEQ:(2 * b + 1) * SEQ]), ALU.mult, ALU.subtract)
                ins.then_inc(qt_l.sem, 1)

            def heads(ap):
                return ap.rearrange("p (h k) -> p h k", h=HG)

            def score_max(p, g):
                ps = (A0, A1, A2, A1)[g]
                s_ps.wait(dve, p, g + 1)
                dve.tensor_reduce(smax[:, g, :], heads(ps[:]), ALONG_FREE, ALU.max).then_inc(s_max.sem, 1)
                s_max.wait(dve, p, g + 1)
                if g < 2:
                    pt_ps.wait(dve, p, 0)
                else:
                    pt_ps.wait(dve, p, g - 1)
                dve.tensor_tensor(heads(prob[:, g % 2, :]), heads(ps[:]),
                                  smax[:, g, :, None].broadcast_to([P, HG, SEQ]), ALU.subtract).then_inc(s_sub.sem, 1)

            def prob_sum(p, g):
                s_exp.wait(dve, p, g + 1)
                dve.tensor_reduce(ssum[:, g, :], heads(prob[:, g % 2, :]), ALONG_FREE, ALU.add).then_inc(s_sum.sem, 1)
                s_sum.wait(dve, p, g + 1)
                dve.reciprocal(srec[:, g, :], ssum[:, g, :]).then_inc(s_rec.sem, 1)

            def residual_a(p):
                y_ps.wait(dve, p, 1)
                x_kept.wait(dve, p, 1)
                dve.tensor_tensor(x_keep[:], A1[:], x_keep[:], ALU.add).then_inc(z_done.sem, 1)
                z_done.wait(dve, p, 1)
                statistics(0, p, x_keep[:])

            def finish_a(p):
                zb_done.wait(dve, p, 0)
                xs_h.wait(dve, p, 0)
                normalize(0, p, x1[:], x_keep[:]).then_inc(x1_done.sem, 1)

            def stacks(p, src, o, h, l):
                h.wait(dve, p, 2)
                for b in range(2):
                    rows, other = slice(b * SEQ, (b + 1) * SEQ), slice((1 - b) * SEQ, (2 - b) * SEQ)
                    dve.tensor_tensor(o[other, b, :], src[rows, :], f32(o[rows, b, :]), ALU.subtract)\
                        .then_inc(l.sem, 1)

            def key_max(p, u):
                k_ps.wait(dve, p, u + 1)
                dve.tensor_reduce(kmax[:, u:u + 1], B0[:], ALONG_FREE, ALU.max).then_inc(k_max.sem, 1)
                k_max.wait(dve, p, u + 1)
                dve.tensor_scalar(kneg[:, u:u + 1], kmax[:, u:u + 1], -1.0, None, ALU.mult).then_inc(k_neg.sem, 1)

            def key_turned(p, u):
                kt_ps.wait(dve, p, u + 1)
                if u < 2:
                    t_ps.wait(dve, p, 0)
                else:
                    t_ps.wait(dve, p, u - 1)
                dve.tensor_copy(ekt[:, u % 2, :], B1[:]).then_inc(ekt_done.sem, 1)

            def key_scale(p, b):
                cols = slice(b * KC, (b + 1) * KC)
                k_exp.wait(dve, p, (b + 1) * KC)
                dve.reciprocal(krec[:, cols], ksum[:, cols]).then_inc(k_rec.sem, 1)
                k_rec.wait(dve, p, b + 1)
                dve.tensor_scalar(krec[:, cols], krec[:, cols], XD ** -0.5, None, ALU.mult).then_inc(k_scl.sem, 1)
                k_scl.wait(dve, p, b + 1)
                m_ps.wait(dve, p, b + 1)
                for half in range(2):
                    rows = slice(half * XD, (half + 1) * XD)
                    ins = dve.tensor_tensor(
                        mt[rows, b], B1[rows, :].rearrange("p (k o) -> p k o", k=KC)[:, :, half * SEQ:(half + 1) * SEQ],
                        krec[rows, cols][:, :, None].broadcast_to([XD, KC, SEQ]), ALU.mult)
                ins.then_inc(mt_done.sem, 1)

            def xheads(ap):
                return ap.rearrange("p (h d) -> p h d", h=XH)

            def query_max(p, v):
                q_ps.wait(dve, p, v + 1)
                dve.tensor_reduce(qmax[:, v, :], xheads(B0[:]), ALONG_FREE, ALU.max).then_inc(q_max.sem, 1)
                q_max.wait(dve, p, v + 1)
                if v < 2:
                    eqt_ps.wait(dve, p, 0)
                    o_sq.wait(dve, p, 0)
                    o_var.wait(dve, p, 0)
                else:
                    eqt_ps.wait(dve, p, v - 1)
                dve.tensor_tensor(xheads(eq[:, v % 2, :]), xheads(B0[:]),
                                  qmax[:, v, :, None].broadcast_to([P, XH, XD]), ALU.subtract).then_inc(q_sub.sem, 1)

            def query_sum(p, v):
                q_exp.wait(dve, p, v + 1)
                dve.tensor_reduce(qsum[:, v, :], xheads(eq[:, v % 2, :]), ALONG_FREE, ALU.add).then_inc(q_sum.sem, 1)
                q_sum.wait(dve, p, v + 1)
                dve.reciprocal(qrec[:, v, :], qsum[:, v, :]).then_inc(q_rec.sem, 1)

            def tiles(ap):
                return ap.rearrange("p (t o) -> p t o", o=SEQ)

            def output_center(p):
                o_ps.wait(dve, p, 8)
                x2_done.wait(dve, p, 0)
                dve.tensor_tensor(tiles(o_sb[:]), tiles(B2[:]), bout[:, None, :].broadcast_to([P, UNITS, SEQ]),
                                  ALU.add).then_inc(o_add.sem, 1)
                o_add.wait(dve, p, 1)
                dve.tensor_reduce(omean[:], tiles(o_sb[:]), ALONG_FREE, ALU.add).then_inc(o_sum.sem, 1)
                o_sum.wait(dve, p, 1)
                dve.tensor_scalar(omean[:], omean[:], 1.0 / SEQ, None, ALU.mult).then_inc(o_mean.sem, 1)
                o_mean.wait(dve, p, 1)
                dve.tensor_tensor(tiles(o_sb[:]), tiles(o_sb[:]), omean[:, :, None].broadcast_to([P, UNITS, SEQ]),
                                  ALU.subtract).then_inc(o_cen.sem, 1)

            def output_var(p):
                o_sq.wait(dve, p, 1)
                dve.tensor_reduce(ovar[:], tiles(eq[:, 0, :]), ALONG_FREE, ALU.add).then_inc(o_var.sem, 1)
                o_var.wait(dve, p, 1)
                dve.tensor_scalar(ovar[:], ovar[:], 1.0 / SEQ, EPS, ALU.mult, ALU.add).then_inc(o_eps.sem, 1)

            def residual_b(p):
                ot_ps.wait(dve, p, 1)
                dve.scalar_tensor_tensor(zb_sb[:], A2[:], gcol[:, 0:1], x1[:], ALU.mult, ALU.add)\
                    .then_inc(zb_done.sem, 1)
                zb_done.wait(dve, p, 1)
                statistics(1, p, zb_sb[:])

            def finish_b(p):
                x2t_ps.wait(dve, p, 0)
                xb_done.wait(dve, p, 0)
                normalize(1, p, x2[:], zb_sb[:]).then_inc(x2_done.sem, 1)

            def x2_low(p):
                x2t_h.wait(dve, p, 1)
                low(x2t_lo[:].rearrange("p k n -> p (k n)"), C0[:], x2t_hi[:].rearrange("p k n -> p (k n)"))\
                    .then_inc(x2t_l.sem, 1)

            def route(p):
                lg_ps.wait(dve, p, 1)
                dve.memset(wait_pad[:], 0.0)
                dve.max(top8[:], C1[:, 0:NE]).then_inc(lg_top.sem, 1)
                lg_top.wait(dve, p, 1)
                ro_done.wait(dve, p, 0)
                dve.tensor_tensor(rsum[:], top8[:, 0:1], top8[:, 1:2], ALU.add).then_inc(lg_sum.sem, 1)

            def ffn_sum(p):
                ro_done.wait(dve, p, 1)
                sh_ps.wait(dve, p, 1)
                dve.tensor_tensor(f_sb, C0[:], routed, ALU.add).then_inc(f_add.sem, 1)
                f_add.wait(dve, p, 1)
                statistics(2, p, f_sb)

            def ffn_norm(p):
                normalize(2, p, f_sb, f_sb).then_inc(f_nrm.sem, 1)

            def residual_c(p):
                f_gam.wait(dve, p, 1)
                xb_done.wait(dve, p, 1)
                dve.tensor_tensor(f_sb, f_sb, x2_beta, ALU.add).then_inc(f_res.sem, 1)
                f_res.wait(dve, p, 1)
                statistics(3, p, f_sb)

            def finish_c(p):
                y_out.wait(dve, p, 0)
                normalize(3, p, y_sb, f_sb).then_inc(y_done.sem, 1)

            def work(due):
                for p, b in due("combined"):
                    key_scale(p, b)
                for p, u in due("keys_turn"):
                    key_turned(p, u)
                for p, u in due("keys"):
                    key_max(p, u)
                for p, v in due("query_sum"):
                    query_sum(p, v)
                for p, v in due("queries"):
                    query_max(p, v)
                for p, g in due("prob_sum"):
                    prob_sum(p, g)
                for p, _ in due("residual_a"):
                    residual_a(p)
                for p, _ in due("residual_b"):
                    residual_b(p)
                for p, _ in due("finish_a"):
                    finish_a(p)
                    stacks(p, x1, xs, xs_h, xs_l)
                for p, _ in due("x_turn"):
                    x_low(p)
                for p, _ in due("kv"):
                    kv_low(p)
                for p, half in due("q"):
                    if half == 1:
                        q_low(p)
                for p, g in due("scores"):
                    score_max(p, g)
                for p, _ in due("c_split"):
                    stacks(p, c_in, cs, cs_h, cs_l)
                for p, _ in due("o_center"):
                    output_center(p)
                for p, _ in due("o_var"):
                    output_var(p)
                for p, _ in due("finish_b"):
                    finish_b(p)
                for p, _ in due("x2_turn"):
                    x2_low(p)
                for p, _ in due("logits"):
                    route(p)
                for p, _ in due("ffn_sum"):
                    ffn_sum(p)
                for p, _ in due("ffn_norm"):
                    ffn_norm(p)
                for p, _ in due("residual_c"):
                    residual_c(p)
                for p, _ in due("finish_c"):
                    finish_c(p)

            drive(dve, setup_a, setup_b, setup_c, work)

        @block.scalar
        def _(act):
            def copy(o, i, scale=1.0):
                return act.activation(o, i, ACT.Copy, scale=scale)

            def setup_a():
                act.wait_ge(ld_wkv, 16)
                wkv_v = cw[:, 0, 0:KC * 2 * HD].rearrange("p (k n) -> p k n", k=KC)
                for k in range(KC):
                    ins = copy(wk_hi[:, k, :].rearrange("p (h d) -> p h d", h=HG),
                               wkv_v[:, k, None, 0:HD].broadcast_to([P, HG, HD]))
                ins.then_inc(hi_a, 1)
                copy(wv_hi[:], wkv_v[:, :, HD:2 * HD]).then_inc(hi_a, 1)
                act.wait_ge(ld_wq, 16)
                copy(wq_hi[:], cw[:, 1:5, :]).then_inc(hi_a, 1)
                act.wait_ge(ld_tab, 16)
                copy(ident_r[:], ident).then_inc(tab_r, 1)
                copy(causal_r[:], tab[:, T_CAUSAL:T_CAUSAL + SEQ]).then_inc(tab_r, 1)
                act.wait_ge(ld_bias, 16)
                copy(left_r[:].rearrange("p g t -> p (g t)"), ekt[:, 0, :]).then_inc(tab_r, 1)
                copy(right_r[:], ekt[:, 1, :]).then_inc(tab_r, 1)

            def setup_b():
                act.wait_ge(tr_b, 1)
                copy(xwq_hi[:], B0[:]).then_inc(hi_b, 1)
                act.wait_ge(tr_b, 2)
                copy(xwk_hi[:], B1[:]).then_inc(hi_b, 1)
                act.wait_ge(tr_b, 3)
                copy(eqt[0:XD, 0, :], B2[0:XD, :]).then_inc(hi_b, 1)
                act.wait_ge(tr_b, 4)
                copy(vout[:], B0[0:XD, :]).then_inc(g_b, 1)

            def setup_c():
                act.wait_ge(ld_up, 16)
                copy(up_hi[:].rearrange("p k n -> p (k n)"), cw[:].rearrange("p s n -> p (s n)")).then_inc(hi_c, 1)
                act.wait_ge(ld_gate, 16)
                copy(gate_hi[:], gate_sb[:]).then_inc(hi_c, 1)
                for n in range(4):
                    act.wait_ge(fold_ps, n + 1)
                    copy(cw[:, (5, 6, 0, 1)[n], :], (C0, C1)[n % 2][:]).then_inc(fold_sb, 1)
                for k in range(KC):
                    act.wait_ge(wr_ps, k + 1)
                    copy(wr_hi[:, k, :], (C0, C1)[k % 2][:]).then_inc(wr_h, 1)

            def load_x(p):
                if first(p):
                    return
                xt_ps.wait(act, p, 0)
                x_kept.wait(act, p, 0)
                act.dma_start(x_in[:], x[p]).then_inc(x_load.sem, 16)

            def load_c(p):
                ct_ps.wait(act, p, 0)
                cs_h.wait(act, p, 0)
                cs_l.wait(act, p, 0)
                act.dma_start(c_in[:], ctx[p]).then_inc(c_load.sem, 16)

            def store_y(p):
                y_done.wait(act, p, 1)
                act.dma_start(out[p], y_sb).then_inc(y_out.sem, 16)

            def keep(p):
                x_load.wait(act, p, 16)
                x1_done.wait(act, p, 0)
                copy(x_keep[:], x_in[:]).then_inc(x_kept.sem, 1)

            def x_high(p):
                xt_ps.wait(act, p, 1)
                copy(xt_hi[:].rearrange("p k n -> p (k n)"), A0[:]).then_inc(xt_h.sem, 1)

            def k_high(p):
                kv_ps.wait(act, p, 1)
                copy(kt_hi[:], A2[:, 0:P]).then_inc(kt_h.sem, 1)

            def q_high(p):
                qt_ps.wait(act, p, 1)
                for b in range(2):
                    ins = copy(qt_hi[:, :, 2 * b * SEQ:(2 * b + 1) * SEQ],
                               A1[:].rearrange("p (g t) -> p g t", g=GROUPS)[:, :, b * SEQ:(b + 1) * SEQ], HD ** -0.5)
                ins.then_inc(qt_h.sem, 1)

            def prob_exp(p, g):
                s_sub.wait(act, p, g + 1)
                act.activation(prob[:, g % 2, :], prob[:, g % 2, :], ACT.Exp).then_inc(s_exp.sem, 1)

            def prob_turned(p, g):
                pt_ps.wait(act, p, g + 1)
                if g < 2:
                    ao_ps.wait(act, p, 0)
                else:
                    ao_ps.wait(act, p, 1)
                copy(pt_sb[:, g % 2, :], (A0, A0, A1, A0)[g][:]).then_inc(pt_done.sem, 1)

            def values_out(p):
                ao_ps.wait(act, p, 2)
                copy(ao_sb[:].rearrange("p g t -> p (g t)"), A2[:]).then_inc(ao_done.sem, 1)

            def stacks(p, src, o, h):
                for b in range(2):
                    rows = slice(b * SEQ, (b + 1) * SEQ)
                    copy(o[rows, b, :], src[rows, :]).then_inc(h.sem, 1)

            def c_high(p):
                c_load.wait(act, p, 16)
                k_ps.wait(act, p, 0)
                stacks(p, c_in, cs, cs_h)

            def c_turned(p):
                ct_ps.wait(act, p, 1)
                t_ps.wait(act, p, 0)
                copy(ct_sb[:].rearrange("p k n -> p (k n)"), A2[:]).then_inc(ct_done.sem, 1)

            def x_stack(p):
                x1_done.wait(act, p, 1)
                q_ps.wait(act, p, 0)
                stacks(p, x1, xs, xs_h)

            def key_exp(p, u):
                k_neg.wait(act, p, u + 1)
                if u < 2:
                    kt_ps.wait(act, p, 0)
                    mt_done.wait(act, p, 0)
                else:
                    kt_ps.wait(act, p, u - 1)
                act.activation(ek[:, u % 2, :], B0[:], ACT.Exp, bias=kneg[:, u:u + 1],
                               accum_out=ksum[:, u:u + 1]).then_inc(k_exp.sem, 1)

            def context_out(p, b):
                t_ps.wait(act, p, (b + 1) * KC)
                m_ps.wait(act, p, b)
                copy(tctx[:], B2[0:SEQ, :]).then_inc(t_done.sem, 1)

            def query_exp(p, v):
                q_sub.wait(act, p, v + 1)
                act.activation(eq[:, v % 2, :], eq[:, v % 2, :], ACT.Exp).then_inc(q_exp.sem, 1)

            def query_turned(p, v):
                eqt_ps.wait(act, p, v + 1)
                if v < 2:
                    o_ps.wait(act, p, 0)
                else:
                    o_ps.wait(act, p, v - 1)
                copy(eqt[:, v % 2, :], B1[:]).then_inc(eqt_done.sem, 1)

            def output_square(p):
                o_cen.wait(act, p, 1)
                eqt_ps.wait(act, p, 8)
                act.activation(eq[:, 0, :], o_sb[:], ACT.Square).then_inc(o_sq.sem, 1)

            def x2_high(p):
                x2t_ps.wait(act, p, 1)
                copy(x2t_hi[:].rearrange("p k n -> p (k n)"), C0[:]).then_inc(x2t_h.sem, 1)

            def relu(p, j):
                h_ps.wait(act, p, j + 1)
                act.activation(h_sb[:, j, :], (C0, C1)[j][:], ACT.Relu).then_inc(h_relu.sem, 1)

            def hidden_turned(p, j):
                ht_ps.wait(act, p, j + 1)
                copy(ht_sb[:, j, :], (C0, C1)[j][:]).then_inc(ht_done.sem, 1)

            def routed_out(p):
                ro_ps.wait(act, p, 1)
                lg_sum.wait(act, p, 1)
                f_add.wait(act, p, 0)
                copy_scaled = act.activation(routed, C1[:], ACT.Copy, scale=rsum[:, 0:1])
                copy_scaled.then_inc(ro_done.sem, 1)

            def work(due):
                for p, _ in due("load_x"):
                    load_x(p)
                for p, _ in due("load_c"):
                    load_c(p)
                for p, _ in due("store"):
                    store_y(p)
                for p, v in due("queries_turn"):
                    query_turned(p, v)
                for p, u in due("keys"):
                    key_exp(p, u)
                for p, v in due("queries"):
                    query_exp(p, v)
                for p, u in due("context"):
                    if u % KC == KC - 1:
                        context_out(p, u // KC)
                for p, _ in due("finish_a"):
                    x_stack(p)
                for p, _ in due("x_turn"):
                    x_high(p)
                    keep(p)
                for p, _ in due("kv"):
                    k_high(p)
                for p, half in due("q"):
                    if half == 1:
                        q_high(p)
                for p, g in due("prob_turn"):
                    prob_turned(p, g)
                for p, g in due("scores"):
                    prob_exp(p, g)
                for p, half in due("values"):
                    if half == 1:
                        values_out(p)
                for p, _ in due("c_split"):
                    c_high(p)
                for p, _ in due("c_turn"):
                    c_turned(p)
                for p, _ in due("o_center"):
                    output_square(p)
                for p, _ in due("x2_turn"):
                    x2_high(p)
                for p, j in due("hidden"):
                    relu(p, j)
                for p, j in due("hidden_turn"):
                    hidden_turned(p, j)
                for p, _ in due("ffn_sum"):
                    routed_out(p)

            drive(act, setup_a, setup_b, setup_c, work)

        @block.gpsimd
        def _(pool):
            def root(n, p):
                ln_eps[n].wait(pool, p, 1)
                pool.tensor_tensor(rstd[n][:], var_eps[n][:], minus_half[:, 0:1], ALU.pow).then_inc(ln_rstd[n].sem, 1)

            def setup_a():
                pool.memset(minus_half[:], -0.5).then_inc(halves, 1)
                pool.wait_ge(halves, 1)
                pool.wait_ge(ld_tab, 16)

            def setup_b():
                pass

            def setup_c():
                pool.wait_ge(ld_gb, 32)
                pool.wait_ge(wr_l, 4)
                pool.wait_ge(lo_c, 2)

            def keys_by_head(p):
                for part, s, kt, kd in ((0, kt_h, kt_hi, kd_hi), (1, kt_l, kt_lo, kd_lo)):
                    s.wait(pool, p, 1)
                    for b in range(2):
                        pool.tensor_tensor(kd[:, b], f32(kt[:, None, b * SEQ:(b + 1) * SEQ]).broadcast_to([P, HG, SEQ]),
                                           own[:, :, None].broadcast_to([P, HG, SEQ]), ALU.mult)\
                            .then_inc(kd_done.sem, 1)

            def prob_norm(p, g):
                s_rec.wait(pool, p, g + 1)
                v = prob[:, g % 2, :].rearrange("p (h k) -> p h k", h=HG)
                pool.tensor_tensor(v, v, srec[:, g, :, None].broadcast_to([P, HG, SEQ]), ALU.mult)\
                    .then_inc(s_nrm.sem, 1)

            def query_norm(p, v):
                q_rec.wait(pool, p, v + 1)
                w = eq[:, v % 2, :].rearrange("p (h d) -> p h d", h=XH)
                pool.tensor_tensor(w, w, qrec[:, v, :, None].broadcast_to([P, XH, XD]), ALU.mult)\
                    .then_inc(q_nrm.sem, 1)

            def output_norm(p):
                o_eps.wait(pool, p, 1)
                pool.tensor_tensor(orstd[:], ovar[:], minus_half[:], ALU.pow).then_inc(o_rstd.sem, 1)
                o_rstd.wait(pool, p, 1)
                w = o_sb[:].rearrange("p (t o) -> p t o", o=SEQ)
                pool.tensor_tensor(w, w, orstd[:, :, None].broadcast_to([P, UNITS, SEQ]), ALU.mult)\
                    .then_inc(o_nrm.sem, 1)

            def add_beta(p):
                x2_done.wait(pool, p, 1)
                f_res.wait(pool, p, 0)
                pool.tensor_tensor(x2_beta, x2[:], beta[:], ALU.add).then_inc(xb_done.sem, 1)

            def square(p, j):
                h_relu.wait(pool, p, j + 1)
                pool.tensor_tensor(h_sb[:, j, :], h_sb[:, j, :], h_sb[:, j, :], ALU.mult).then_inc(h_sq.sem, 1)

            def times_gamma(p):
                f_nrm.wait(pool, p, 1)
                pool.tensor_tensor(f_sb, f_sb, gamma[:], ALU.mult).then_inc(f_gam.sem, 1)

            def work(due):
                for p, _ in due("residual_a"):
                    root(0, p)
                for p, _ in due("residual_b"):
                    root(1, p)
                for p, v in due("query_sum"):
                    query_norm(p, v)
                for p, g in due("prob_sum"):
                    prob_norm(p, g)
                for p, _ in due("kv"):
                    keys_by_head(p)
                for p, _ in due("o_var"):
                    output_norm(p)
                for p, _ in due("add_beta"):
                    add_beta(p)
                for p, j in due("hidden"):
                    square(p, j)
                for p, _ in due("ffn_sum"):
                    root(2, p)
                for p, _ in due("ffn_norm"):
                    times_gamma(p)
                for p, _ in due("residual_c"):
                    root(3, p)

            drive(pool, setup_a, setup_b, setup_c, work)


_INS = ["x", "ctx_4096", "L0_attn_Wq", "L0_attn_Wkv", "L0_attn_Wo", "L0_xattn_Wq", "L0_xattn_Wkv", "L0_xattn_Wout",
        "L0_xattn_b_out", "L0_xattn_g", "L0_ffn_gate_w", "L0_ffn_up_w", "L0_ffn_down_w", "L0_ffn_fc1_w",
        "L0_ffn_fc2_w", "L0_ffn_expert_w", "L0_ffn_ln_gamma", "L0_ffn_ln_beta"]


def kernel(**inputs):
    import numpy as _np
    import concourse.bacc as _bacc
    from concourse.bass_utils import run_bass_kernel_spmd as _run

    nc = _bacc.Bacc("TRN2", target_bir_lowering=False, num_devices=1)
    arrays, args = {}, []
    for name in _INS:
        v = _np.ascontiguousarray(inputs[name])
        if name in ("x", "ctx_4096"):
            v = v.reshape(PAIRS, P, DM)
        arrays[f"in_{name}"] = v
        args.append(nc.dram_tensor(f"in_{name}", v.shape, F32, kind="ExternalInput").ap())
    arrays["tables"], arrays["bias_rows"] = shape_tables()
    args.append(nc.dram_tensor("tables", (P, T_ALL), F32, kind="ExternalInput").ap())
    args.append(nc.dram_tensor("bias_rows", (P, 2, DM), F32, kind="ExternalInput").ap())
    args.append(nc.dram_tensor("out", (PAIRS, P, DM), F32, kind="ExternalOutput").ap())
    decoder_kernel(nc, *args)
    r = _run(nc, [arrays], core_ids=[0])
    return r.results[0]["out"].reshape(BATCH, SEQ, DM)
```

```python
from contextlib import ExitStack

import numpy as np

import concourse.bass as bass
from concourse import mybir

F32 = mybir.dt.float32
F32R = mybir.dt.float32r
ALU = mybir.AluOpType
ACT = mybir.ActivationFunctionType
ALONG_FREE = mybir.AxisListType.X

P = 128
BATCH, SEQ, DM = 16, 64, 512
PAIRS = BATCH * SEQ // P
KC = DM // P
HEADS, HD = 32, 16
GROUPS = 4
HG = HEADS // GROUPS
QUADS, HQ = HEADS // 4, 4
XH, XD = 8, 64
INT, LAT, NE = 1024, 256, 8
IC, LC = INT // P, LAT // P
EPS = 1e-5
MASKED = -1e30
ROUNDS, DEPTH = 64, 4
UNITS = 8


WHEN = {
    "pe": {
        "weights_b": [23, 24, 24, 24], "fold": [101, 101, 105, 107, 109, 111, 114, 116], "x_turn": [6], "qkv": [13],
        "qk_turn": [15], "scores": [27, 31, 33, 37], "prob_turn": [33, 37, 41, 45], "values": [41, 50],
        "project": [54, 57], "c_turn": [22], "keys": [41, 45, 49, 53, 57, 62, 65, 69],
        "keys_turn": [48, 49, 53, 57, 62, 65, 69, 73], "context": [52, 61, 68, 75], "combine": [69, 86],
        "queries": [73, 77, 79, 85, 89, 93, 97, 101], "queries_turn": [79, 85, 89, 93, 97, 101, 105, 109],
        "attend": [83, 87, 94, 100, 100, 104, 108, 112], "o_var": [117], "o_spread": [128], "x2_turn": [141],
        "logits": [143], "hidden": [151, 155], "hidden_turn": [163, 171], "shared": [176, 179, 191, 195],
        "routing": [193],
    },
    "dve": {
        "split_wq": [9, 9, 10, 11], "weights_b": [23, 24, 24, 24], "split_up": [45, 49, 51, 54],
        "fold": [104, 104, 107, 108, 110, 113, 116, 118], "x_turn": [10], "qkv": [13], "qk_turn": [18],
        "scores": [27, 31, 33, 37], "prob_sum": [31, 33, 37, 41], "residual_a": [61], "finish_a": [67],
        "c_split": [17], "c_turn": [23], "keys": [41, 44, 49, 53, 57, 62, 65, 69],
        "keys_turn": [48, 53, 53, 57, 62, 65, 69, 73], "combined": [72, 86],
        "queries": [73, 77, 79, 85, 89, 93, 97, 101], "query_sum": [76, 79, 83, 89, 93, 97, 99, 105], "o_var": [117],
        "residual_b": [126], "finish_b": [137], "x2_turn": [142], "logits": [145], "ffn_sum": [204],
        "ffn_norm": [211], "residual_c": [214], "finish_c": [217], "query_sub": [73, 77, 79, 85, 89, 93, 97, 101],
        "query_rec": [76, 79, 83, 89, 93, 97, 99, 105], "score_sub": [27, 31, 33, 37], "prob_rec": [31, 33, 37, 41],
        "residual_b_add": [126], "statistics_0": [61], "statistics_1": [126], "statistics_2": [204],
        "statistics_3": [215], "mean_var_0": [62], "mean_var_1": [131], "mean_var_2": [205], "mean_var_3": [215],
    },
    "act": {
        "load_x": [1], "load_c": [7], "split_wq": [9, 10, 10, 10], "weights_b": [23, 24, 24, 24],
        "split_up": [45, 49, 50, 50], "fold": [101, 101, 105, 107, 109, 111, 114, 116], "x_turn": [7], "qkv": [13],
        "qk_turn": [15], "scores": [27, 32, 34, 37], "prob_turn": [33, 37, 43, 47], "values": [41, 50],
        "finish_a": [65], "c_split": [14], "c_turn": [21], "keys": [41, 45, 49, 53, 57, 62, 65, 69],
        "keys_turn": [45, 49, 53, 57, 62, 65, 69, 73], "context": [51, 59, 67, 75],
        "queries": [73, 77, 79, 85, 89, 93, 97, 101], "queries_turn": [79, 85, 89, 93, 95, 101, 106, 109],
        "o_bias": [111], "x2_turn": [141], "hidden": [151, 154], "hidden_turn": [162, 172], "ffn_sum": [201],
        "store": [251],
    },
    "pool": {
        "qk_turn": [17], "prob_sum": [32, 33, 38, 41], "residual_a": [54],
        "query_sum": [77, 79, 83, 90, 93, 97, 99, 105], "o_var": [116], "residual_b": [134], "add_beta": [168],
        "hidden": [148, 158], "ffn_sum": [207], "ffn_norm": [211], "residual_c": [214],
    },
}


def shape_tables():
    start = 2.0 ** (-2.0 ** (-(np.log2(HEADS) - 3)))
    slopes = np.array([start ** (i + 1) for i in range(HEADS)], dtype=np.float32)
    pos = np.arange(SEQ)
    causal = np.where(pos[None, :] <= pos[:, None], 0.0, MASKED).astype(np.float32)
    own = np.zeros((P, HQ), np.float32)
    for row in range(P):
        own[row, row // HD % HQ] = 1.0
    q = np.tile(pos, 2).astype(np.float32)
    left = np.zeros((P, GROUPS, P), np.float32)
    right = np.zeros((P, HG, SEQ), np.float32)
    for h in range(HG):
        for g in range(GROUPS):
            for r, v in ((0, slopes[g * HG + h] * np.ones(P, np.float32)), (2, slopes[g * HG + h] * q)):
                v = v.astype(np.float32)
                hi = (v.view(np.uint32) & np.uint32(0xFFFFF000)).view(np.float32)
                left[r * HG + h, g] = hi
                left[(r + 1) * HG + h, g] = v - hi
        right[h, h] = right[HG + h, h] = pos
        right[2 * HG + h, h] = right[3 * HG + h, h] = -1.0
    left[4 * HG:4 * HG + SEQ] = (pos[:, None] == q[None, :])[:, None, :]
    right[4 * HG:4 * HG + SEQ] = causal[:, None, :]
    batch_mean = np.zeros((P, 2), np.float32)
    for b in range(2):
        batch_mean[b * SEQ:(b + 1) * SEQ, b] = 1.0 / SEQ
    return (np.concatenate([np.eye(P, dtype=np.float32), own, batch_mean], 1),
            np.stack([left.reshape(P, -1), right.reshape(P, -1)], 1))


T_IDENT, T_OWN, T_MEAN, T_ALL = 0, P, P + HQ, P + HQ + 2


class Signal:

    def __init__(self, sem, per):
        self.sem, self.per = sem, per

    def wait(self, eng, pair, nth):
        value = pair * self.per + nth
        if not isinstance(value, int) or value > 0:
            eng.wait_ge(self.sem, value)


def decoder_kernel(nc, x, ctx, wq, wkv, wo, xwq, xwkv, xwout, xb_out, xg, gate_w, up_w, down_w,
                   fc1_w, fc2_w, expert_w, ln_gamma, ln_beta, tables, bias_rows, out):
    stack = ExitStack()
    with stack:
        def sb(name, shape, dt=F32):
            return stack.enter_context(nc.sbuf_tensor(name, shape, dt))

        def sem(name):
            return stack.enter_context(nc.semaphore(name))

        def sig(name, per=1):
            return Signal(sem(name), per)

        tab = sb("tab", [P, T_ALL])
        ident = tab[:, T_IDENT:T_IDENT + P]
        own = tab[:, T_OWN:T_OWN + HQ]
        batch_mean = tab[:, T_MEAN:T_MEAN + 2]
        left_r = sb("left_r", [P, GROUPS, P], F32R)
        right_r = sb("right_r", [P, HG * SEQ], F32R)
        wq_hi, wq_lo = sb("wq_hi", [P, KC, DM], F32R), sb("wq_lo", [P, KC, DM], F32R)
        wkv_hi, wkv_lo = sb("wkv_hi", [P, KC, 2 * HD], F32R), sb("wkv_lo", [P, KC, 2 * HD], F32R)
        wo_sb = sb("wo_sb", [P, KC, DM])
        xwq_hi, xwq_lo = sb("xwq_hi", [P, DM], F32R), sb("xwq_lo", [P, DM], F32R)
        xwk_hi, xwk_lo = sb("xwk_hi", [P, DM], F32R), sb("xwk_lo", [P, DM], F32R)
        vout, vmean = sb("vout", [P, XH * SEQ]), sb("vmean", [XD, XH])
        bout, bmean = sb("bout", [P, SEQ]), sb("bmean", [P, 1])
        bcol, gcol = sb("bcol", [P, 1]), sb("gcol", [P, 1])
        gate_sb = sb("gate_sb", [P, KC, NE])
        gate_hi, gate_lo = sb("gate_hi", [P, KC, NE], F32R), sb("gate_lo", [P, KC, NE], F32R)
        up_hi, up_lo = sb("up_hi", [P, KC, INT], F32R), sb("up_lo", [P, KC, INT], F32R)
        down_sb = sb("down_sb", [P, IC, DM])
        wr_hi, wr_lo = sb("wr_hi", [P, KC, DM], F32R), sb("wr_lo", [P, KC, DM], F32R)
        gamma, beta = sb("gamma", [P, DM]), sb("beta", [P, DM])
        minus_half = sb("minus_half", [P, UNITS])

        x_in, x_keep, x1 = sb("x_in", [P, DM]), sb("x_keep", [P, DM]), sb("x1", [P, DM])
        xt_hi, xt_lo = sb("xt_hi", [P, KC, P], F32R), sb("xt_lo", [P, KC, P], F32R)
        qt = sb("qt", [P, QUADS, 3 * SEQ], F32R)
        k_sb = sb("k_sb", [P, P])
        kt_hi, kt_lo = sb("kt_hi", [P, P], F32R), sb("kt_lo", [P, P], F32R)
        kd_hi, kd_lo = sb("kd_hi", [P, 2, HQ, SEQ], F32R), sb("kd_lo", [P, 2, HQ, SEQ], F32R)
        vpair = sb("vpair", [P, 2, 2 * HD])
        prob = sb("prob", [P, 2, HG * SEQ])
        pt_sb = sb("pt_sb", [P, 2, DM])
        q_sb = pt_sb[:].rearrange("p g n -> p (g n)").rearrange("p (u s n) -> p u s n", u=QUADS, s=2)
        ao_sb = sb("ao_sb", [P, GROUPS, P])
        smax, ssum, srec = sb("smax", [P, GROUPS, HG]), sb("ssum", [P, GROUPS, HG]), sb("srec", [P, GROUPS, HG])
        c_in = sb("c_in", [P, DM])
        xs, cs = sb("xs", [P, 2, DM], F32R), sb("cs", [P, 2, DM], F32R)
        ct = sb("ct", [P, 2 * KC, 2, SEQ], F32R)
        ek = sb("ek", [P, 2, DM])
        ekt_hi, ekt_lo = sb("ekt_hi", [P, KC, 2, P], F32R), sb("ekt_lo", [P, KC, 2, P], F32R)
        tctx = sb("tctx", [P, DM])
        mt = sb("mt", [P, 2, KC, SEQ])
        eq, eqt = sb("eq", [P, 2, DM]), sb("eqt", [P, 2, DM])
        kneg, ksum, krec = sb("kneg", [P, UNITS]), sb("ksum", [P, UNITS]), sb("krec", [P, UNITS])
        qmax, qsum, qrec = sb("qmax", [P, UNITS, XH]), sb("qsum", [P, UNITS, XH]), sb("qrec", [P, UNITS, XH])
        o_sb, x2 = sb("o_sb", [P, DM]), sb("x2", [P, DM])
        zb_sb = o_sb
        ovar, orstd = sb("ovar", [P, UNITS]), sb("orstd", [P, UNITS])
        x2t_hi, x2t_lo = sb("x2t_hi", [P, KC, P], F32R), sb("x2t_lo", [P, KC, P], F32R)
        cw = sb("cw", [P, 8, DM])
        h_sb, ht_sb = cw[:, 0:2, :], cw[:, 2:4, :]
        routed, f_sb, x2_beta, y_sb = cw[:, 4, :], cw[:, 5, :], cw[:, 6, :], cw[:, 7, :]
        top8, rsum = sb("top8", [P, NE]), sb("rsum", [P, 1])
        stats = [sb(f"stats{n}", [P, 6]) for n in range(4)]
        meanvar = [sb(f"meanvar{n}", [P, 2]) for n in range(4)]
        var_eps = [sb(f"var_eps{n}", [P, 1]) for n in range(4)]
        rstd = [sb(f"rstd{n}", [P, 1]) for n in range(4)]

        wait_pad = sb("wait_pad", [P, 1])

        bank = [stack.enter_context(nc.psum_tensor(f"bank{n}", [P, DM], F32)) for n in range(8)]
        A0, A1, A2, B0, B1, B2, C0, C1 = bank

        ld_tab, ld_bias, ld_wq, ld_wkv, ld_wo = sem("ld_tab"), sem("ld_bias"), sem("ld_wq"), sem("ld_wkv"), sem("ld_wo")
        ld_xwq, ld_xwk, ld_xwv, ld_xwo, ld_xb = (sem("ld_xwq"), sem("ld_xwk"), sem("ld_xwv"), sem("ld_xwo"),
                                                 sem("ld_xb"))
        ld_up, ld_down, ld_gate, ld_fc, ld_gb = sem("ld_up"), sem("ld_down"), sem("ld_gate"), sem("ld_fc"), sem("ld_gb")
        tab_r, hi_a, lo_a, zeroed = sem("tab_r"), sem("hi_a"), sem("lo_a"), sem("zeroed")
        tr_b, hi_b, lo_b, g_b, g_c = sem("tr_b"), sem("hi_b"), sem("lo_b"), sem("g_b"), sem("g_c")
        hi_c, lo_c, fold_ps, fold_sb, wr_ps, wr_h, wr_l = (sem("hi_c"), sem("lo_c"), sem("fold_ps"), sem("fold_sb"),
                                                           sem("wr_ps"), sem("wr_h"), sem("wr_l"))
        halves = sem("halves")

        x_load, x_kept = sig("x_load", 16), sig("x_kept")
        xt_ps, xt_h, xt_l = sig("xt_ps"), sig("xt_h"), sig("xt_l")
        q_ps_a, q_h, q_l, qt_ps, qt_done = sig("q_ps_a"), sig("q_h"), sig("q_l"), sig("qt_ps", 2), sig("qt_done", 2)
        kv_ps, k_rep, v_done = sig("kv_ps"), sig("k_rep"), sig("v_done")
        ktr_ps, kt_h, kt_l = sig("ktr_ps"), sig("kt_h"), sig("kt_l")
        kd_done = sig("kd_done", 4)
        s_ps, s_max, s_sub, s_exp = sig("s_ps", 4), sig("s_max", 4), sig("s_sub", 4), sig("s_exp", 4)
        s_sum, s_rec, s_nrm = sig("s_sum", 4), sig("s_rec", 4), sig("s_nrm", 4)
        pt_ps, pt_done, ao_ps, ao_done = sig("pt_ps", 4), sig("pt_done", 4), sig("ao_ps", 2), sig("ao_done")
        y_ps, z_done = sig("y_ps"), sig("z_done")
        ln_stat = [sig(f"ln_stat{n}") for n in range(4)]
        ln_mean = [sig(f"ln_mean{n}") for n in range(4)]
        ln_eps = [sig(f"ln_eps{n}") for n in range(4)]
        ln_rstd = [sig(f"ln_rstd{n}") for n in range(4)]
        x1_done = sig("x1_done")
        c_load, ct_ps, ct_h, ct_done = sig("c_load", 16), sig("ct_ps"), sig("ct_h"), sig("ct_done")
        cs_h, cs_l, xs_h, xs_l = sig("cs_h", 2), sig("cs_l", 2), sig("xs_h", 2), sig("xs_l", 2)
        k_ps, k_neg, k_exp = sig("k_ps", 8), sig("k_neg", 8), sig("k_exp", 8)
        kt_ps, ekt_h, ekt_done, t_ps, t_done, m_ps = (sig("kt_ps", 8), sig("ekt_h", 8), sig("ekt_done", 8),
                                                      sig("t_ps", 4), sig("t_done", 2), sig("m_ps", 2))
        k_rec, k_scl, mt_done = sig("k_rec", 2), sig("k_scl", 2), sig("mt_done", 2)
        q_ps, q_max, q_sub, q_exp = sig("q_ps", 8), sig("q_max", 8), sig("q_sub", 8), sig("q_exp", 8)
        q_sum, q_rec, q_nrm = sig("q_sum", 8), sig("q_rec", 8), sig("q_nrm", 8)
        eqt_ps, eqt_done, o_ps = sig("eqt_ps", 8), sig("eqt_done", 8), sig("o_ps", 8)
        o_add, o_sq, ov_ps, o_eps, o_rstd, or_ps, o_nrm = (sig("o_add"), sig("o_sq"), sig("ov_ps"), sig("o_eps"),
                                                           sig("o_rstd"), sig("or_ps"), sig("o_nrm"))
        zb_done, x2_done = sig("zb_done"), sig("x2_done")
        x2t_ps, x2t_h, x2t_l, xb_done = sig("x2t_ps"), sig("x2t_h"), sig("x2t_l"), sig("xb_done")
        lg_ps, lg_top, lg_sum = sig("lg_ps"), sig("lg_top"), sig("lg_sum")
        h_ps, h_relu, h_sq, ht_ps, ht_done = sig("h_ps", 2), sig("h_relu", 2), sig("h_sq", 2), sig("ht_ps", 2), sig("ht_done", 2)
        sh_ps, ro_ps, ro_done, f_add, f_nrm, f_gam, f_res, y_done, y_out = (
            sig("sh_ps"), sig("ro_ps"), sig("ro_done"), sig("f_add"), sig("f_nrm"), sig("f_gam"), sig("f_res"),
            sig("y_done"), sig("y_out", 16))

        block = stack.enter_context(nc.Block())

        def due(when, pairs, rnd):
            def of(name):
                return [(pairs[t // ROUNDS], part) for part, t in enumerate(when[name])
                        if t % ROUNDS == rnd and pairs[t // ROUNDS] is not None]
            return of

        def once(due, name):
            return [part for p, part in due(name) if first(p)]

        def drive(eng, when, setup, work):
            def step(i):
                inside = [i - k if not isinstance(i, int) or 0 <= i - k < PAIRS else None for k in range(DEPTH)]
                for rnd in range(ROUNDS):
                    work(due(when, inside, rnd))

            setup()
            for i in range(DEPTH - 1):
                step(i)
            with eng.Fori(DEPTH - 1, PAIRS - 1, 2) as i:
                step(i)
                step(i + 1)
            for i in range(PAIRS - 1, PAIRS + DEPTH - 1):
                step(i)

        def first(p):
            return isinstance(p, int) and p == 0

        def f32(ap):
            return ap.bitcast(F32)

        @block.sync
        def _(sp):
            sp.dma_start(x_in[:], x[0]).then_inc(x_load.sem, 16)
            sp.dma_start(tab[:], tables).then_inc(ld_tab, 16)
            sp.dma_start(cw[:, 0, 0:KC * 2 * HD].rearrange("p (k n) -> p k n", k=KC),
                         wkv.rearrange("(k p) n -> p k n", p=P)).then_inc(ld_wkv, 16)
            sp.dma_start(cw[:, 1:5, :], wq.rearrange("(k p) n -> p k n", p=P)).then_inc(ld_wq, 16)
            sp.dma_start(eqt[:], bias_rows).then_inc(ld_bias, 16)
            sp.dma_start(wo_sb[:], wo.rearrange("(k p) n -> p k n", p=P)).then_inc(ld_wo, 16)
            for slot, s, rows in ((ek, ld_xwq, xwq), (eq, ld_xwk, xwkv[0:DM, :])):
                for twice in range(2):
                    sp.dma_start(slot[:, 0, :].rearrange("p (k t c) -> p k t c", k=KC, t=2)[:, :, twice, :],
                                 rows.rearrange("(k p) c -> p k c", p=P)).then_inc(s, 16)
            sp.dma_start(ek[0:XD, 1, :].rearrange("e (h c) -> e h c", h=XH),
                         xwkv[DM:2 * DM, :].rearrange("(h e) c -> e h c", h=XH)).then_inc(ld_xwv, 16)
            sp.dma_start(eq[0:SEQ, 1, :], xwout).then_inc(ld_xwo, 16)
            sp.dma_start(bout[:], xb_out.partition_broadcast(P)).then_inc(ld_xb, 16)
            for b in range(2):
                sp.dma_start(bcol[b * SEQ:(b + 1) * SEQ, :], xb_out.rearrange("(o n) -> o n", n=1)).then_inc(ld_xb, 16)
                sp.dma_start(gcol[b * SEQ:(b + 1) * SEQ, :], xg.rearrange("a c n -> (a c) n")).then_inc(ld_xb, 16)
            sp.dma_start(down_sb[:], down_w.rearrange("(k p) n -> p k n", p=P)).then_inc(ld_down, 16)
            sp.dma_start(gamma[:], ln_gamma.partition_broadcast(P)).then_inc(ld_gb, 16)
            sp.dma_start(beta[:], ln_beta.partition_broadcast(P)).then_inc(ld_gb, 16)
            sp.wait_ge(lo_a, 1 + KC)
            sp.dma_start(cw[:].rearrange("p (k j) n -> p k j n", k=KC),
                         up_w.rearrange("(k p) (j n) -> p k j n", p=P, j=2)).then_inc(ld_up, 16)
            sp.dma_start(gate_sb[:],
                         gate_w.rearrange("(k p) n -> p k n", p=P)).then_inc(ld_gate, 16)
            sp.wait_ge(lo_c, 1 + KC)
            sp.dma_start(cw[:, 0:2, :].rearrange("p j n -> p (j n)").rearrange("p (k n) -> p k n", k=KC),
                         fc1_w.rearrange("(k p) n -> p k n", p=P)).then_inc(ld_fc, 16)
            sp.dma_start(cw[:, 2, :].rearrange("p (k n) -> p k n", k=LC),
                         expert_w.rearrange("(k p) n -> p k n", p=P)).then_inc(ld_fc, 16)
            sp.dma_start(cw[:, 3:5, :], fc2_w.rearrange("(k p) n -> p k n", p=P)).then_inc(ld_fc, 16)
            y_out.wait(sp, PAIRS, 0)

        @block.tensor
        def _(pe):
            def product(o, pairs_of, start, stop, **kw):
                n = len(pairs_of)
                for j, (l, r) in enumerate(pairs_of):
                    ins = pe.matmul(o, l, r, start=start and j == 0, stop=stop and j == n - 1, **kw)
                return ins

            def split(l_hi, l_lo, r_hi, r_lo):
                return [(l_hi, r_hi), (l_hi, r_lo), (l_lo, r_hi)]

            def turn(o, src):
                for j in range(KC):
                    ins = pe.transpose(o[:, j * P:(j + 1) * P], src[:, j * P:(j + 1) * P], ident)
                return ins

            def setup():
                pe.wait_ge(ld_tab, 16)

            def weights_b(part):
                if part < 2:
                    s, slot, o = ((ld_xwq, ek, B0), (ld_xwk, eq, B1))[part]
                    pe.wait_ge(s, 32)
                    turn(o, slot[:, 0, :]).then_inc(tr_b, 1)
                elif part == 2:
                    pe.wait_ge(ld_xwo, 16)
                    for h in range(XH):
                        ins = pe.transpose(B2[0:XD, h * SEQ:(h + 1) * SEQ], eq[0:SEQ, 1, h * XD:(h + 1) * XD],
                                           ident[0:SEQ, 0:SEQ])
                    ins.then_inc(tr_b, 1)
                else:
                    pe.wait_ge(hi_b, 3)
                    pe.wait_ge(lo_b, 2)
                    pe.wait_ge(ld_xwv, 16)
                    for h in range(XH):
                        ins = pe.matmul(B0[0:XD, h * SEQ:(h + 1) * SEQ], ek[0:XD, 1, h * XD:(h + 1) * XD],
                                        eqt[0:XD, 0, h * SEQ:(h + 1) * SEQ], start=True, stop=True)
                    ins.then_inc(tr_b, 1)

            def fold(part):
                n = part % 2
                o = (C0, C1)[n]
                if part < 2:
                    pe.wait_ge(ld_fc, 48)
                    fc1 = cw[:, 0:2, :].rearrange("p j n -> p (j n)").rearrange("p (k n) -> p k n", k=KC)
                    for k in range(KC):
                        ins = pe.transpose(o[:, k * P:(k + 1) * P], fc1[:, k, n * P:(n + 1) * P], ident)
                    ins.then_inc(fold_ps, 1)
                elif part < 4:
                    pe.wait_ge(fold_sb, 2)
                    product(o[:], [(cw[:, 2, l * LAT + n * P:l * LAT + (n + 1) * P], cw[:, 5 + l, :])
                                   for l in range(LC)], True, True).then_inc(fold_ps, 1)
                else:
                    k = part - 4
                    pe.wait_ge(fold_sb, 4)
                    if k >= 2:
                        pe.wait_ge(wr_l, k - 1)
                    product(o[:], [(cw[:, m, k * P:(k + 1) * P], cw[:, 3 + m, :]) for m in range(LC)],
                            True, True).then_inc(wr_ps, 1)

            def x_turn(p):
                x_load.wait(pe, p, 16)
                pt_done.wait(pe, p, 0)
                turn(A0, x_in).then_inc(xt_ps.sem, 1)

            def qkv(p):
                if first(p):
                    pe.wait_ge(lo_a, 1 + KC)
                xt_h.wait(pe, p, 1)
                xt_l.wait(pe, p, 1)
                o_nrm.wait(pe, p - 1, 0)
                product(A2[:, 0:2 * HD], [t for k in range(KC) for t in
                                          split(xt_hi[:, k, :], xt_lo[:, k, :], wkv_hi[:, k, :], wkv_lo[:, k, :])],
                        True, True).then_inc(kv_ps.sem, 1)
                z_done.wait(pe, p, 0)
                product(A1[:], [t for k in range(KC) for t in
                                split(xt_hi[:, k, :], xt_lo[:, k, :], wq_hi[:, k, :], wq_lo[:, k, :])],
                        True, True).then_inc(q_ps_a.sem, 1)

            def qk_turn(p):
                k_rep.wait(pe, p, 1)
                pe.transpose(A2[:, 0:P], k_sb[:], ident).then_inc(ktr_ps.sem, 1)
                q_h.wait(pe, p, 1)
                q_l.wait(pe, p, 1)
                for half, o in enumerate((A0, A1)):
                    turn(o, q_sb[:, half * KC:(half + 1) * KC].rearrange("p u s n -> p (u s n)"))\
                        .then_inc(qt_ps.sem, 1)

            S_BANK = (A0, A1, A2, A1)

            def scores(p, g):
                if g == 0:
                    if first(p):
                        pe.wait_ge(tab_r, 2)
                        pe.wait_ge(zeroed, 2)
                    kd_done.wait(pe, p, 4)
                if g < 2:
                    qt_done.wait(pe, p, 2 if g else 1)
                if g == 2:
                    ct_done.wait(pe, p, 1)
                if g == 3:
                    s_sub.wait(pe, p, 2)
                pe.matmul(S_BANK[g][:], left_r[:, g, :], right_r[:], start=True, stop=False)
                for n, quad in enumerate((2 * g, 2 * g + 1)):
                    o = S_BANK[g][:, n * HQ * SEQ:(n + 1) * HQ * SEQ]
                    ins = product(o, [(qt[:, quad, b * SEQ:b * SEQ + P], kd[:, b].rearrange("p h k -> p (h k)"))
                                      for b in range(2) for kd in (kd_hi, kd_lo)], False, n == 1)
                ins.then_inc(s_ps.sem, 1)

            PT_BANK = (A0, A0, A1, A0)

            def prob_turn(p, g):
                s_nrm.wait(pe, p, g + 1)
                if g in (1, 3):
                    pt_done.wait(pe, p, g)
                if g == 2:
                    s_sub.wait(pe, p, 4)
                turn(PT_BANK[g], prob[:, g % 2, :]).then_inc(pt_ps.sem, 1)

            def values(p, half):
                pt_done.wait(pe, p, 2 * half + 2)
                if half == 0:
                    s_sub.wait(pe, p, 3)
                ao = A2[:].rearrange("p (g t) -> p g t", g=GROUPS)
                for j in range(HG // 2):
                    for b in range(2):
                        ins = pe.matmul(ao[j * 2 * HD:(j + 1) * 2 * HD, 2 * half:2 * half + 2, b * SEQ:(b + 1) * SEQ],
                                        vpair[:, b, :], pt_sb[:, :, j * P + b * SEQ:j * P + (b + 1) * SEQ],
                                        start=True, stop=True)
                ins.then_inc(ao_ps.sem, 1)

            def project(p, half):
                if first(p):
                    pe.wait_ge(ld_wo, 16)
                if half == 0:
                    ao_done.wait(pe, p, 1)
                    pt_done.wait(pe, p, 3)
                ins = product(A1[:], [(ao_sb[:, g, :], wo_sb[:, g, :]) for g in (2 * half, 2 * half + 1)],
                              half == 0, half == 1)
                if half == 1:
                    ins.then_inc(y_ps.sem, 1)

            def c_turn(p):
                c_load.wait(pe, p, 16)
                kt_l.wait(pe, p, 1)
                turn(A2, c_in).then_inc(ct_ps.sem, 1)

            def keys(p, u):
                b, blk = divmod(u, KC)
                if u == 0:
                    if first(p):
                        pe.wait_ge(g_c, 3)
                    cs_h.wait(pe, p, 2)
                    cs_l.wait(pe, p, 2)
                    q_sub.wait(pe, p, 0)
                else:
                    k_exp.wait(pe, p, u)
                cols = slice(blk * P, (blk + 1) * P)
                product(B0[:], [(xwk_hi[:, cols], cs[:, b, :]), (xwk_lo[:, cols], cs[:, b, :])],
                        True, True).then_inc(k_ps.sem, 1)

            def keys_turn(p, u):
                k_exp.wait(pe, p, u + 1)
                if u == 0:
                    eqt_done.wait(pe, p, 0)
                elif u == 7:
                    mt_done.wait(pe, p, 1)
                else:
                    ekt_done.wait(pe, p, u)
                turn(B1, ek[:, u % 2, :]).then_inc(kt_ps.sem, 1)

            def context(p, w):
                b, half = divmod(w, 2)
                ekt_done.wait(pe, p, 2 * w + 2)
                if w == 0:
                    o_add.wait(pe, p, 0)
                    ct_done.wait(pe, p, 1)
                if w == 2:
                    t_done.wait(pe, p, 1)
                product(B2[:, half * 2 * P:(half + 1) * 2 * P],
                        [(ct[:, 2 * n + b].rearrange("p s c -> p (s c)"), e[:, n].rearrange("p u m -> p (u m)"))
                         for n in range(KC) for e in (ekt_hi, ekt_lo)], True, True).then_inc(t_ps.sem, 1)

            def combine(p, b):
                t_done.wait(pe, p, b + 1)
                if b == 0:
                    ekt_done.wait(pe, p, 7)
                else:
                    eqt_done.wait(pe, p, 2)
                for h in range(XH):
                    cols = slice(h * XD, (h + 1) * XD)
                    ins = pe.matmul(B1[h % 2 * XD:(h % 2 + 1) * XD, h // 2 * SEQ:(h // 2 + 1) * SEQ],
                                    tctx[:, cols], vout[:, cols], start=True, stop=True)
                ins.then_inc(m_ps.sem, 1)

            def queries(p, v):
                b, n = divmod(v, KC)
                if v == 0:
                    xs_h.wait(pe, p, 2)
                    xs_l.wait(pe, p, 2)
                    k_exp.wait(pe, p, 8)
                else:
                    q_sub.wait(pe, p, v)
                cols = slice(n * P, (n + 1) * P)
                product(B0[:], [(xs[:, b, cols], xwq_hi[:]), (xs[:, b, cols], xwq_lo[:])],
                        True, True).then_inc(q_ps.sem, 1)

            def queries_turn(p, v):
                q_nrm.wait(pe, p, v + 1)
                if v == 0:
                    ekt_done.wait(pe, p, 8)
                elif v == 2:
                    mt_done.wait(pe, p, 2)
                else:
                    eqt_done.wait(pe, p, v)
                turn(B1, eq[:, v % 2, :]).then_inc(eqt_ps.sem, 1)

            def attend(p, v):
                b, n = divmod(v, KC)
                eqt_done.wait(pe, p, v + 1)
                if v == 0:
                    t_done.wait(pe, p, 2)
                mt_done.wait(pe, p, b + 1)
                product(B2[b * SEQ:(b + 1) * SEQ, n * P:(n + 1) * P],
                        [(mt[:, b, blk, :], eqt[:, v % 2, blk * P:(blk + 1) * P]) for blk in range(KC)],
                        True, True).then_inc(o_ps.sem, 1)

            def o_var(p):
                o_sq.wait(pe, p, 1)
                if not isinstance(p, int) or p + 1 < PAIRS:
                    ao_done.wait(pe, p + 1, 1)
                for n in range(KC):
                    ins = pe.matmul(A2[:, 2 * n:2 * n + 2], eq[:, 0, n * P:(n + 1) * P], batch_mean,
                                    start=True, stop=True)
                ins.then_inc(ov_ps.sem, 1)

            def o_spread(p):
                o_rstd.wait(pe, p, 1)
                for n in range(KC):
                    for b in range(2):
                        ins = pe.matmul(A2[b * SEQ:(b + 1) * SEQ, n * P:(n + 1) * P],
                                        orstd[:, 2 * n + b:2 * n + b + 1].broadcast_to([P, SEQ]), ident,
                                        start=True, stop=True)
                ins.then_inc(or_ps.sem, 1)

            def x2_turn(p):
                if first(p):
                    pe.wait_ge(wr_l, 4)
                    pe.wait_ge(lo_c, 1 + KC)
                x2_done.wait(pe, p, 1)
                f_add.wait(pe, p, 0)
                turn(C0, x2).then_inc(x2t_ps.sem, 1)

            def logits(p):
                x2t_h.wait(pe, p, 1)
                x2t_l.wait(pe, p, 1)
                ro_done.wait(pe, p, 0)
                product(C1[:, 0:NE], [t for k in range(KC) for t in
                                      split(x2t_hi[:, k, :], x2t_lo[:, k, :], gate_hi[:, k, :], gate_lo[:, k, :])],
                        True, True).then_inc(lg_ps.sem, 1)

            def hidden(p, j):
                if j == 1:
                    lg_top.wait(pe, p, 1)
                cols = slice(j * DM, (j + 1) * DM)
                product((C0, C1)[j][:], [t for k in range(KC) for t in
                                         split(x2t_hi[:, k, :], x2t_lo[:, k, :], up_hi[:, k, cols], up_lo[:, k, cols])],
                        True, True).then_inc(h_ps.sem, 1)

            def hidden_turn(p, j):
                h_sq.wait(pe, p, j + 1)
                turn((C0, C1)[j], h_sb[:, j, :]).then_inc(ht_ps.sem, 1)

            def shared(p, part):
                if part == 0:
                    if first(p):
                        pe.wait_ge(ld_down, 16)
                    ht_done.wait(pe, p, 2)
                ins = product(C0[:], [(ht_sb[:, n // KC, (n % KC) * P:(n % KC + 1) * P], down_sb[:, n, :])
                                      for n in (2 * part, 2 * part + 1)], part == 0, part == 3)
                if part == 3:
                    ins.then_inc(sh_ps.sem, 1)

            def routing(p):
                product(C1[:], [t for k in range(KC) for t in
                                split(x2t_hi[:, k, :], x2t_lo[:, k, :], wr_hi[:, k, :], wr_lo[:, k, :])],
                        True, True).then_inc(ro_ps.sem, 1)

            def work(due):
                for part in once(due, "weights_b"):
                    weights_b(part)
                for part in once(due, "fold"):
                    fold(part)
                for p, v in due("attend"):
                    attend(p, v)
                for p, u in due("context"):
                    context(p, u)
                for p, v in due("queries_turn"):
                    queries_turn(p, v)
                for p, u in due("keys_turn"):
                    keys_turn(p, u)
                for p, u in due("keys"):
                    keys(p, u)
                for p, v in due("queries"):
                    queries(p, v)
                for p, _ in due("x_turn"):
                    x_turn(p)
                for p, _ in due("qkv"):
                    qkv(p)
                for p, _ in due("qk_turn"):
                    qk_turn(p)
                for p, g in due("prob_turn"):
                    prob_turn(p, g)
                for p, g in due("scores"):
                    scores(p, g)
                for p, half in due("values"):
                    values(p, half)
                for p, half in due("project"):
                    project(p, half)
                for p, _ in due("c_turn"):
                    c_turn(p)
                for p, _ in due("x2_turn"):
                    x2_turn(p)
                for p, _ in due("logits"):
                    logits(p)
                for p, j in due("hidden"):
                    hidden(p, j)
                for p, j in due("hidden_turn"):
                    hidden_turn(p, j)
                for p, part in due("shared"):
                    shared(p, part)
                for p, _ in due("routing"):
                    routing(p)
                for p, b in due("combine"):
                    combine(p, b)
                for p, _ in due("o_var"):
                    o_var(p)
                for p, _ in due("o_spread"):
                    o_spread(p)

            drive(pe, WHEN["pe"], setup, work)

        @block.vector
        def _(dve):
            def low(o, whole, hi):
                return dve.tensor_tensor(o, whole, f32(hi), ALU.subtract)

            def statistics(n, p):
                z, done = ((x_keep[:], z_done), (zb_sb[:], zb_done), (f_sb, f_add), (f_sb, f_res))[n]
                done.wait(dve, p, 1)
                dve.bn_stats(stats[n][:], z).then_inc(ln_stat[n].sem, 1)

            def mean_var(n, p):
                ln_stat[n].wait(dve, p, 1)
                dve.memset(wait_pad[:], 0.0)
                dve.bn_aggr(meanvar[n][:], stats[n][:]).then_inc(ln_mean[n].sem, 1)
                ln_mean[n].wait(dve, p, 1)
                dve.tensor_scalar(var_eps[n][:], meanvar[n][:, 1:2], EPS, None, ALU.add).then_inc(ln_eps[n].sem, 1)

            def normalize(n, p, o, z):
                ln_rstd[n].wait(dve, p, 1)
                return dve.tensor_scalar(o, z, meanvar[n][:, 0:1], rstd[n][:, 0:1], ALU.subtract, ALU.mult)

            def setup():
                dve.memset(f32(qt[:, :, SEQ:2 * SEQ]), 0.0).then_inc(zeroed, 1)
                dve.memset(vpair[:], 0.0).then_inc(zeroed, 1)
                dve.wait_ge(zeroed, 2)
                dve.wait_ge(ld_wkv, 16)
                wkv_v = cw[:, 0, 0:KC * 2 * HD].rearrange("p (k n) -> p k n", k=KC)
                dve.wait_ge(hi_a, 1)
                low(wkv_lo[:], wkv_v, wkv_hi[:]).then_inc(lo_a, 1)

            def split_wq(k):
                dve.wait_ge(hi_a, 2 + k)
                low(wq_lo[:, k], cw[:, 1 + k, :], wq_hi[:, k]).then_inc(lo_a, 1)

            def weights_b(part):
                if part < 2:
                    o, hi, ps = ((xwq_lo, xwq_hi, B0), (xwk_lo, xwk_hi, B1))[part]
                    dve.wait_ge(hi_b, part + 1)
                    low(o[:], ps[:], hi[:]).then_inc(lo_b, 1)
                elif part == 3:
                    dve.wait_ge(tr_b, 4)
                    v = B0[0:XD, :].rearrange("c (h o) -> c h o", o=SEQ)
                    dve.tensor_reduce(vmean[:], v, ALONG_FREE, ALU.add).then_inc(g_b, 1)
                    dve.wait_ge(g_b, 1)
                    dve.tensor_scalar(vmean[:], vmean[:], 1.0 / SEQ, None, ALU.mult).then_inc(g_b, 1)
                    dve.wait_ge(g_b, 2)
                    for twice in range(2):
                        dve.tensor_tensor(vout[twice * XD:(twice + 1) * XD, :].rearrange("c (h o) -> c h o", o=SEQ), v,
                                          vmean[:, :, None].broadcast_to([XD, XH, SEQ]), ALU.subtract).then_inc(g_c, 1)
                    dve.wait_ge(ld_xb, 80)
                    dve.tensor_reduce(bmean[:], bout[:], ALONG_FREE, ALU.add).then_inc(g_b, 1)
                    dve.wait_ge(g_b, 3)
                    dve.tensor_scalar(bmean[:], bmean[:], 1.0 / SEQ, None, ALU.mult).then_inc(g_b, 1)
                    dve.wait_ge(g_b, 4)
                    dve.tensor_scalar(bcol[:], bcol[:], bmean[:, 0:1], None, ALU.subtract).then_inc(g_c, 1)

            def split_up(k):
                if k == 0:
                    dve.wait_ge(hi_c, 1)
                    low(gate_lo[:], gate_sb[:], gate_hi[:]).then_inc(lo_c, 1)
                dve.wait_ge(hi_c, 2 + k)
                low(up_lo[:, k, :], cw[:, 2 * k:2 * k + 2, :].rearrange("p s n -> p (s n)"), up_hi[:, k, :])\
                    .then_inc(lo_c, 1)

            def fold(part):
                if part >= 4:
                    k = part - 4
                    dve.wait_ge(wr_h, k + 1)
                    low(wr_lo[:, k, :], (C0, C1)[k % 2][:], wr_hi[:, k, :]).then_inc(wr_l, 1)

            def x_low(p):
                xt_h.wait(dve, p, 1)
                low(xt_lo[:].rearrange("p k n -> p (k n)"), A0[:], xt_hi[:].rearrange("p k n -> p (k n)"))\
                    .then_inc(xt_l.sem, 1)

            def values_by_pair(p):
                kv_ps.wait(dve, p, 1)
                for b in range(2):
                    for half in range(2):
                        ins = dve.tensor_copy(
                            vpair[half * SEQ:(half + 1) * SEQ, b, half * HD:(half + 1) * HD],
                            A2[b * SEQ:(b + 1) * SEQ, HD:2 * HD])
                ins.then_inc(v_done.sem, 1)

            def q_low(p):
                q_h.wait(dve, p, 1)
                dve.scalar_tensor_tensor(q_sb[:, :, 1, :], A1[:].rearrange("p (u n) -> p u n", u=QUADS), HD ** -0.5,
                                         q_sb[:, :, 0, :], ALU.mult, ALU.subtract).then_inc(q_l.sem, 1)

            def k_low(p):
                kt_h.wait(dve, p, 1)
                low(kt_lo[:], A2[:, 0:P], kt_hi[:]).then_inc(kt_l.sem, 1)

            def heads(ap):
                return ap.rearrange("p (h k) -> p h k", h=HG)

            def score_max(p, g):
                ps = (A0, A1, A2, A1)[g]
                s_ps.wait(dve, p, g + 1)
                dve.tensor_reduce(smax[:, g, :], heads(ps[:]), ALONG_FREE, ALU.max).then_inc(s_max.sem, 1)

            def score_sub(p, g):
                ps = (A0, A1, A2, A1)[g]
                s_max.wait(dve, p, g + 1)
                if g < 2:
                    pt_ps.wait(dve, p, 0)
                else:
                    pt_ps.wait(dve, p, g - 1)
                dve.tensor_tensor(heads(prob[:, g % 2, :]), heads(ps[:]),
                                  smax[:, g, :, None].broadcast_to([P, HG, SEQ]), ALU.subtract).then_inc(s_sub.sem, 1)

            def prob_sum(p, g):
                s_exp.wait(dve, p, g + 1)
                dve.tensor_reduce(ssum[:, g, :], heads(prob[:, g % 2, :]), ALONG_FREE, ALU.add).then_inc(s_sum.sem, 1)

            def prob_rec(p, g):
                s_sum.wait(dve, p, g + 1)
                dve.reciprocal(srec[:, g, :], ssum[:, g, :]).then_inc(s_rec.sem, 1)

            def residual_a(p):
                y_ps.wait(dve, p, 1)
                x_kept.wait(dve, p, 1)
                dve.tensor_tensor(x_keep[:], A1[:], x_keep[:], ALU.add).then_inc(z_done.sem, 1)

            def finish_a(p):
                zb_done.wait(dve, p, 0)
                xs_h.wait(dve, p, 0)
                normalize(0, p, x1[:], x_keep[:]).then_inc(x1_done.sem, 1)

            def stacks(p, src, o, h, l):
                h.wait(dve, p, 2)
                for b in range(2):
                    rows, other = slice(b * SEQ, (b + 1) * SEQ), slice((1 - b) * SEQ, (2 - b) * SEQ)
                    low(o[other, b, :], src[rows, :], o[rows, b, :]).then_inc(l.sem, 1)

            def key_max(p, u):
                k_ps.wait(dve, p, u + 1)
                dve.tensor_reduce(kneg[:, u:u + 1], B0[:], ALONG_FREE, ALU.max, negate=True).then_inc(k_neg.sem, 1)

            def key_turned(p, u):
                ekt_h.wait(dve, p, u + 1)
                low(ekt_lo[:, :, u % 2, :], B1[:].rearrange("p (n m) -> p n m", n=KC), ekt_hi[:, :, u % 2, :])\
                    .then_inc(ekt_done.sem, 1)

            def c_turned_low(p):
                ct_h.wait(dve, p, 1)
                low(ct[:, :, 1, :], A2[:].rearrange("p (x c) -> p x c", c=SEQ), ct[:, :, 0, :]).then_inc(ct_done.sem, 1)

            def key_scale(p, b):
                cols = slice(b * KC, (b + 1) * KC)
                k_exp.wait(dve, p, (b + 1) * KC)
                dve.reciprocal(krec[:, cols], ksum[:, cols]).then_inc(k_rec.sem, 1)
                k_rec.wait(dve, p, b + 1)
                dve.tensor_scalar(krec[:, cols], krec[:, cols], XD ** -0.5, None, ALU.mult).then_inc(k_scl.sem, 1)
                k_scl.wait(dve, p, b + 1)
                m_ps.wait(dve, p, b + 1)
                dve.tensor_tensor(mt[:, b], B1[:, 0:KC * SEQ].rearrange("p (k o) -> p k o", k=KC),
                                  krec[:, cols][:, :, None].broadcast_to([P, KC, SEQ]), ALU.mult)\
                    .then_inc(mt_done.sem, 1)

            def xheads(ap):
                return ap.rearrange("p (h d) -> p h d", h=XH)

            def query_max(p, v):
                q_ps.wait(dve, p, v + 1)
                dve.tensor_reduce(qmax[:, v, :], xheads(B0[:]), ALONG_FREE, ALU.max).then_inc(q_max.sem, 1)

            def query_sub(p, v):
                q_max.wait(dve, p, v + 1)
                if v < 2:
                    eqt_ps.wait(dve, p, 0)
                    ov_ps.wait(dve, p, 0)
                else:
                    eqt_ps.wait(dve, p, v - 1)
                dve.tensor_tensor(xheads(eq[:, v % 2, :]), xheads(B0[:]),
                                  qmax[:, v, :, None].broadcast_to([P, XH, XD]), ALU.subtract).then_inc(q_sub.sem, 1)

            def query_sum(p, v):
                q_exp.wait(dve, p, v + 1)
                dve.tensor_reduce(qsum[:, v, :], xheads(eq[:, v % 2, :]), ALONG_FREE, ALU.add).then_inc(q_sum.sem, 1)

            def query_rec(p, v):
                q_sum.wait(dve, p, v + 1)
                dve.reciprocal(qrec[:, v, :], qsum[:, v, :]).then_inc(q_rec.sem, 1)

            def output_var(p):
                ov_ps.wait(dve, p, 1)
                dve.tensor_scalar(ovar[:], A2[:, 0:UNITS], EPS, None, ALU.add).then_inc(o_eps.sem, 1)

            def residual_b(p):
                or_ps.wait(dve, p, 1)
                dve.scalar_tensor_tensor(zb_sb[:], o_sb[:], gcol[:, 0:1], A2[:], ALU.mult, ALU.mult)\
                    .then_inc(o_nrm.sem, 1)

            def residual_b_add(p):
                o_nrm.wait(dve, p, 1)
                dve.tensor_tensor(zb_sb[:], zb_sb[:], x1[:], ALU.add).then_inc(zb_done.sem, 1)

            def finish_b(p):
                x2t_ps.wait(dve, p, 0)
                xb_done.wait(dve, p, 0)
                normalize(1, p, x2[:], zb_sb[:]).then_inc(x2_done.sem, 1)

            def x2_low(p):
                x2t_h.wait(dve, p, 1)
                low(x2t_lo[:].rearrange("p k n -> p (k n)"), C0[:], x2t_hi[:].rearrange("p k n -> p (k n)"))\
                    .then_inc(x2t_l.sem, 1)

            def route(p):
                lg_ps.wait(dve, p, 1)
                dve.memset(wait_pad[:], 0.0)
                dve.max(top8[:], C1[:, 0:NE]).then_inc(lg_top.sem, 1)
                lg_top.wait(dve, p, 1)
                ro_done.wait(dve, p, 0)
                dve.tensor_tensor(rsum[:], top8[:, 0:1], top8[:, 1:2], ALU.add).then_inc(lg_sum.sem, 1)

            def ffn_sum(p):
                ro_done.wait(dve, p, 1)
                sh_ps.wait(dve, p, 1)
                dve.tensor_tensor(f_sb, C0[:], routed, ALU.add).then_inc(f_add.sem, 1)

            def ffn_norm(p):
                normalize(2, p, f_sb, f_sb).then_inc(f_nrm.sem, 1)

            def residual_c(p):
                f_gam.wait(dve, p, 1)
                xb_done.wait(dve, p, 1)
                dve.tensor_tensor(f_sb, f_sb, x2_beta, ALU.add).then_inc(f_res.sem, 1)

            def finish_c(p):
                y_out.wait(dve, p, 0)
                normalize(3, p, y_sb, f_sb).then_inc(y_done.sem, 1)

            def work(due):
                for k in once(due, "split_wq"):
                    split_wq(k)
                for part in once(due, "weights_b"):
                    weights_b(part)
                for k in once(due, "split_up"):
                    split_up(k)
                for part in once(due, "fold"):
                    fold(part)
                for p, b in due("combined"):
                    key_scale(p, b)
                for p, u in due("keys_turn"):
                    key_turned(p, u)
                for p, u in due("keys"):
                    key_max(p, u)
                for p, v in due("query_sum"):
                    query_sum(p, v)
                for p, v in due("queries"):
                    query_max(p, v)
                for p, g in due("prob_sum"):
                    prob_sum(p, g)
                for p, v in due("query_rec"):
                    query_rec(p, v)
                for p, v in due("query_sub"):
                    query_sub(p, v)
                for p, g in due("prob_rec"):
                    prob_rec(p, g)
                for p, _ in due("residual_a"):
                    residual_a(p)
                for p, _ in due("residual_b"):
                    residual_b(p)
                for p, _ in due("residual_b_add"):
                    residual_b_add(p)
                for p, _ in due("finish_a"):
                    finish_a(p)
                    stacks(p, x1, xs, xs_h, xs_l)
                for p, _ in due("x_turn"):
                    x_low(p)
                for p, _ in due("qkv"):
                    values_by_pair(p)
                    q_low(p)
                for p, _ in due("qk_turn"):
                    k_low(p)
                for p, g in due("scores"):
                    score_max(p, g)
                for p, g in due("score_sub"):
                    score_sub(p, g)
                for p, _ in due("c_split"):
                    stacks(p, c_in, cs, cs_h, cs_l)
                for p, _ in due("c_turn"):
                    c_turned_low(p)
                for p, _ in due("o_var"):
                    output_var(p)
                for p, _ in due("finish_b"):
                    finish_b(p)
                for p, _ in due("x2_turn"):
                    x2_low(p)
                for p, _ in due("logits"):
                    route(p)
                for p, _ in due("ffn_sum"):
                    ffn_sum(p)
                for p, _ in due("ffn_norm"):
                    ffn_norm(p)
                for p, _ in due("residual_c"):
                    residual_c(p)
                for p, _ in due("finish_c"):
                    finish_c(p)
                for n in range(4):
                    for p, _ in due(f"statistics_{n}"):
                        statistics(n, p)
                for n in range(4):
                    for p, _ in due(f"mean_var_{n}"):
                        mean_var(n, p)

            drive(dve, WHEN["dve"], setup, work)

        @block.scalar
        def _(act):
            def copy(o, i, scale=1.0):
                return act.activation(o, i, ACT.Copy, scale=scale)

            def setup():
                act.wait_ge(ld_wkv, 16)
                wkv_v = cw[:, 0, 0:KC * 2 * HD].rearrange("p (k n) -> p k n", k=KC)
                copy(wkv_hi[:], wkv_v).then_inc(hi_a, 1)

            def split_wq(k):
                act.wait_ge(ld_wq, 16)
                copy(wq_hi[:, k], cw[:, 1 + k, :]).then_inc(hi_a, 1)
                if k == KC - 1:
                    act.wait_ge(ld_bias, 16)
                    copy(left_r[:].rearrange("p g t -> p (g t)"), eqt[:, 0, :]).then_inc(tab_r, 1)
                    copy(right_r[:], eqt[:, 1, :]).then_inc(tab_r, 1)

            def weights_b(part):
                if part < 3:
                    act.wait_ge(tr_b, part + 1)
                    o = (xwq_hi[:], xwk_hi[:], eqt[0:XD, 0, :])[part]
                    copy(o, (B0[:], B1[:], B2[0:XD, :])[part]).then_inc(hi_b, 1)

            def split_up(k):
                if k == 0:
                    act.wait_ge(ld_gate, 16)
                    copy(gate_hi[:], gate_sb[:]).then_inc(hi_c, 1)
                    act.wait_ge(ld_up, 16)
                copy(up_hi[:, k, :], cw[:, 2 * k:2 * k + 2, :].rearrange("p s n -> p (s n)")).then_inc(hi_c, 1)

            def fold(part):
                ps = (C0, C1)[part % 2]
                if part < 4:
                    act.wait_ge(fold_ps, part + 1)
                    copy(cw[:, (5, 6, 0, 1)[part], :], ps[:]).then_inc(fold_sb, 1)
                else:
                    act.wait_ge(wr_ps, part - 3)
                    copy(wr_hi[:, part - 4, :], ps[:]).then_inc(wr_h, 1)

            def load_x(p):
                if first(p):
                    return
                xt_ps.wait(act, p, 0)
                x_kept.wait(act, p, 0)
                act.dma_start(x_in[:], x[p]).then_inc(x_load.sem, 16)

            def load_c(p):
                ct_ps.wait(act, p, 0)
                cs_h.wait(act, p, 0)
                cs_l.wait(act, p, 0)
                act.dma_start(c_in[:], ctx[p]).then_inc(c_load.sem, 16)

            def store_y(p):
                y_done.wait(act, p, 1)
                act.dma_start(out[p], y_sb).then_inc(y_out.sem, 16)

            def keep(p):
                x_load.wait(act, p, 16)
                x1_done.wait(act, p, 0)
                copy(x_keep[:], x_in[:]).then_inc(x_kept.sem, 1)

            def x_high(p):
                xt_ps.wait(act, p, 1)
                copy(xt_hi[:].rearrange("p k n -> p (k n)"), A0[:]).then_inc(xt_h.sem, 1)

            def qkv_high(p):
                v_done.wait(act, p, 1)
                copy(k_sb[:].rearrange("p (h d) -> p h d", d=HD), A2[:, None, 0:HD].broadcast_to([P, HG, HD]))\
                    .then_inc(k_rep.sem, 1)
                q_ps_a.wait(act, p, 1)
                ao_ps.wait(act, p, 0)
                copy(q_sb[:, :, 0, :].bitcast(F32R), A1[:].rearrange("p (u n) -> p u n", u=QUADS), HD ** -0.5)\
                    .then_inc(q_h.sem, 1)

            def qk_turned(p):
                ktr_ps.wait(act, p, 1)
                copy(kt_hi[:], A2[:, 0:P]).then_inc(kt_h.sem, 1)
                for half, ps in enumerate((A0, A1)):
                    qt_ps.wait(act, p, half + 1)
                    copy(qt[:, half * KC:(half + 1) * KC].rearrange("p u (b t) -> p u b t", t=SEQ)[:, :, 0:3:2, :],
                         ps[:].rearrange("p (u b t) -> p u b t", u=KC, b=2)).then_inc(qt_done.sem, 1)

            def prob_exp(p, g):
                s_sub.wait(act, p, g + 1)
                act.activation(prob[:, g % 2, :], prob[:, g % 2, :], ACT.Exp).then_inc(s_exp.sem, 1)

            def prob_turned(p, g):
                pt_ps.wait(act, p, g + 1)
                if g < 2:
                    ao_ps.wait(act, p, 0)
                else:
                    ao_ps.wait(act, p, 1)
                copy(pt_sb[:, g % 2, :], (A0, A0, A1, A0)[g][:]).then_inc(pt_done.sem, 1)

            def values_out(p):
                ao_ps.wait(act, p, 2)
                copy(ao_sb[:].rearrange("p g t -> p (g t)"), A2[:]).then_inc(ao_done.sem, 1)

            def stacks(p, src, o, h):
                for b in range(2):
                    rows = slice(b * SEQ, (b + 1) * SEQ)
                    copy(o[rows, b, :], src[rows, :]).then_inc(h.sem, 1)

            def c_high(p):
                c_load.wait(act, p, 16)
                k_ps.wait(act, p, 0)
                stacks(p, c_in, cs, cs_h)

            def c_turned(p):
                ct_ps.wait(act, p, 1)
                t_ps.wait(act, p, 0)
                copy(ct[:, :, 0, :], A2[:].rearrange("p (x c) -> p x c", c=SEQ)).then_inc(ct_h.sem, 1)

            def x_stack(p):
                x1_done.wait(act, p, 1)
                q_ps.wait(act, p, 0)
                stacks(p, x1, xs, xs_h)

            def key_exp(p, u):
                k_neg.wait(act, p, u + 1)
                if u < 2:
                    kt_ps.wait(act, p, 0)
                    mt_done.wait(act, p, 0)
                else:
                    kt_ps.wait(act, p, u - 1)
                act.activation(ek[:, u % 2, :], B0[:], ACT.Exp, bias=kneg[:, u:u + 1],
                               accum_out=ksum[:, u:u + 1]).then_inc(k_exp.sem, 1)

            def key_turned(p, u):
                kt_ps.wait(act, p, u + 1)
                t_ps.wait(act, p, u // 2)
                copy(ekt_hi[:, :, u % 2, :], B1[:].rearrange("p (n m) -> p n m", n=KC)).then_inc(ekt_h.sem, 1)

            def context_out(p, b):
                t_ps.wait(act, p, 2 * (b + 1))
                m_ps.wait(act, p, b)
                copy(tctx[:], B2[:]).then_inc(t_done.sem, 1)

            def query_exp(p, v):
                q_sub.wait(act, p, v + 1)
                act.activation(eq[:, v % 2, :], eq[:, v % 2, :], ACT.Exp).then_inc(q_exp.sem, 1)

            def query_turned(p, v):
                eqt_ps.wait(act, p, v + 1)
                if v < 2:
                    o_ps.wait(act, p, 0)
                else:
                    o_ps.wait(act, p, v - 1)
                copy(eqt[:, v % 2, :], B1[:]).then_inc(eqt_done.sem, 1)

            def output_square(p):
                if first(p):
                    act.wait_ge(g_c, 3)
                o_ps.wait(act, p, 8)
                x2_done.wait(act, p, 0)
                act.activation(o_sb[:], B2[:], ACT.Identity, bias=bcol[:, 0:1]).then_inc(o_add.sem, 1)
                o_add.wait(act, p, 1)
                eqt_ps.wait(act, p, 8)
                act.activation(eq[:, 0, :], o_sb[:], ACT.Square).then_inc(o_sq.sem, 1)

            def x2_high(p):
                x2t_ps.wait(act, p, 1)
                copy(x2t_hi[:].rearrange("p k n -> p (k n)"), C0[:]).then_inc(x2t_h.sem, 1)

            def relu(p, j):
                if first(p) and j == 0:
                    act.wait_ge(wr_ps, 4)
                h_ps.wait(act, p, j + 1)
                act.activation(h_sb[:, j, :], (C0, C1)[j][:], ACT.Relu).then_inc(h_relu.sem, 1)

            def hidden_turned(p, j):
                ht_ps.wait(act, p, j + 1)
                copy(ht_sb[:, j, :], (C0, C1)[j][:]).then_inc(ht_done.sem, 1)

            def routed_out(p):
                ro_ps.wait(act, p, 1)
                lg_sum.wait(act, p, 1)
                f_add.wait(act, p, 0)
                act.activation(routed, C1[:], ACT.Copy, scale=rsum[:, 0:1]).then_inc(ro_done.sem, 1)

            def work(due):
                for k in once(due, "split_wq"):
                    split_wq(k)
                for part in once(due, "weights_b"):
                    weights_b(part)
                for k in once(due, "split_up"):
                    split_up(k)
                for part in once(due, "fold"):
                    fold(part)
                for p, _ in due("load_x"):
                    load_x(p)
                for p, _ in due("load_c"):
                    load_c(p)
                for p, _ in due("store"):
                    store_y(p)
                for p, v in due("queries_turn"):
                    query_turned(p, v)
                for p, u in due("keys_turn"):
                    key_turned(p, u)
                for p, u in due("keys"):
                    key_exp(p, u)
                for p, v in due("queries"):
                    query_exp(p, v)
                for p, w in due("context"):
                    if w % 2 == 1:
                        context_out(p, w // 2)
                for p, _ in due("finish_a"):
                    x_stack(p)
                for p, _ in due("x_turn"):
                    x_high(p)
                    keep(p)
                for p, _ in due("qkv"):
                    qkv_high(p)
                for p, _ in due("qk_turn"):
                    qk_turned(p)
                for p, g in due("prob_turn"):
                    prob_turned(p, g)
                for p, g in due("scores"):
                    prob_exp(p, g)
                for p, half in due("values"):
                    if half == 1:
                        values_out(p)
                for p, _ in due("c_split"):
                    c_high(p)
                for p, _ in due("c_turn"):
                    c_turned(p)
                for p, _ in due("o_bias"):
                    output_square(p)
                for p, _ in due("x2_turn"):
                    x2_high(p)
                for p, j in due("hidden"):
                    relu(p, j)
                for p, j in due("hidden_turn"):
                    hidden_turned(p, j)
                for p, _ in due("ffn_sum"):
                    routed_out(p)

            drive(act, WHEN["act"], setup, work)

        @block.gpsimd
        def _(pool):
            def root(n, p):
                ln_eps[n].wait(pool, p, 1)
                pool.tensor_tensor(rstd[n][:], var_eps[n][:], minus_half[:, 0:1], ALU.pow).then_inc(ln_rstd[n].sem, 1)

            def setup():
                pool.memset(minus_half[:], -0.5).then_inc(halves, 1)
                pool.wait_ge(halves, 1)
                pool.wait_ge(ld_tab, 16)

            def keys_by_head(p):
                for part, s, kt, kd in ((0, kt_h, kt_hi, kd_hi), (1, kt_l, kt_lo, kd_lo)):
                    s.wait(pool, p, 1)
                    for b in range(2):
                        pool.tensor_tensor(kd[:, b], f32(kt[:, None, b * SEQ:(b + 1) * SEQ]).broadcast_to([P, HQ, SEQ]),
                                           own[:, :, None].broadcast_to([P, HQ, SEQ]), ALU.mult)\
                            .then_inc(kd_done.sem, 1)

            def prob_norm(p, g):
                s_rec.wait(pool, p, g + 1)
                v = prob[:, g % 2, :].rearrange("p (h k) -> p h k", h=HG)
                pool.tensor_tensor(v, v, srec[:, g, :, None].broadcast_to([P, HG, SEQ]), ALU.mult)\
                    .then_inc(s_nrm.sem, 1)

            def query_norm(p, v):
                q_rec.wait(pool, p, v + 1)
                w = eq[:, v % 2, :].rearrange("p (h d) -> p h d", h=XH)
                pool.tensor_tensor(w, w, qrec[:, v, :, None].broadcast_to([P, XH, XD]), ALU.mult)\
                    .then_inc(q_nrm.sem, 1)

            def output_root(p):
                o_eps.wait(pool, p, 1)
                pool.tensor_tensor(orstd[:], ovar[:], minus_half[:], ALU.pow).then_inc(o_rstd.sem, 1)

            def add_beta(p):
                if first(p):
                    pool.wait_ge(ld_gb, 32)
                    pool.wait_ge(wr_ps, 4)
                x2_done.wait(pool, p, 1)
                f_res.wait(pool, p, 0)
                pool.tensor_tensor(x2_beta, x2[:], beta[:], ALU.add).then_inc(xb_done.sem, 1)

            def square(p, j):
                h_relu.wait(pool, p, j + 1)
                pool.tensor_tensor(h_sb[:, j, :], h_sb[:, j, :], h_sb[:, j, :], ALU.mult).then_inc(h_sq.sem, 1)

            def times_gamma(p):
                f_nrm.wait(pool, p, 1)
                pool.tensor_tensor(f_sb, f_sb, gamma[:], ALU.mult).then_inc(f_gam.sem, 1)

            def work(due):
                for p, _ in due("residual_a"):
                    root(0, p)
                for p, _ in due("residual_b"):
                    root(1, p)
                for p, v in due("query_sum"):
                    query_norm(p, v)
                for p, g in due("prob_sum"):
                    prob_norm(p, g)
                for p, _ in due("qk_turn"):
                    keys_by_head(p)
                for p, _ in due("o_var"):
                    output_root(p)
                for p, _ in due("add_beta"):
                    add_beta(p)
                for p, j in due("hidden"):
                    square(p, j)
                for p, _ in due("ffn_sum"):
                    root(2, p)
                for p, _ in due("ffn_norm"):
                    times_gamma(p)
                for p, _ in due("residual_c"):
                    root(3, p)

            drive(pool, WHEN["pool"], setup, work)


_INS = ["x", "ctx_4096", "L0_attn_Wq", "L0_attn_Wkv", "L0_attn_Wo", "L0_xattn_Wq", "L0_xattn_Wkv", "L0_xattn_Wout",
        "L0_xattn_b_out", "L0_xattn_g", "L0_ffn_gate_w", "L0_ffn_up_w", "L0_ffn_down_w", "L0_ffn_fc1_w",
        "L0_ffn_fc2_w", "L0_ffn_expert_w", "L0_ffn_ln_gamma", "L0_ffn_ln_beta"]


def kernel(**inputs):
    import numpy as _np
    import concourse.bacc as _bacc
    from concourse.bass_utils import run_bass_kernel_spmd as _run

    nc = _bacc.Bacc("TRN2", target_bir_lowering=False, num_devices=1)
    arrays, args = {}, []
    for name in _INS:
        v = _np.ascontiguousarray(inputs[name])
        if name in ("x", "ctx_4096"):
            v = v.reshape(PAIRS, P, DM)
        arrays[f"in_{name}"] = v
        args.append(nc.dram_tensor(f"in_{name}", v.shape, F32, kind="ExternalInput").ap())
    arrays["tables"], arrays["bias_rows"] = shape_tables()
    args.append(nc.dram_tensor("tables", (P, T_ALL), F32, kind="ExternalInput").ap())
    args.append(nc.dram_tensor("bias_rows", (P, 2, DM), F32, kind="ExternalInput").ap())
    args.append(nc.dram_tensor("out", (PAIRS, P, DM), F32, kind="ExternalOutput").ap())
    decoder_kernel(nc, *args)
    r = _run(nc, [arrays], core_ids=[0])
    return r.results[0]["out"].reshape(BATCH, SEQ, DM)
```
